# Optimizing a Trainium2 kernel written in Bass

```python
import numpy as np
import jax
import jax.numpy as jnp

def _softmax(x, axis=-1):
    return jax.nn.softmax(x, axis=axis)

def _gelu(x):
    return jax.nn.gelu(x, approximate=True)

def _silu(x):
    return jax.nn.silu(x)

def _sigmoid(x):
    return jax.nn.sigmoid(x)

def _layernorm(x, axis=-1, eps=1e-05):
    m = jnp.mean(x, axis=axis, keepdims=True)
    v = jnp.var(x, axis=axis, keepdims=True)
    return (x - m) / jnp.sqrt(v + eps)

def _scatter_add(tgt, idx, src, axis=0):
    return tgt.at[idx].add(src)

def _segment_sum(src, seg, n):
    return jax.ops.segment_sum(src, seg, n)
kernel_name = 'mk_early_fusion_d1_tok_img768_r4_188ae3'

def setup_inputs(seed: int=0):
    np.random.seed(seed)
    _w = jnp.asarray

    def _rec_inputs():
        import jax
        import jax.numpy as jnp
        _rk = jax.random.key(seed)
        x = -0.000356955 + 1 * jax.random.normal(jax.random.fold_in(_rk, 1), (8, 3, 112, 112), jnp.float32)
        txt = -0.00143004 + 1.14228 * jax.random.normal(jax.random.fold_in(_rk, 2), (8, 128, 192), jnp.float32)
        return (x, txt)
    x, txt = _rec_inputs()

    def _L0_tok_setup():
        import jax, jax.numpy as jnp
        import numpy as np
        PATCH = 16
        POS_GRID = (14, 14)
        EMBED = 192
        C_IN = 3

        def _nearest_resize(x, out_h, out_w):
            _, _, h, w = x.shape
            ih = jnp.arange(out_h) * h // out_h
            iw = jnp.arange(out_w) * w // out_w
            return x[:, :, ih][:, :, :, iw]
        key = jax.random.key(seed)
        k1, k2, k3, k4, k5 = jax.random.split(key, 5)
        im = jax.random.normal(k1, (128, C_IN, 224, 224), dtype=jnp.float32)
        W = jax.random.normal(k2, (C_IN * PATCH * PATCH, EMBED), dtype=jnp.float32) * 0.02
        b = jax.random.normal(k3, (EMBED,), dtype=jnp.float32) * 0.02
        positions = jax.random.normal(k4, (1, EMBED, POS_GRID[0], POS_GRID[1]), dtype=jnp.float32)
        cls_embedding = jax.random.normal(k5, (1, 1, EMBED), dtype=jnp.float32)
        return {'im': im, 'W': W, 'b': b, 'positions': positions, 'cls_embedding': cls_embedding}
    _L0_tok_all = _L0_tok_setup()
    _L0_tok_in = {k: v for k, v in _L0_tok_all.items() if k in ('W', 'b', 'positions', 'cls_embedding')}
    del _L0_tok_all

    def _L0_attn_setup():
        import jax, jax.numpy as jnp
        import numpy as np
        import math
        B, S, E = (2, 512, 192)
        H = 12
        V = 50257
        EPS = 1e-05

        def _layernorm(x, w):
            mu = jnp.mean(x, axis=-1, keepdims=True)
            var = jnp.mean(jnp.square(x - mu), axis=-1, keepdims=True)
            return (x - mu) * jax.lax.rsqrt(var + EPS) * w
        key = jax.random.key(seed)
        ks = jax.random.split(key, 7)
        x = jax.random.normal(ks[0], (B, S, E), dtype=jnp.float32)
        e = jax.random.normal(ks[1], (B, S, E), dtype=jnp.float32)
        p = jax.random.normal(ks[2], (B, S, E), dtype=jnp.float32)
        ln_w = jnp.ones((E,), dtype=jnp.float32)
        W_qk = 0.02 * jax.random.normal(ks[3], (H, E), dtype=jnp.float32)
        W_o = 0.02 / math.sqrt(2 * 12) * jax.random.normal(ks[4], (E, H * E), dtype=jnp.float32)
        wte = 0.02 * jax.random.normal(ks[5], (V, E), dtype=jnp.float32)
        return {'x': x, 'e': e, 'p': p, 'ln_w': ln_w, 'W_qk': W_qk, 'W_o': W_o, 'wte': wte}
    _L0_attn_all = _L0_attn_setup()
    _L0_attn_in = {k: v for k, v in _L0_attn_all.items() if k in ('e', 'p', 'ln_w', 'W_qk', 'W_o', 'wte')}
    del _L0_attn_all

    def _L0_ffn_setup():
        import jax, jax.numpy as jnp
        import numpy as np
        DIM = 192
        HID = 128
        E = 16
        G = 8
        TOPK_G = 4
        TOPK_E = 4
        SCALE = 2.5
        B, S = (2, 512)
        key = jax.random.key(seed)
        ks = jax.random.split(key, 9)
        init = lambda k, shape: jax.random.normal(k, shape, dtype=jnp.float32) * 0.02
        z = lambda shape: jnp.zeros(shape, jnp.float32)
        return {'x': jax.random.normal(ks[0], (B, S, DIM), dtype=jnp.float32), 'gate_w': init(ks[1], (DIM, E)), 'gate_b': z((E,)), 'bias': z((E,)), 'Wu': init(ks[2], (E, DIM, HID)), 'bu': z((E, HID)), 'Wg': init(ks[3], (E, DIM, HID)), 'bg': z((E, HID)), 'Wd': init(ks[4], (E, HID, DIM)), 'bd': z((E, DIM)), 'sWu': init(ks[5], (DIM, HID)), 'sbu': z((HID,)), 'sWg': init(ks[6], (DIM, HID)), 'sbg': z((HID,)), 'sWd': init(ks[7], (HID, DIM)), 'sbd': z((DIM,))}
    _L0_ffn_all = _L0_ffn_setup()
    _L0_ffn_in = {k: v for k, v in _L0_ffn_all.items() if k in ('gate_w', 'gate_b', 'bias', 'Wu', 'bu', 'Wg', 'bg', 'Wd', 'bd', 'sWu', 'sbu', 'sWg', 'sbg', 'sWd', 'sbd')}
    del _L0_ffn_all
    return {'x': x, 'txt': txt, 'L0_tok_W': _L0_tok_in['W'], 'L0_tok_b': _L0_tok_in['b'], 'L0_tok_positions': _L0_tok_in['positions'], 'L0_tok_cls_embedding': _L0_tok_in['cls_embedding'], 'L0_attn_e': _L0_attn_in['e'], 'L0_attn_p': _L0_attn_in['p'], 'L0_attn_ln_w': _L0_attn_in['ln_w'], 'L0_attn_W_qk': _L0_attn_in['W_qk'], 'L0_attn_W_o': _L0_attn_in['W_o'], 'L0_attn_wte': _L0_attn_in['wte'], 'L0_ffn_gate_w': _L0_ffn_in['gate_w'], 'L0_ffn_gate_b': _L0_ffn_in['gate_b'], 'L0_ffn_bias': _L0_ffn_in['bias'], 'L0_ffn_Wu': _L0_ffn_in['Wu'], 'L0_ffn_bu': _L0_ffn_in['bu'], 'L0_ffn_Wg': _L0_ffn_in['Wg'], 'L0_ffn_bg': _L0_ffn_in['bg'], 'L0_ffn_Wd': _L0_ffn_in['Wd'], 'L0_ffn_bd': _L0_ffn_in['bd'], 'L0_ffn_sWu': _L0_ffn_in['sWu'], 'L0_ffn_sbu': _L0_ffn_in['sbu'], 'L0_ffn_sWg': _L0_ffn_in['sWg'], 'L0_ffn_sbg': _L0_ffn_in['sbg'], 'L0_ffn_sWd': _L0_ffn_in['sWd'], 'L0_ffn_sbd': _L0_ffn_in['sbd']}

def reference(x, txt, L0_tok_W, L0_tok_b, L0_tok_positions, L0_tok_cls_embedding, L0_attn_e, L0_attn_p, L0_attn_ln_w, L0_attn_W_qk, L0_attn_W_o, L0_attn_wte, L0_ffn_gate_w, L0_ffn_gate_b, L0_ffn_bias, L0_ffn_Wu, L0_ffn_bu, L0_ffn_Wg, L0_ffn_bg, L0_ffn_Wd, L0_ffn_bd, L0_ffn_sWu, L0_ffn_sbu, L0_ffn_sWg, L0_ffn_sbg, L0_ffn_sWd, L0_ffn_sbd):
    import jax
    import jax.numpy as jnp

    def _L0_tok_ref(im, W, b, positions, cls_embedding):
        import jax, jax.numpy as jnp
        import numpy as np
        PATCH = 16
        POS_GRID = (14, 14)
        EMBED = 192
        C_IN = 3

        def _nearest_resize(x, out_h, out_w):
            _, _, h, w = x.shape
            ih = jnp.arange(out_h) * h // out_h
            iw = jnp.arange(out_w) * w // out_w
            return x[:, :, ih][:, :, :, iw]
        B, C, H, Wd = im.shape
        ph, pw = (PATCH, PATCH)
        gh, gw = (H // ph, Wd // pw)
        patches = im.reshape(B, C, gh, ph, gw, pw)
        patches = patches.transpose(0, 2, 4, 1, 3, 5).reshape(B, gh * gw, C * ph * pw)
        pos = _nearest_resize(positions, gh, gw)
        pos = pos.reshape(1, EMBED, gh * gw).transpose(0, 2, 1)
        embeds = jnp.einsum('bsp,pd->bsd', patches, W) + b + pos
        cls_tok = jnp.broadcast_to(cls_embedding, (B, 1, EMBED))
        return jnp.concatenate((cls_tok, embeds), axis=1)

    def _L0_attn_ref(x, e, p, ln_w, W_qk, W_o, wte):
        import jax, jax.numpy as jnp
        import numpy as np
        import math
        B, S, E = (2, 512, 192)
        H = 12
        V = 50257
        EPS = 1e-05

        def _layernorm(x, w):
            mu = jnp.mean(x, axis=-1, keepdims=True)
            var = jnp.mean(jnp.square(x - mu), axis=-1, keepdims=True)
            return (x - mu) * jax.lax.rsqrt(var + EPS) * w
        xb, sb, eb = x.shape
        xn = _layernorm(x, ln_w)
        avg_wte = jnp.mean(wte, axis=0)
        Q = xn[:, None, :, :] * W_qk[None, :, None, :]
        attn = jnp.einsum('bhse,bhte->bhst', Q, Q) / math.sqrt(eb)
        causal = jnp.tril(jnp.ones((sb, sb), dtype=bool))
        attn = jnp.where(causal[None, None], attn, -jnp.inf)
        attn = jax.nn.softmax(attn, axis=-1)
        Vv = xn[:, None, :, :] - avg_wte[None, None, None, :]
        out = jnp.einsum('bhst,bhte->bhse', attn, Vv)
        N_reg = 1.0 / jnp.arange(1, sb + 1, dtype=jnp.float32)
        out = out * N_reg[None, None, :, None]
        out = out.transpose(0, 2, 1, 3).reshape(xb, sb, H * eb)
        out = out @ W_o.T
        return out

    def _L0_ffn_ref(x, gate_w, gate_b, bias, Wu, bu, Wg, bg, Wd, bd, sWu, sbu, sWg, sbg, sWd, sbd):
        import jax, jax.numpy as jnp
        import numpy as np
        DIM = 192
        HID = 128
        E = 16
        G = 8
        TOPK_G = 4
        TOPK_E = 4
        SCALE = 2.5
        B, S = (2, 512)
        orig_shape = x.shape
        xt = x.reshape(-1, DIM)
        T = xt.shape[0]
        scores = jax.nn.softmax(xt @ gate_w + gate_b, axis=-1)
        orig_scores = jax.lax.stop_gradient(scores)
        s = scores + bias[None, :]
        s3 = s.reshape(T, G, E // G)
        group_scores = jax.lax.top_k(s3, 2)[0].sum(-1)
        gidx = jax.lax.top_k(group_scores, TOPK_G)[1]
        gmask = jnp.any(jnp.arange(G)[None, None, :] == gidx[:, :, None], axis=1)
        s_masked = jnp.where(gmask[:, :, None], s3, -jnp.inf).reshape(T, E)
        _, idx = jax.lax.top_k(s_masked, TOPK_E)
        w = jnp.take_along_axis(orig_scores, idx, axis=1) * SCALE
        w_full = jnp.zeros((T, E), xt.dtype).at[jnp.arange(T)[:, None], idx].add(w)
        up = jax.nn.silu(jnp.einsum('td,edh->teh', xt, Wu) + bu)
        gt = jnp.einsum('td,edh->teh', xt, Wg) + bg
        act = up * gt * w_full[:, :, None]
        y = jnp.einsum('teh,ehd->td', act, Wd) + w_full @ bd
        sh = jax.nn.silu(xt @ sWu + sbu) * (xt @ sWg + sbg)
        y = y + sh @ sWd + sbd
        return y.reshape(orig_shape)
    h = _L0_tok_ref(x, L0_tok_W, L0_tok_b, L0_tok_positions, L0_tok_cls_embedding)
    h = jnp.concatenate([h, txt], axis=1)
    h = h + _L0_attn_ref(_layernorm(h, axis=-1), L0_attn_e, L0_attn_p, L0_attn_ln_w, L0_attn_W_qk, L0_attn_W_o, L0_attn_wte)
    h = h + _L0_ffn_ref(_layernorm(h, axis=-1), L0_ffn_gate_w, L0_ffn_gate_b, L0_ffn_bias, L0_ffn_Wu, L0_ffn_bu, L0_ffn_Wg, L0_ffn_bg, L0_ffn_Wd, L0_ffn_bd, L0_ffn_sWu, L0_ffn_sbu, L0_ffn_sWg, L0_ffn_sbg, L0_ffn_sWd, L0_ffn_sbd)
    return h

_drawn_inputs = setup_inputs


def setup_inputs(seed=0):
    import zlib

    import numpy as np

    out = dict(_drawn_inputs(seed))
    spreads = {'L0_attn_ln_w': (1.0, 0.6),
     'L0_ffn_gate_b': (0.0, 0.669),
     'L0_ffn_bias': (0.0, 0.1),
     'L0_ffn_bu': (0.0, 0.8),
     'L0_ffn_bg': (0.0, 0.8),
     'L0_ffn_bd': (0.0, 0.663),
     'L0_ffn_sbu': (0.0, 0.8),
     'L0_ffn_sbg': (0.0, 0.8),
     'L0_ffn_sbd': (0.0, 0.6)}
    factors = {'L0_tok_b': 6.029,
     'L0_attn_W_qk': 41.009,
     'L0_attn_W_o': 3.262,
     'L0_attn_wte': 64.0,
     'L0_ffn_gate_w': 3.406,
     'L0_ffn_Wu': 8.0,
     'L0_ffn_Wg': 8.0,
     'L0_ffn_Wd': 8.0,
     'L0_ffn_sWu': 6.964,
     'L0_ffn_sWg': 6.916,
     'L0_ffn_sWd': 6.476}
    for name, (base, spread) in spreads.items():
        noise = np.random.default_rng([zlib.crc32(name.encode()), seed]).standard_normal(out[name].shape)
        drawn = base * np.exp(spread * noise) if base else spread * noise
        out[name] = jnp.asarray(drawn.astype(out[name].dtype))
    for name, factor in factors.items():
        out[name] = (out[name] * factor).astype(out[name].dtype)
    return out
```

```python
from contextlib import ExitStack

import concourse.bass as bass
from concourse import mybir

F32 = mybir.dt.float32
BF16 = mybir.dt.bfloat16
ALU = mybir.AluOpType
ACT = mybir.ActivationFunctionType
AX = mybir.AxisListType

P = 128
EPS = 1e-5
MASKED = -1e30
NEVER = -3e38


class Tally:

    def __init__(self, sem):
        self.sem, self.base, self.n = sem, 0, 0

    @property
    def at(self):
        return self.base + self.n

    def mark(self, ins):
        ins.then_inc(self.sem, 1)
        self.n += 1

    def restart(self, base):
        self.base, self.n = base, 0


def early_fusion_kernel(nc, x, txt, tok_W, tok_b, tok_pos, tok_cls, ln_w, W_qk, W_o, wte,
                        gate_w, gate_b, bias, Wu, bu, Wg, bg, Wd, bd, sWu, sbu, sWg, sbg, sWd, sbd, out):
    B, C, HI, WI = x.shape
    NTXT, E = txt.shape[1:]
    PS = 16
    G = HI // PS
    NIMG = 1 + G * G
    S = NIMG + NTXT
    TAIL = S - P
    NH = W_qk.shape[0]
    EB = E - P
    V = wte.shape[0]
    NE = Wu.shape[0]
    HID = Wu.shape[2]
    PAIRS = B // 2
    GRP = 4
    UPB = NH // GRP
    UPP = 2 * UPB
    SP = P + 64
    CW = 2 * S
    TT = 2 * TAIL
    COLS = [(0, P), (CW - P, P), (P, TT)]
    NCH = NH * E // P
    SCALE = float(E) ** -0.5
    KC = C * PS * PS // P
    BG = B * G
    WROWS = V // P
    WR = 49
    WREST = V - P * WROWS
    assert TAIL <= 64 and EB == 64 and HID == P and WROWS == WR * B and NH == GRP * UPB
    NT = 3 * PAIRS
    TG = NE // 2
    TOPK = 4
    ROUTE = 2.5
    NW = NE + 1

    with ExitStack() as ctx:
        def sb(name, shape, dt=F32):
            return ctx.enter_context(nc.sbuf_tensor(name, shape, dt))

        def sem(name):
            return ctx.enter_context(nc.semaphore(name))

        bank = [ctx.enter_context(nc.psum_tensor(f"bank{n}", [P, 512], F32)) for n in range(8)]

        ident = sb("ident", [P, P])
        identb = sb("identb", [P, P], BF16)
        cmask = sb("cmask", [P, P], BF16)
        tmask = sb("tmask", [P, 64], BF16)
        ones = sb("ones", [P, P])
        mhalf = sb("mhalf", [P, 4])
        vmean = sb("vmean", [P, 1])
        nregi = sb("nregi", [P, 2], mybir.dt.int32)
        nregf = sb("nregf", [P, 2])
        firsthalf = sb("firsthalf", [P, 1])
        nreg = sb("nreg", [P, 2])
        nnreg = sb("nnreg", [P, 2])
        before = sb("before", [P, NE, NE])
        wtok = sb("wtok", [P, KC, E])
        brow = sb("brow", [1, E])
        posr = sb("posr", [P, 2, 4 * G * G])
        posx = sb("posx", [P, 2, G, B, G])
        area_a = sb("area_a", [P, 2 * NH * SP])
        area_b = sb("area_b", [P, C * PS * WI])

        def part_of(area, at, *shape):
            n = 1
            for d in shape[1:]:
                n *= d
            names = "abcd"[:len(shape) - 1]
            dims = {c: d for c, d in zip(names, shape[1:])}
            return area[0:shape[0], at:at + n].rearrange(f"p ({' '.join(names)}) -> p {' '.join(names)}", **dims)

        wo_raw = part_of(area_a, 0, P, 2, NCH, P)
        xpat = part_of(area_b, 0, BG, C, G, PS * PS)
        woT = sb("woT", [P, NCH, E])
        wqk = sb("wqk", [NH, E])
        w2a = sb("w2a", [P, NH])
        w2b = sb("w2b", [64, NH])
        lnw = sb("lnw", [P, E])
        gwa = sb("gwa", [P, NE])
        gwb = sb("gwb", [64, NE])
        gbb = sb("gbb", [P, NE])
        rbias = sb("rbias", [P, NE])
        bdx = sb("bdx", [NW, E])
        patT = sb("patT", [P, 2, KC, BG])
        emb = sb("emb", [BG, G, E])
        hin = sb("hin", [P, B, 2, E])
        htail = sb("htail", [P, PAIRS, E])
        R = sb("R", [P, NT, E])
        z1 = sb("z1", [P, 2, E])
        z2 = sb("z2", [P, 2, E])
        st = sb("st", [P, 3, 6])
        mv = sb("mv", [P, 3, 2])
        pause = sb("pause", [P, 1])
        ve = sb("ve", [P, 4])
        rs = sb("rs", [P, 4])
        xn = sb("xn", [P, 2, 2, E])
        xa = sb("xa", [P, 2, SP])
        xb = sb("xb", [64, 2, SP])
        qa = part_of(area_a, 0, P, 2, NH, SP)
        qb = part_of(area_b, 0, 64, 2, NH, SP)
        nmax = sb("nmax", [P, 2, 6])
        psums = sb("psums", [P, 2, 6])
        rsum = sb("rsum", [P, 6])
        pm = sb("pm", [P, 2, GRP, P])
        pt = sb("pt", [P, 2, 2, S])
        pT0 = sb("pT0", [P, GRP, S])
        pT1 = sb("pT1", [64, GRP, TAIL])
        oT = sb("oT", [P, NCH, CW])
        ximg = oT[0:BG].rearrange("p c t -> p (c t)")[:, 0:C * PS * WI].rearrange("p (c w) -> p c w", c=C)
        wacc = sb("wacc", [P, WR, E])
        wrest = sb("wrest", [P, E])
        wsum = sb("wsum", [P, E])
        avg = sb("avg", [P, 2])
        cbc = sb("cbc", [P, E])
        fa = part_of(area_a, 0, P, PAIRS, CW)
        fb = part_of(area_a, PAIRS * CW, 64, PAIRS, CW)
        xf = part_of(area_a, 2 * PAIRS * CW, P, 2, 3, E)
        lg = sb("lg", [P, NT, NE])
        mx = sb("mx", [P, NT])
        sc = sb("sc", [P, NT, NE])
        sel = sb("sel", [P, NT, NE])
        gs = sb("gs", [P, NT, TG])
        cmp = sb("cmp", [P, NE, NE])
        cmp2 = sb("cmp2", [P, NE, NE])
        rank = sb("rank", [P, NT, NE])
        wts = sb("wts", [P, NT, NW])
        wT = part_of(area_b, 0, NW, NT, P)
        wup_a = sb("wup_a", [P, 2, HID])
        wup_b = sb("wup_b", [64, 2, HID])
        wgt_a = sb("wgt_a", [P, 2, HID])
        wgt_b = sb("wgt_b", [64, 2, HID])
        wdn = sb("wdn", [P, 2, E])
        bcol = sb("bcol", [P, 2, 2])
        sil = part_of(area_b, NT * P, P, 2, CW)
        hidT = sb("hidT", [P, 2, CW])

        s_const = sem("s_const")
        s_x = sem("s_x")
        s_tokw = sem("s_tokw")
        s_xpat = sem("s_xpat")
        s_pos = sem("s_pos")
        s_wo = sem("s_wo")
        s_small = sem("s_small")
        s_small2 = sem("s_small2")
        s_text = sem("s_text")
        s_emb = sem("s_emb")
        s_zero = sem("s_zero")
        s_posx = sem("s_posx")
        s_patps = sem("s_patps")
        s_patT = sem("s_patT")
        s_embps = sem("s_embps")
        s_embsb = sem("s_embsb")
        s_wops = sem("s_wops")
        s_woT = sem("s_woT")
        s_wqps = sem("s_wqps")
        s_w2 = sem("s_w2")
        var_ready = sem("var_ready")
        rstd_ready = sem("rstd_ready")
        xn_ready = sem("xn_ready")
        xnT_psum = sem("xnT_psum")
        xnT_ready = sem("xnT_ready")
        qa_ready = sem("qa_ready")
        qb_ready = sem("qb_ready")
        scores_main = sem("scores_main")
        scores_tail = sem("scores_tail")
        max_main = sem("max_main")
        max_tail = sem("max_tail")
        exp_main = sem("exp_main")
        exp_tail = sem("exp_tail")
        prob_main = sem("prob_main")
        prob_tail = sem("prob_tail")
        turned_main = sem("turned_main")
        turned_tail = sem("turned_tail")
        probT_main = sem("probT_main")
        probT_tail = sem("probT_tail")
        pv_done = sem("pv_done")
        ot_act = sem("ot_act")
        ot_dve = sem("ot_dve")
        wo_done = sem("wo_done")
        proj_read = sem("proj_read")
        wte_in = sem("wte_in")
        wte_rest = sem("wte_rest")
        wsum_ready = sem("wsum_ready")
        avg_psum = sem("avg_psum")
        avg_ready = sem("avg_ready")
        c_psum = sem("c_psum")
        xf_ready = sem("xf_ready")
        xfT_psum = sem("xfT_psum")
        xfT_act = sem("xfT_act")
        xfT_dve = sem("xfT_dve")
        gate_psum = sem("gate_psum")
        gate_ready = sem("gate_ready")
        nmx_ready = sem("nmx_ready")
        gexp = sem("gexp")
        wts_ready = sem("wts_ready")
        wT_psum = sem("wT_psum")
        wT_ready = sem("wT_ready")
        bias_psum = sem("bias_psum")
        bias_added = sem("bias_added")
        w_in = [sem("w_in0"), sem("w_in1")]
        up_ready = sem("up_ready")
        gt_ready = sem("gt_ready")
        silu_ready = sem("silu_ready")
        hid_ready = sem("hid_ready")
        down_done = sem("down_done")
        acc_done = sem("acc_done")
        out_done = sem("out_done")
        dve_own = sem("dve_own")
        pool_own = sem("pool_own")

        WLOADS = 7
        n_small = 0
        block = ctx.enter_context(nc.Block())

        @block.sync
        def _(sp):
            for b in range(B):
                sp.dma_start(ximg[b * G:(b + 1) * G, :, :],
                             x[b].rearrange("c (g p) w -> g c (p w)", p=PS)).then_inc(s_x, 16)
            sp.dma_start(wtok[:], tok_W.rearrange("(k p) e -> p k e", p=P)).then_inc(s_tokw, 16)
            sp.dma_start(brow[:], tok_b.rearrange("(a e) -> a e", a=1)).then_inc(s_tokw, 16)
            sp.wait_ge(s_zero, 2)
            TM = P - NIMG
            for b in range(B):
                sp.dma_start(hin[0:1, b, 0, :], tok_cls[0]).then_inc(s_text, 16)
                sp.dma_start(hin[NIMG:P, b, 0, :], txt[b, 0:TM, :]).then_inc(s_text, 16)
                sp.dma_start(hin[0:TAIL, b, 1, :], txt[b, TM:NTXT, :]).then_inc(s_text, 16)
                sp.dma_start(htail[TAIL * (b % 2):TAIL * (b % 2) + TAIL, b // 2, :], txt[b, TM:NTXT, :]).then_inc(s_text, 16)
            sp.wait_ge(s_embsb, G)
            for b in range(B):
                sp.dma_start(hin[1:NIMG, b, 0, :], emb[b * G:(b + 1) * G, :, :]).then_inc(s_emb, 16)

            def load_expert(slot, up, gt, dn, b1, b2):
                q = w_in[slot]
                sp.dma_start(wup_a[:, slot, :], up[0:P, :]).then_inc(q, 16)
                sp.dma_start(wup_b[:, slot, :], up[P:E, :]).then_inc(q, 16)
                sp.dma_start(wgt_a[:, slot, :], gt[0:P, :]).then_inc(q, 16)
                sp.dma_start(wgt_b[:, slot, :], gt[P:E, :]).then_inc(q, 16)
                sp.dma_start(wdn[:, slot, :], dn).then_inc(q, 16)
                sp.dma_start(bcol[:, slot, 0:1], b1).then_inc(q, 16)
                sp.dma_start(bcol[:, slot, 1:2], b2).then_inc(q, 16)

            def load_routed(slot, e):
                load_expert(slot, Wu[bass.ds(e, 1)].rearrange("a k h -> (a k) h"),
                            Wg[bass.ds(e, 1)].rearrange("a k h -> (a k) h"),
                            Wd[bass.ds(e, 1)].rearrange("a k h -> (a k) h"),
                            bu[bass.ds(e, 1)].rearrange("a h -> h a"), bg[bass.ds(e, 1)].rearrange("a h -> h a"))

            load_expert(0, sWu, sWg, sWd, sbu.rearrange("(h a) -> h a", a=1), sbg.rearrange("(h a) -> h a", a=1))
            load_routed(1, 0)
            with sp.Fori(0, (NE - 2) // 2) as j:
                sp.wait_ge(down_done, 16 * j + 8)
                load_routed(0, 2 * j + 1)
                sp.wait_ge(down_done, 16 * j + 16)
                load_routed(1, 2 * j + 2)
            sp.wait_ge(down_done, 8 * (NE - 1))
            load_routed(0, NE - 1)
            for i in range(PAIRS):
                sp.wait_ge(acc_done, 2 * (PAIRS * NE + i + 1))
                for k in range(2):
                    sp.dma_start(out[2 * i + k, 0:P, :], R[:, 3 * i + k, :]).then_inc(out_done, 16)
                    sp.dma_start(out[2 * i + k, P:S, :], R[TAIL * k:TAIL * k + TAIL, 3 * i + 2, :]).then_inc(out_done, 16)
            sp.wait_ge(out_done, 16 * 4 * PAIRS)

        @block.gpsimd
        def _(pool):
            own = Tally(pool_own)
            wte_v = wte[0:P * WROWS, :].rearrange("(p c r) e -> c p r e", p=P, r=WR)
            pool.dma_start(wacc[:], wte_v[0]).then_inc(wte_in, 16)
            own.mark(pool.memset(ident[:], 0.0))
            own.mark(pool.memset(cmask[:], 0.0))
            own.mark(pool.memset(tmask[:], 0.0))
            own.mark(pool.memset(wrest[:], 0.0))
            own.mark(pool.memset(before[:], 0.0))
            pool.wait_ge(pool_own, own.at)
            pool.dma_start(wrest[0:WREST, :], wte[P * WROWS:V, :]).then_inc(wte_rest, 16)
            own.mark(pool.affine_select(out=ident[:], in_=ident[:], compare_op=ALU.not_equal, fill=1.0,
                                        base=0, pattern=[[-1, P]], channel_multiplier=1))
            own.mark(pool.affine_select(out=cmask[:], in_=cmask[:], compare_op=ALU.is_ge, fill=MASKED,
                                        base=0, pattern=[[-1, P]], channel_multiplier=1))
            own.mark(pool.affine_select(out=tmask[0:64, :], in_=tmask[0:64, :], compare_op=ALU.is_ge, fill=MASKED,
                                        base=0, pattern=[[-1, 64]], channel_multiplier=1))
            pool.wait_ge(pool_own, own.at)
            own.mark(pool.affine_select(out=tmask[64:P, :], in_=tmask[64:P, :], compare_op=ALU.is_ge, fill=MASKED,
                                        base=0, pattern=[[-1, 64]], channel_multiplier=1))
            pool.wait_ge(pool_own, own.at)
            own.mark(pool.affine_select(out=before[:], in_=before[:], compare_op=ALU.is_ge, fill=1.0,
                                        base=0, pattern=[[-1, NE], [1, NE]], channel_multiplier=0))
            own.mark(pool.memset(ones[:], 1.0))
            own.mark(pool.memset(mhalf[:], -0.5))
            own.mark(pool.memset(vmean[:], 1.0 / V))
            own.mark(pool.iota(nregi[:, 0:1], pattern=[[0, 1]], base=1, channel_multiplier=1))
            own.mark(pool.iota(nregi[:, 1:2], pattern=[[0, 1]], base=P + 1 - TAIL, channel_multiplier=1))
            own.mark(pool.memset(firsthalf[:], 0.0))
            pool.wait_ge(pool_own, own.at)
            own.mark(pool.affine_select(out=firsthalf[:], in_=firsthalf[:], compare_op=ALU.is_ge, fill=float(TAIL),
                                        base=-TAIL, pattern=[[0, 1]], channel_multiplier=1))
            own.mark(pool.tensor_copy(identb[:], ident[:]))
            own.mark(pool.tensor_copy(nregf[:], nregi[:]))
            pool.wait_ge(pool_own, own.at)
            own.mark(pool.tensor_tensor(nregf[:, 1:2], nregf[:, 1:2], firsthalf[:], ALU.add))
            pool.wait_ge(pool_own, own.at)
            pool.memset(wts[:], 1.0).then_inc(s_const, 1)
            pool.wait_ge(s_x, 16 * B)
            pool.tensor_copy(xpat[:, 2].rearrange("t g (r w) -> t g r w", w=PS),
                             ximg[:, 2].rearrange("t (r g w) -> t g r w", g=G, w=PS)).then_inc(s_xpat, 1)

            def rstd(n, count):
                pool.wait_ge(var_ready, count)
                pool.tensor_tensor(rs[:, 0:n], ve[:, 0:n], mhalf[:, 0:n], ALU.pow).then_inc(rstd_ready, 1)

            def batch(i, b):
                bt = 2 * i + b
                rstd(2, 2 * bt + 1)
                rstd(2, 2 * bt + 2)
                pool.wait_ge(xnT_ready, 2 * bt + 2)
                pool.tensor_tensor(qb[:, b, 0, :], xb[:, b, :], w2b[:, 0:1].broadcast_to([64, SP]), ALU.mult)
                for h in range(1, NH):
                    last = pool.tensor_scalar(qb[:, b, h, :], xb[:, b, :], w2b[:, h:h + 1], None, ALU.mult)
                last.then_inc(qb_ready, 1)

            def add_rows(c):
                pool.wait_ge(wte_in, 16 * c)
                pool.dma_start(wacc[:], wte_v[bass.ds(c, 1)].rearrange("a p r e -> (a p) r e"),
                               accum_op=ALU.add, max_dma_last_dim=4 * WR * E // 6).then_inc(wte_in, 16)

            pool.wait_ge(s_w2, 2)
            batch(0, 0)
            add_rows(1)
            batch(0, 1)
            with pool.Fori(0, PAIRS - 1) as i:
                for b in range(2):
                    add_rows(2 * i + 2 + b)
                    batch(i + 1, b)
            for i in range(PAIRS):
                rstd(3, 2 * B + i + 1)

        @block.scalar
        def _(act):
            act.dma_start(posr[:, 0, :], tok_pos[0, 0:P].rearrange("d h w -> d (h w)")).then_inc(s_pos, 16)
            act.dma_start(posr[0:64, 1, :], tok_pos[0, P:E].rearrange("d h w -> d (h w)")).then_inc(s_pos, 16)
            act.dma_start(wqk[:], W_qk).then_inc(s_small, 16)
            act.dma_start(lnw[:], ln_w.rearrange("(a e) -> a e", a=1).broadcast_to([P, E])).then_inc(s_small, 16)
            for part, rows in ((0, P), (1, 64)):
                src = W_o[P * part:P * part + rows, :].rearrange("o (q j e) -> o q j e", q=NH // 2, j=2)
                dst = wo_raw[0:rows, part].rearrange("o (q c) e -> o q c e", c=3)
                for j in range(2):
                    act.dma_start(dst[:, :, j, :], src[:, :, j, 0:P]).then_inc(s_wo, 16)
                    act.dma_start(dst[:, :, 2, 64 * j:64 * j + 64], src[:, :, j, P:E]).then_inc(s_wo, 16)
            act.dma_start(gwa[:], gate_w[0:P, :]).then_inc(s_small2, 16)
            act.dma_start(gwb[:], gate_w[P:E, :]).then_inc(s_small2, 16)
            act.dma_start(gbb[:], gate_b.rearrange("(a e) -> a e", a=1).broadcast_to([P, NE])).then_inc(s_small2, 16)
            act.dma_start(rbias[:], bias.rearrange("(a e) -> a e", a=1).broadcast_to([P, NE])).then_inc(s_small2, 16)
            act.dma_start(bdx[0:NE, :], bd).then_inc(s_small2, 16)
            act.dma_start(bdx[NE:NW, :], sbd.rearrange("(a e) -> a e", a=1)).then_inc(s_small2, 16)
            act.wait_ge(s_x, 16 * B)
            act.activation(xpat[:, 1].rearrange("t g (r w) -> t g r w", w=PS),
                           ximg[:, 1].rearrange("t (r g w) -> t g r w", g=G, w=PS), ACT.Copy).then_inc(s_xpat, 1)
            for g in range(G):
                act.wait_ge(s_patps, g + 1)
                if g >= 2:
                    act.wait_ge(s_embps, g - 1)
                act.activation(patT[:, g % 2], bank[g % 2][:, 0:KC * BG].rearrange("p (k t) -> p k t", k=KC),
                               ACT.Copy).then_inc(s_patT, 1)

            def turn_out(b, bt):
                act.wait_ge(xnT_psum, bt + 1)
                act.activation(xa[:, b, :], bank[7][:, 0:SP], ACT.Copy).then_inc(xnT_ready, 1)
                act.activation(xb[:, b, :], bank[7][0:64, SP:2 * SP], ACT.Copy).then_inc(xnT_ready, 1)

            def exps(u, U):
                sl = u % 2
                act.wait_ge(max_main, U + 1)
                for j in range(GRP):
                    last = act.activation(pm[:, sl, j, :], bank[0][:, j * P:(j + 1) * P], ACT.Exp,
                                          bias=nmax[:, sl, j:j + 1], accum_out=psums[:, sl, j:j + 1])
                last.then_inc(exp_main, 1)
                act.wait_ge(max_tail, U + 1)
                for k in range(2):
                    last = act.activation(pt[:, sl, k, :], bank[1][:, k * S:(k + 1) * S], ACT.Exp,
                                          bias=nmax[:, sl, 4 + k:5 + k], accum_out=psums[:, sl, 4 + k:5 + k])
                last.then_inc(exp_tail, 1)

            def prob_out(u, U):
                act.wait_ge(turned_main, U + 1)
                at = 0 if u < UPB else TAIL
                act.activation(pT0[:, :, at:at + P], bank[2][:, :].rearrange("p (j t) -> p j t", j=GRP),
                               ACT.Copy).then_inc(probT_main, 1)

            def mix_out(u, U):
                g, b = u % UPB, u // UPB
                act.wait_ge(pv_done, 3 * U + 1)
                act.activation(oT[:, 6 * g:6 * g + 2, b * S:(b + 1) * S],
                               bank[4][:, 0:2 * S].rearrange("p (j t) -> p j t", j=2), ACT.Copy).then_inc(ot_act, 1)

            turn_out(0, 0)
            exps(0, 0)
            turn_out(1, 1)

            def pair(i, last):
                U = UPP * i
                for u in range(UPP - 1):
                    exps(u + 1, U + u + 1)
                    if u >= 1:
                        mix_out(u - 1, U + u - 1)
                    if u == 4 and not last:
                        turn_out(0, 2 * i + 2)
                    prob_out(u, U + u)
                mix_out(4, U + 4)
                prob_out(5, U + 5)
                if not last:
                    exps(0, U + 6)
                mix_out(5, U + 5)
                if not last:
                    turn_out(1, 2 * i + 3)

            with act.Fori(0, PAIRS - 1) as i:
                pair(i, False)
            pair(PAIRS - 1, True)

            for i in range(PAIRS):
                act.wait_ge(xfT_psum, i + 1)
                act.activation(fa[:, i, :], bank[i % 2][:, 0:CW], ACT.Copy).then_inc(xfT_act, 1)
            act.wait_ge(nmx_ready, 1)
            act.activation(sc[:], lg[:], ACT.Exp).then_inc(gexp, 1)

            def silu(st_, n):
                sl = n % 2
                act.wait_ge(up_ready, st_ + 1)
                if n >= 2:
                    act.wait_ge(hid_ready, st_ - 1)
                act.activation(sil[:, sl, :], bank[sl][:, 0:CW], ACT.Silu,
                               bias=bcol[:, (n // PAIRS) % 2, 0:1]).then_inc(silu_ready, 1)

            for n in range(PAIRS):
                if n == 0:
                    act.wait_ge(w_in[0], 16 * WLOADS)
                silu(n, n)
            with act.Fori(0, NE // 2) as j:
                for m in range(2 * PAIRS):
                    if m == 0:
                        act.wait_ge(w_in[1], 16 * WLOADS * j + 16 * WLOADS)
                    if m == PAIRS:
                        act.wait_ge(w_in[0], 16 * WLOADS * j + 32 * WLOADS)
                    silu(2 * PAIRS * j + PAIRS + m, PAIRS + m)

        @block.tensor
        def _(pe):
            pe.wait_ge(s_const, 1)
            pe.wait_ge(s_xpat, 3)

            def patch_turn(g):
                if g >= 2:
                    pe.wait_ge(s_patT, g - 1)
                for k in range(KC):
                    src = xpat[:, k // 2, g, (k % 2) * P:(k % 2) * P + P]
                    last = pe.transpose(bank[g % 2][:, k * BG:(k + 1) * BG], src, ident[0:BG, 0:BG])
                last.then_inc(s_patps, 1)

            def patch_embed(g):
                o = bank[2 + g % 2]
                pe.wait_ge(s_patT, g + 1)
                if g >= 2:
                    pe.wait_ge(s_embsb, g - 1)
                for k in range(KC):
                    pe.matmul(o[0:BG, 0:E], patT[:, g % 2, k, :], wtok[:, k, :], start=(k == 0), stop=False)
                pe.matmul(o[0:BG, 0:E], ones[0:1, 0:BG], brow[:], start=False, stop=True)
                pe.matmul(o[0:BG, 0:P], posx[:, 0, g].rearrange("p b h -> p (b h)"), ident[:], start=False, stop=True,
                          skip_group_check=True)
                pe.matmul(o[0:BG, P:E], posx[0:64, 1, g].rearrange("p b h -> p (b h)"), ident[0:64, 0:64], start=False,
                          stop=True, skip_group_check=True).then_inc(s_embps, 1)

            patch_turn(0)
            pe.wait_ge(s_tokw, 32)
            pe.wait_ge(s_posx, 2)
            for g in range(G):
                if g + 1 < G:
                    patch_turn(g + 1)
                patch_embed(g)
            pe.wait_ge(s_small, 32)
            pe.transpose(bank[6][:, 0:NH], wqk[:, 0:P], ident[0:NH, 0:NH])
            pe.transpose(bank[6][0:64, NH:2 * NH], wqk[:, P:E], ident[0:NH, 0:NH]).then_inc(s_wqps, 1)
            pe.wait_ge(s_wo, 16 * 8)
            for c in range(NCH):
                if c >= 2:
                    pe.wait_ge(s_woT, c - 1)
                for part, rows in ((0, P), (1, 64)):
                    last = pe.transpose(bank[4 + c % 2][:, part * P:part * P + rows], wo_raw[0:rows, part, c, :],
                                        ident[0:rows, 0:rows])
                last.then_inc(s_wops, 1)

            def turn_in(b, bt):
                pe.wait_ge(xn_ready, bt + 1)
                if not isinstance(bt, int) or bt:
                    pe.wait_ge(xnT_ready, 2 * bt)
                pe.transpose(bank[7][:, 0:P], xn[:, b, 0, 0:P], ident[:])
                pe.transpose(bank[7][:, P:SP], xn[0:64, b, 1, 0:P], ident[0:64, 0:64])
                pe.transpose(bank[7][0:64, SP:SP + P], xn[:, b, 0, P:E], ident[:])
                pe.transpose(bank[7][0:64, SP + P:2 * SP], xn[0:64, b, 1, P:E], ident[0:64, 0:64]).then_inc(xnT_psum, 1)

            def scores(u, U):
                g, b = u % UPB, u // UPB
                h = GRP * g
                main = bank[0][:, :].rearrange("p (j t) -> p j t", j=GRP)
                if not isinstance(U, int) or U:
                    pe.wait_ge(exp_main, U)
                pe.matmul(main, xa[:, b, 0:P], qa[:, b, h:h + GRP, 0:P], start=True, stop=False)
                pe.matmul(main, xb[:, b, 0:P], qb[:, b, h:h + GRP, 0:P], start=False, stop=False)
                pe.matmul(main, identb[:], cmask[:].rearrange("p (a t) -> p a t", a=1).broadcast_to([P, GRP, P]),
                          start=False, stop=True).then_inc(scores_main, 1)
                if not isinstance(U, int) or U:
                    pe.wait_ge(exp_tail, U)
                for half in range(2):
                    o = bank[1][64 * half:64 * half + 64, 0:2 * S].rearrange("p (j t) -> p j t", j=2)
                    hh = h + 2 * half
                    pe.matmul(o, xa[:, b, P:SP], qa[:, b, hh:hh + 2, 0:S], start=True, stop=False)
                    pe.matmul(o, xb[:, b, P:SP], qb[:, b, hh:hh + 2, 0:S], start=False, stop=True)
                o = bank[1][:, 0:2 * S].rearrange("p (j t) -> p j t", j=2)[:, :, P:S]
                pe.matmul(o, identb[:], tmask[:, 0:TAIL].rearrange("p (a t) -> p a t", a=1).broadcast_to([P, 2, TAIL]),
                          start=False, stop=True, skip_group_check=True).then_inc(scores_tail, 1)

            def queries_in(bt):
                pe.wait_ge(qa_ready, bt + 1)
                pe.wait_ge(qb_ready, bt + 1)

            def turn_probs(u, U):
                sl = u % 2
                pe.wait_ge(prob_main, U + 1)
                for j in range(GRP):
                    last = pe.transpose(bank[2][:, j * P:(j + 1) * P], pm[:, sl, j, :], ident[:])
                last.then_inc(turned_main, 1)
                pe.wait_ge(prob_tail, U + 1)
                for k in range(2):
                    pe.transpose(bank[3][:, k * P:(k + 1) * P], pt[:, sl, k, 0:P], ident[:])
                    last = pe.transpose(bank[3][0:TAIL, (2 + k) * P:(3 + k) * P], pt[:, sl, k, P:S], ident[:])
                last.then_inc(turned_tail, 1)

            def mix(u, U, i):
                b = u // UPB
                tl = slice(P, S) if b == 0 else slice(0, TAIL)
                pe.wait_ge(probT_main, U + 1)
                pe.wait_ge(probT_tail, 2 * U + 2)
                if u == 0:
                    pe.wait_ge(proj_read, 3 * i + 1)
                for q in range(2):
                    if u >= 1:
                        if q == 0:
                            pe.wait_ge(ot_act, U)
                        else:
                            pe.wait_ge(ot_dve, 2 * U)
                    o = bank[4 + q][:, 0:2 * S].rearrange("p (j t) -> p j t", j=2)
                    pe.matmul(o, xn[:, b, 0, 0:P], pT0[:, 2 * q:2 * q + 2, :], start=True, stop=True)
                    pe.matmul(o[:, :, tl], xn[0:TAIL, b, 1, 0:P], pT1[0:TAIL, 2 * q:2 * q + 2, :], start=False,
                              stop=True, skip_group_check=True).then_inc(pv_done, 1)
                for jj in range(2):
                    o = bank[6][64 * jj:64 * jj + 64, 0:2 * S].rearrange("p (q t) -> p q t", q=2)
                    pe.matmul(o, xn[:, b, 0, P:E], pT0[:, jj:GRP:2, :], start=True, stop=True)
                    last = pe.matmul(o[:, :, tl], xn[0:TAIL, b, 1, P:E], pT1[0:TAIL, jj:GRP:2, :], start=False,
                                     stop=True, skip_group_check=True)
                last.then_inc(pv_done, 1)

            def project(U):
                pe.wait_ge(ot_act, U + UPP)
                pe.wait_ge(ot_dve, 2 * (U + UPP))
                for t, (at, n) in enumerate(COLS):
                    o = bank[4][:, t * E:(t + 1) * E] if t < 2 else bank[5][0:TT, 0:E]
                    for c in range(NCH):
                        last = pe.matmul(o, oT[:, c, at:at + n], woT[:, c, :], start=(c == 0), stop=(c == NCH - 1))
                    if t >= 1:
                        last.then_inc(wo_done, 1)

            turn_in(0, 0)
            queries_in(0)
            scores(0, 0)
            turn_in(1, 1)

            def pair(i, last):
                U = UPP * i
                for u in range(UPP - 1):
                    if u + 1 == UPB:
                        queries_in(2 * i + 1)
                    scores(u + 1, U + u + 1)
                    if u >= 1:
                        mix(u - 1, U + u - 1, i)
                    if u == 4 and not last:
                        turn_in(0, 2 * i + 2)
                    turn_probs(u, U + u)
                mix(4, U + 4, i)
                turn_probs(5, U + 5)
                if not last:
                    queries_in(2 * i + 2)
                    scores(0, U + 6)
                mix(5, U + 5, i)
                project(U)
                if not last:
                    turn_in(1, 2 * i + 3)

            pe.wait_ge(s_woT, NCH - 1)
            with pe.Fori(0, PAIRS - 1) as i:
                pair(i, False)
            pair(PAIRS - 1, True)

            pe.wait_ge(wsum_ready, 1)
            pe.matmul(bank[7][:, 0:1], wsum[:, 0:P], vmean[:], start=True, stop=True)
            pe.matmul(bank[7][0:64, 1:2], wsum[:, P:E], vmean[:], start=True, stop=True)
            pe.matmul(bank[7][64:P, 1:2], wsum[:, P:E], vmean[:], start=True, stop=True).then_inc(avg_psum, 1)
            pe.wait_ge(avg_ready, 1)
            for c in range(NCH):
                m = 0 if c % 3 < 2 else 1
                last = pe.matmul(bank[6][:, 0:E], avg[:, m:m + 1].broadcast_to([P, P]), woT[:, c, :],
                                 start=(c == 0), stop=(c == NCH - 1))
            last.then_inc(c_psum, 1)

            def turn_ffn(i):
                pe.wait_ge(xf_ready, i + 1)
                if i >= 2:
                    pe.wait_ge(xfT_act, i - 1)
                    pe.wait_ge(xfT_dve, i - 1)
                for t, (at, n) in enumerate(COLS):
                    pe.transpose(bank[i % 2][:, at:at + n], xf[0:n, i % 2, t, 0:P], ident[0:n, 0:n])
                    last = pe.transpose(bank[2 + i % 2][0:64, at:at + n], xf[0:n, i % 2, t, P:E], ident[0:n, 0:n])
                last.then_inc(xfT_psum, 1)

            def gate(i):
                pe.wait_ge(xfT_act, i + 1)
                pe.wait_ge(xfT_dve, i + 1)
                if i >= 1:
                    pe.wait_ge(gate_ready, i)
                for t, (at, n) in enumerate(COLS):
                    o = bank[4][0:n, t * NE:(t + 1) * NE]
                    pe.matmul(o, fa[:, i, at:at + n], gwa[:], start=True, stop=False)
                    last = pe.matmul(o, fb[:, i, at:at + n], gwb[:], start=False, stop=True)
                last.then_inc(gate_psum, 1)

            pe.wait_ge(s_small2, 96)
            turn_ffn(0)
            for i in range(PAIRS):
                if i + 1 < PAIRS:
                    turn_ffn(i + 1)
                gate(i)

            def up_gate(n, st_, k):
                sl = n % 2
                if n >= 2:
                    pe.wait_ge(silu_ready, st_ - 1)
                pe.matmul(bank[sl][:, 0:CW], wup_a[:, k, :], fa[:, n % PAIRS, :], start=True, stop=False)
                pe.matmul(bank[sl][:, 0:CW], wup_b[:, k, :], fb[:, n % PAIRS, :], start=False,
                          stop=True).then_inc(up_ready, 1)
                if n >= 2:
                    pe.wait_ge(hid_ready, st_ - 1)
                pe.matmul(bank[2 + sl][:, 0:CW], wgt_a[:, k, :], fa[:, n % PAIRS, :], start=True, stop=False)
                pe.matmul(bank[2 + sl][:, 0:CW], wgt_b[:, k, :], fb[:, n % PAIRS, :], start=False,
                          stop=True).then_inc(gt_ready, 1)

            def down(n, st_, k):
                sl = n % 2
                pe.wait_ge(hid_ready, st_ + 1)
                for t, (at, rows) in enumerate(COLS):
                    if n >= 2 and t != 1:
                        pe.wait_ge(acc_done, 2 * (st_ - 1) - (1 if t == 0 else 0))
                    o = bank[4 + sl][:, t * E:(t + 1) * E] if t < 2 else bank[6 + sl][0:TT, 0:E]
                    last = pe.matmul(o, hidT[:, sl, at:at + rows], wdn[:, k, :], start=True, stop=True)
                    if t >= 1:
                        last.then_inc(down_done, 1)

            def expert_steps(n0, st0, j, first, last):
                count = PAIRS if first else 2 * PAIRS
                for m in range(count):
                    n, s_ = n0 + m, st0 + m
                    if not (last and m == count - 1):
                        if (n + 1) % PAIRS == 0:
                            k = ((n + 1) // PAIRS) % 2
                            if first:
                                pe.wait_ge(w_in[1], 16 * WLOADS)
                            elif k == 0:
                                pe.wait_ge(w_in[0], 16 * WLOADS * j + 32 * WLOADS)
                            else:
                                pe.wait_ge(w_in[1], 16 * WLOADS * j + 32 * WLOADS)
                        up_gate(n + 1, s_ + 1, ((n + 1) // PAIRS) % 2)
                    down(n, s_, (n // PAIRS) % 2)

            pe.wait_ge(gate_ready, PAIRS)
            pe.wait_ge(w_in[0], 16 * WLOADS)
            up_gate(0, 0, 0)
            expert_steps(0, 0, None, True, False)
            pe.wait_ge(wts_ready, 1)
            pe.wait_ge(acc_done, 2 * PAIRS)
            for t in range(NT):
                if t >= 2:
                    pe.wait_ge(wT_ready, t - 1)
                pe.transpose(bank[4 + t % 2][0:NW, 0:P], wts[:, t, :], ident[:]).then_inc(wT_psum, 1)
            for t in range(NT):
                pe.wait_ge(wT_ready, t + 1)
                if t >= 2:
                    pe.wait_ge(bias_added, t - 1)
                pe.matmul(bank[6 + t % 2][:, 0:E], wT[:, t, :], bdx[:], start=True, stop=True).then_inc(bias_psum, 1)
            pe.wait_ge(bias_added, NT)
            with pe.Fori(0, NE // 2 - 1) as j:
                expert_steps(PAIRS, 2 * PAIRS * j + PAIRS, j, False, False)
            expert_steps(PAIRS, 2 * PAIRS * (NE // 2 - 1) + PAIRS, NE // 2 - 1, False, True)

        @block.vector
        def _(dve):
            own = Tally(dve_own)

            def link(ins):
                own.mark(ins)
                dve.wait_ge(dve_own, own.at)

            dve.memset(hin[:], 0.0).then_inc(s_zero, 1)
            dve.memset(htail[:], 0.0).then_inc(s_zero, 1)
            own.mark(dve.memset(lg[:], 0.0))
            own.mark(dve.memset(mv[:], 1.0))
            dve.wait_ge(s_x, 16 * B)
            dve.tensor_copy(xpat[:, 0].rearrange("t g (r w) -> t g r w", w=PS),
                            ximg[:, 0].rearrange("t (r g w) -> t g r w", g=G, w=PS)).then_inc(s_xpat, 1)
            dve.wait_ge(s_pos, 32)
            for part, rows in ((0, P), (1, 64)):
                grid = posr[0:rows, part, :].rearrange("p (h a w c) -> p h a w c", h=G, a=2, c=2)
                for g in range(G):
                    src = grid[:, :, 0, g, 0].rearrange("p (a h) -> p a h", a=1).broadcast_to([rows, B, G])
                    last = dve.tensor_copy(posx[0:rows, part, g], src)
                last.then_inc(s_posx, 1)
            dve.wait_ge(s_const, 1)
            own.mark(dve.reciprocal(nreg[:], nregf[:]))
            dve.wait_ge(dve_own, own.at)
            own.mark(dve.tensor_scalar(nnreg[:], nreg[:], -1.0, None, ALU.mult))
            for g in range(G):
                dve.wait_ge(s_embps, g + 1)
                dve.tensor_copy(emb[:, g, :], bank[2 + g % 2][0:BG, 0:E]).then_inc(s_embsb, 1)
            dve.wait_ge(s_wqps, 1)
            link(dve.tensor_copy(w2a[:], bank[6][:, 0:NH]))
            link(dve.tensor_copy(w2b[:], bank[6][0:64, NH:2 * NH]))
            dve.scalar_tensor_tensor(out=w2a[:], in0=w2a[:], scalar=SCALE, in1=w2a[:], op0=ALU.mult,
                                     op1=ALU.mult).then_inc(s_w2, 1)
            dve.scalar_tensor_tensor(out=w2b[:], in0=w2b[:], scalar=SCALE, in1=w2b[:], op0=ALU.mult,
                                     op1=ALU.mult).then_inc(s_w2, 1)
            for c in range(NCH):
                dve.wait_ge(s_wops, c + 1)
                dve.tensor_copy(woT[:, c, :], bank[4 + c % 2][:, 0:E]).then_inc(s_woT if c + 1 < NCH else proj_read, 1)
            dve.wait_ge(s_w2, 2)
            dve.wait_ge(s_text, 16 * 4 * B)
            dve.wait_ge(s_emb, 16 * B)
            dve.wait_ge(s_small, 32)

            def stats(tiles, count):
                n = len(tiles)
                for t, src in enumerate(tiles):
                    own.mark(dve.bn_stats(st[0:src.shape[0], t, :], src))
                dve.wait_ge(dve_own, own.at)
                dve.memset(pause[:], 0.0)
                for t, src in enumerate(tiles):
                    own.mark(dve.bn_aggr(mv[0:src.shape[0], t, :], st[0:src.shape[0], t, :]))
                dve.wait_ge(dve_own, own.at)
                dve.tensor_scalar(ve[:, 0:n], mv[:, 0:n, 1], EPS, None, ALU.add).then_inc(var_ready, 1)
                dve.wait_ge(rstd_ready, count)

            def normalise(b, bt, h):
                stats([h[:, 0, :], h[:, 1, :]], 2 * bt + 1)
                for t in range(2):
                    own.mark(dve.tensor_scalar(z1[:, t, :], h[:, t, :], mv[:, t, 0:1], rs[:, t:t + 1],
                                               ALU.subtract, ALU.mult))
                dve.wait_ge(dve_own, own.at)
                stats([z1[:, 0, :], z1[:, 1, :]], 2 * bt + 2)
                for t in range(2):
                    own.mark(dve.tensor_scalar(z2[:, t, :], z1[:, t, :], mv[:, t, 0:1], rs[:, t:t + 1],
                                               ALU.subtract, ALU.mult))
                dve.wait_ge(dve_own, own.at)
                dve.tensor_tensor(xn[:, b], z2[:], lnw[:].rearrange("p (a e) -> p a e", a=1).broadcast_to([P, 2, E]),
                                  ALU.mult).then_inc(xn_ready, 1)

            def queries(b, bt):
                dve.wait_ge(xnT_ready, 2 * bt + 2)
                for h in range(NH):
                    last = dve.tensor_scalar(qa[:, b, h, :], xa[:, b, :], w2a[:, h:h + 1], None, ALU.mult)
                last.then_inc(qa_ready, 1)

            def maxima(u, U):
                sl = u % 2
                dve.wait_ge(scores_main, U + 1)
                dve.tensor_reduce(nmax[:, sl, 0:GRP], bank[0][:, :].rearrange("p (j t) -> p j t", j=GRP), AX.X,
                                  ALU.max, negate=True).then_inc(max_main, 1)
                dve.wait_ge(scores_tail, U + 1)
                dve.tensor_reduce(nmax[:, sl, GRP:GRP + 2], bank[1][:, 0:2 * S].rearrange("p (j t) -> p j t", j=2),
                                  AX.X, ALU.max, negate=True).then_inc(max_tail, 1)

            def divide(u, U):
                sl = u % 2
                dve.wait_ge(exp_main, U + 1)
                dve.wait_ge(exp_tail, U + 1)
                link(dve.reciprocal(rsum[:], psums[:, sl, :]))
                dve.tensor_tensor(pm[:, sl], pm[:, sl],
                                  rsum[:, 0:GRP].rearrange("p (j a) -> p j a", a=1).broadcast_to([P, GRP, P]),
                                  ALU.mult).then_inc(prob_main, 1)
                dve.tensor_tensor(pt[:, sl], pt[:, sl],
                                  rsum[:, GRP:GRP + 2].rearrange("p (j a) -> p j a", a=1).broadcast_to([P, 2, S]),
                                  ALU.mult).then_inc(prob_tail, 1)

            def tails_out(u, U):
                at = P if u < UPB else 0
                dve.wait_ge(turned_tail, U + 1)
                for half in range(2):
                    src = bank[3][:, 0:2 * P].rearrange("p (k a t) -> p k a t", k=2, a=2)[:, :, half, 0:TAIL]
                    last = dve.tensor_copy(pT0[:, 2 * half:2 * half + 2, at:at + TAIL], src)
                last.then_inc(probT_tail, 1)
                for half in range(2):
                    src = bank[3][0:TAIL, 2 * P:4 * P].rearrange("p (k a t) -> p k a t", k=2, a=2)[:, :, half, 0:TAIL]
                    last = dve.tensor_copy(pT1[0:TAIL, 2 * half:2 * half + 2, :], src)
                last.then_inc(probT_tail, 1)

            def mix_out(u, U):
                g, b = u % UPB, u // UPB
                dve.wait_ge(pv_done, 3 * U + 2)
                dve.tensor_copy(oT[:, 6 * g + 3:6 * g + 5, b * S:(b + 1) * S],
                                bank[5][:, 0:2 * S].rearrange("p (j t) -> p j t", j=2)).then_inc(ot_dve, 1)
                dve.wait_ge(pv_done, 3 * U + 3)
                dve.tensor_copy(oT[:, 6 * g + 2:6 * g + 6:3, b * S:(b + 1) * S],
                                bank[6][:, 0:2 * S].rearrange("p (q t) -> p q t", q=2)).then_inc(ot_dve, 1)

            def residual(i):
                for t in range(3):
                    dve.wait_ge(wo_done, 2 * i + (1 if t < 2 else 2))
                    n, m = COLS[t][1], t // 2
                    src = bank[4][:, t * E:(t + 1) * E] if t < 2 else bank[5][0:n, 0:E]
                    old = hin[:, 2 * i + t, 0, :] if t < 2 else htail[0:n, i, :]
                    dve.scalar_tensor_tensor(out=R[0:n, 3 * i + t, :], in0=src, scalar=nreg[0:n, m:m + 1], in1=old,
                                             op0=ALU.mult, op1=ALU.add).then_inc(proj_read, 1)

            normalise(0, 0, hin[:, 0])
            queries(0, 0)
            normalise(1, 1, hin[:, 1])
            maxima(0, 0)
            queries(1, 1)

            def pair(i, last):
                U = UPP * i
                for u in range(UPP - 1):
                    divide(u, U + u)
                    maxima(u + 1, U + u + 1)
                    if u >= 1:
                        mix_out(u - 1, U + u - 1)
                    tails_out(u, U + u)
                    if u == 3 and not last:
                        normalise(0, 2 * i + 2, hin[:, 2 * i + 2])
                    if u == 4 and not last:
                        queries(0, 2 * i + 2)
                divide(5, U + 5)
                mix_out(4, U + 4)
                tails_out(5, U + 5)
                if not last:
                    maxima(0, U + 6)
                mix_out(5, U + 5)
                if not last:
                    normalise(1, 2 * i + 3, hin[:, 2 * i + 3])
                else:
                    dve.wait_ge(wte_in, 16 * B)
                    dve.wait_ge(wte_rest, 16)
                    link(dve.tensor_reduce(wsum[:], wacc[:].rearrange("p r e -> p e r"), AX.X, ALU.add))
                    dve.tensor_tensor(wsum[:], wsum[:], wrest[:], ALU.add).then_inc(wsum_ready, 1)
                residual(i)
                if not last:
                    queries(1, 2 * i + 3)

            start = own.at
            per = UPP + 2 * 12
            with dve.Fori(0, PAIRS - 1) as i:
                own.restart(per * i + start)
                pair(i, False)
                assert own.n == per
            own.restart(start + per * (PAIRS - 1))
            pair(PAIRS - 1, True)

            def logits(i):
                dve.wait_ge(gate_psum, i + 1)
                dve.tensor_tensor(lg[:, 3 * i:3 * i + 2, :], bank[4][:, 0:2 * NE].rearrange("p (t e) -> p t e", t=2),
                                  gbb[:].rearrange("p (a e) -> p a e", a=1).broadcast_to([P, 2, NE]), ALU.add)
                dve.tensor_tensor(lg[0:TT, 3 * i + 2, :], bank[4][0:TT, 2 * NE:3 * NE], gbb[0:TT, :],
                                  ALU.add).then_inc(gate_ready, 1)

            dve.wait_ge(avg_psum, 1)
            dve.tensor_copy(avg[:], bank[7][:, 0:2]).then_inc(avg_ready, 1)
            dve.wait_ge(c_psum, 1)
            link(dve.tensor_copy(cbc[:], bank[6][:, 0:E]))
            dve.wait_ge(proj_read, 3 * PAIRS + 1)
            for i in range(PAIRS):
                tiles = [R[0:COLS[t][1], 3 * i + t, :] for t in range(3)]
                for t in range(3):
                    n, m = COLS[t][1], t // 2
                    own.mark(dve.scalar_tensor_tensor(out=tiles[t], in0=cbc[0:n, :], scalar=nnreg[0:n, m:m + 1],
                                                      in1=tiles[t], op0=ALU.mult, op1=ALU.add))
                dve.wait_ge(dve_own, own.at)
                stats(tiles, 2 * B + i + 1)
                if i >= 2:
                    dve.wait_ge(xfT_psum, i - 1)
                for t in range(3):
                    n = COLS[t][1]
                    last = dve.tensor_scalar(xf[0:n, i % 2, t, :], tiles[t], mv[0:n, t, 0:1], rs[0:n, t:t + 1],
                                             ALU.subtract, ALU.mult)
                last.then_inc(xf_ready, 1)
                dve.wait_ge(xfT_psum, i + 1)
                dve.tensor_copy(fb[:, i, :], bank[2 + i % 2][0:64, 0:CW]).then_inc(xfT_dve, 1)
                if i >= 1:
                    logits(i - 1)
            logits(PAIRS - 1)

            def rows(v, n):
                return v.rearrange("p (t a) -> p t a", a=1).broadcast_to([P, NT, n])

            dve.wait_ge(gate_ready, PAIRS)
            link(dve.tensor_reduce(mx[:], lg[:], AX.X, ALU.max))
            dve.tensor_tensor(lg[:], lg[:], rows(mx[:], NE), ALU.subtract).then_inc(nmx_ready, 1)
            dve.wait_ge(gexp, 1)
            link(dve.tensor_reduce(mx[:], sc[:], AX.X, ALU.add))
            link(dve.reciprocal(mx[:], mx[:]))
            link(dve.tensor_tensor(sc[:], sc[:], rows(mx[:], NE), ALU.mult))
            link(dve.tensor_tensor(sel[:], sc[:], rbias[:].rearrange("p (a e) -> p a e", a=1).broadcast_to([P, NT, NE]),
                                   ALU.add))
            link(dve.tensor_reduce(gs[:], sel[:].rearrange("p t (g a) -> p t g a", a=2), AX.X, ALU.add))

            def ranks(v, n, t):
                mine = v[:, t, :].rearrange("p (g a) -> p g a", a=1).broadcast_to([P, n, n])
                other = v[:, t, :].rearrange("p (a g) -> p a g", a=1).broadcast_to([P, n, n])
                a, c = cmp[:, 0:n, 0:n], cmp2[:, 0:n, 0:n]
                own.mark(dve.tensor_tensor(a, other, mine, ALU.is_gt))
                link(dve.tensor_tensor(c, other, mine, ALU.is_equal))
                link(dve.tensor_tensor(c, c, before[:, 0:n, 0:n], ALU.mult))
                link(dve.tensor_tensor(a, a, c, ALU.add))
                link(dve.tensor_reduce(rank[:, t, 0:n], a, AX.X, ALU.add))

            for t in range(NT):
                ranks(gs, TG, t)
            link(dve.tensor_scalar(gs[:], rank[:, :, 0:TG], float(TOPK), None, ALU.is_lt))
            pairs = gs[:].rearrange("p t (g a) -> p t g a", a=1).broadcast_to([P, NT, TG, 2])
            link(dve.tensor_tensor(sel[:].rearrange("p t (g a) -> p t g a", a=2),
                                   sel[:].rearrange("p t (g a) -> p t g a", a=2), pairs, ALU.mult))
            link(dve.tensor_scalar(gs[:], gs[:], -1.0, -NEVER, ALU.add, ALU.mult))
            link(dve.tensor_tensor(sel[:].rearrange("p t (g a) -> p t g a", a=2),
                                   sel[:].rearrange("p t (g a) -> p t g a", a=2), pairs, ALU.add))
            for t in range(NT):
                ranks(sel, NE, t)
            link(dve.tensor_scalar(rank[:], rank[:], float(TOPK), ROUTE, ALU.is_lt, ALU.mult))
            dve.tensor_tensor(wts[:, :, 0:NE], rank[:], sc[:], ALU.mult).then_inc(wts_ready, 1)
            dve.wait_ge(wts_ready, 1)

            def fuse(n, st_):
                sl = n % 2
                dve.wait_ge(gt_ready, st_ + 1)
                dve.wait_ge(silu_ready, st_ + 1)
                if n >= 2:
                    dve.wait_ge(down_done, 2 * (st_ - 1))
                dve.scalar_tensor_tensor(out=hidT[:, sl, 0:CW], in0=bank[2 + sl][:, 0:CW],
                                         scalar=bcol[:, (n // PAIRS) % 2, 1:2], in1=sil[:, sl, :], op0=ALU.add,
                                         op1=ALU.mult).then_inc(hid_ready, 1)

            def gather(n, st_, e):
                sl, i = n % 2, n % PAIRS
                for t in range(3):
                    rows_ = COLS[t][1]
                    if t != 1:
                        dve.wait_ge(down_done, 2 * st_ + (1 if t < 2 else 2))
                    src = bank[4 + sl][:, t * E:(t + 1) * E] if t < 2 else bank[6 + sl][0:TT, 0:E]
                    if t == 0:
                        dve.wait_ge(acc_done, 2 * (st_ - PAIRS + 1)) if n >= PAIRS else None
                    old = R[0:rows_, 3 * i + t, :]
                    last = dve.scalar_tensor_tensor(out=old, in0=src,
                                                    scalar=wts[0:rows_, 3 * i + t, bass.ds(e, 1)], in1=old,
                                                    op0=ALU.mult, op1=ALU.add)
                    if t >= 1:
                        last.then_inc(acc_done, 1)

            dve.wait_ge(w_in[0], 16 * WLOADS)
            fuse(0, 0)
            for n in range(PAIRS):
                if n == PAIRS - 1:
                    dve.wait_ge(w_in[1], 16 * WLOADS)
                fuse(n + 1, n + 1)
                gather(n, n, NE)

            for t in range(NT):
                dve.wait_ge(wT_psum, t + 1)
                dve.tensor_copy(wT[:, t, :], bank[4 + t % 2][0:NW, 0:P]).then_inc(wT_ready, 1)
            dve.wait_ge(acc_done, 2 * PAIRS)
            for t in range(NT):
                dve.wait_ge(bias_psum, t + 1)
                dve.tensor_tensor(R[0:COLS[t % 3][1], t, :], bank[6 + t % 2][0:COLS[t % 3][1], 0:E],
                                  R[0:COLS[t % 3][1], t, :], ALU.add).then_inc(bias_added, 1)
            dve.wait_ge(bias_added, NT)

            def two_experts(j, last):
                for m in range(2 * PAIRS):
                    n, s_ = PAIRS + m, 2 * PAIRS * j + PAIRS + m
                    if m == PAIRS - 1:
                        dve.wait_ge(w_in[0], 16 * WLOADS * j + 32 * WLOADS)
                    if m == 2 * PAIRS - 1 and not last:
                        dve.wait_ge(w_in[1], 16 * WLOADS * j + 32 * WLOADS)
                    if not (last and m == 2 * PAIRS - 1):
                        fuse(n + 1, s_ + 1)
                    gather(n, s_, 2 * j + m // PAIRS)

            with dve.Fori(0, NE // 2 - 1) as j:
                two_experts(j, False)
            two_experts(NE // 2 - 1, True)


_INS = ['x', 'txt', 'L0_tok_W', 'L0_tok_b', 'L0_tok_positions', 'L0_tok_cls_embedding', 'L0_attn_ln_w', 'L0_attn_W_qk',
        'L0_attn_W_o', 'L0_attn_wte', 'L0_ffn_gate_w', 'L0_ffn_gate_b', 'L0_ffn_bias', 'L0_ffn_Wu', 'L0_ffn_bu',
        'L0_ffn_Wg', 'L0_ffn_bg', 'L0_ffn_Wd', 'L0_ffn_bd', 'L0_ffn_sWu', 'L0_ffn_sbu', 'L0_ffn_sWg', 'L0_ffn_sbg',
        'L0_ffn_sWd', 'L0_ffn_sbd']
_OUTS = [((8, 178, 192), 'float32')]


def kernel(**inputs):
    import numpy as _np
    import concourse.bacc as _bacc
    from concourse import mybir as _mybir
    from concourse.bass_utils import run_bass_kernel_spmd as _run

    nc = _bacc.Bacc("TRN2", target_bir_lowering=False, num_devices=1)
    arrays, args = {}, []
    for name in _INS:
        a = _np.ascontiguousarray(inputs[name])
        arrays[f"in_{name}_dram"] = a
        args.append(nc.dram_tensor(f"in_{name}_dram", a.shape, _mybir.dt.from_np(a.dtype), kind="ExternalInput").ap())
    for i, (shape, dtype) in enumerate(_OUTS):
        dt = _mybir.dt.from_np(_np.dtype(dtype))
        args.append(nc.dram_tensor(f"out_{i}_dram", shape, dt, kind="ExternalOutput").ap())
    early_fusion_kernel(nc, *args)
    r = _run(nc, [arrays], core_ids=[0])
    return r.results[0]["out_0_dram"]
```

```python
from contextlib import ExitStack

import concourse.bass as bass
from concourse import mybir

F32 = mybir.dt.float32
F32R = mybir.dt.float32r
BF16 = mybir.dt.bfloat16
ALU = mybir.AluOpType
ACT = mybir.ActivationFunctionType
AX = mybir.AxisListType

P = 128
EPS = 1e-5
MASKED = -1e30
NEVER = -3e38


class Tally:

    def __init__(self, sem):
        self.sem, self.base, self.n = sem, 0, 0

    @property
    def at(self):
        return self.base + self.n

    def mark(self, ins):
        ins.then_inc(self.sem, 1)
        self.n += 1

    def restart(self, base):
        self.base, self.n = base, 0


def early_fusion_kernel(nc, x, txt, tok_W, tok_b, tok_pos, tok_cls, ln_w, W_qk, W_o, wte,
                        gate_w, gate_b, bias, Wu, bu, Wg, bg, Wd, bd, sWu, sbu, sWg, sbg, sWd, sbd, out):
    B, C, HI, WI = x.shape
    NTXT, E = txt.shape[1:]
    PS = 16
    G = HI // PS
    NIMG = 1 + G * G
    S = NIMG + NTXT
    TAIL = S - P
    NH = W_qk.shape[0]
    EB = E - P
    V = wte.shape[0]
    NE = Wu.shape[0]
    HID = Wu.shape[2]
    PAIRS = B // 2
    GRP = 4
    UPB = NH // GRP
    UPP = 2 * UPB
    SP = P + 64
    CW = 2 * S
    TT = 2 * TAIL
    COLS = [(0, P), (CW - P, P), (P, TT)]
    NCH = NH * E // P
    SCALE = float(E) ** -0.5
    KC = C * PS * PS // P
    BG = B * G
    WROWS = V // P
    WR = 49
    WREST = V - P * WROWS
    assert TAIL <= 64 and EB == 64 and HID == P and WROWS == WR * B and NH == GRP * UPB
    NT = 3 * PAIRS
    TG = NE // 2
    TOPK = 4
    ROUTE = 2.5
    NW = NE + 1

    with ExitStack() as ctx:
        def sb(name, shape, dt=F32):
            return ctx.enter_context(nc.sbuf_tensor(name, shape, dt))

        def sem(name):
            return ctx.enter_context(nc.semaphore(name))

        bank = [ctx.enter_context(nc.psum_tensor(f"bank{n}", [P, 512], F32)) for n in range(8)]

        ident = sb("ident", [P, P])
        identb = sb("identb", [P, P], BF16)
        cmask = sb("cmask", [P, P], BF16)
        tmask = sb("tmask", [P, 64], BF16)
        ones = sb("ones", [P, P])
        mhalf = sb("mhalf", [P, 4])
        vmean = sb("vmean", [P, 1])
        nregi = sb("nregi", [P, 2], mybir.dt.int32)
        nregf = sb("nregf", [P, 2])
        firsthalf = sb("firsthalf", [P, 1])
        nreg = sb("nreg", [P, 2])
        nnreg = sb("nnreg", [P, 2])
        upper = sb("upper", [P, 1])
        sign = sb("sign", [P, 1])
        wtok = sb("wtok", [P, KC, E])
        brow = sb("brow", [1, E])
        posr = sb("posr", [P, 2, 4 * G * G])
        posx = sb("posx", [P, 2, G, B, G])
        area_a = sb("area_a", [P, 2 * NH * SP])
        area_b = sb("area_b", [P, C * PS * WI])

        def part_of(area, at, *shape):
            n = 1
            for d in shape[1:]:
                n *= d
            names = "abcd"[:len(shape) - 1]
            dims = {c: d for c, d in zip(names, shape[1:])}
            return area[0:shape[0], at:at + n].rearrange(f"p ({' '.join(names)}) -> p {' '.join(names)}", **dims)

        wo_raw = part_of(area_a, 0, P, 2, NCH, P)
        xpat = part_of(area_b, 0, BG, C, G, PS * PS)
        woT = sb("woT", [P, NCH, E])
        wqk = sb("wqk", [NH, E])
        w2a = sb("w2a", [P, NH])
        w2b = sb("w2b", [64, NH])
        lnw = sb("lnw", [P, E])
        gwa = sb("gwa", [P, NE])
        gwb = sb("gwb", [64, NE])
        gbb = sb("gbb", [P, NE])
        rbias = sb("rbias", [P, NE])
        bdx = sb("bdx", [NW, E])
        patT = sb("patT", [P, 2, KC, BG])
        emb = sb("emb", [BG, G, E])
        hin = sb("hin", [P, B, 2, E])
        htail = sb("htail", [P, PAIRS, E])
        R = sb("R", [P, NT, E])
        z = sb("z", [P, 2, 2, E])
        st = sb("st", [P, 4, 6])
        mv = sb("mv", [P, 4, 2])
        pause = sb("pause", [P, 1])
        ve = sb("ve", [P, 4])
        rs = sb("rs", [P, 4])
        xn = sb("xn", [P, 2, 2, E])
        xa = sb("xa", [P, 2, SP])
        xb = sb("xb", [64, 2, SP])
        qa = part_of(area_a, 0, P, 2, NH, SP)
        qb = part_of(area_b, 0, 64, 2, NH, SP)
        nmax = sb("nmax", [P, 2, 6])
        psums = sb("psums", [P, 2, 6])
        rsum = sb("rsum", [P, 6])
        pm = sb("pm", [P, 2, GRP, P])
        pt = sb("pt", [P, 2, 2, S])
        pT0 = sb("pT0", [P, GRP, S])
        pT1 = sb("pT1", [64, GRP, TAIL])
        oT = sb("oT", [P, NCH, CW])
        ximg = oT[0:BG].rearrange("p c t -> p (c t)")[:, 0:C * PS * WI].rearrange("p (c w) -> p c w", c=C)
        wrest = sb("wrest", [P, E])
        avg = sb("avg", [P, 2])
        cbc = sb("cbc", [P, E])
        fa = part_of(area_a, 0, P, PAIRS, CW)
        fb = part_of(area_a, PAIRS * CW, P, PAIRS, CW)
        xf = hin[:].rearrange("p b c e -> p (b c e)").rearrange("p (i t e) -> p i t e", i=PAIRS, t=3)
        lg = sb("lg", [P, NT, NE])
        mx = sb("mx", [P, NT])
        sc = sb("sc", [P, NT, NE])
        sel = sb("sel", [P, NT, NE])
        gs = sb("gs", [P, NT, TG])
        top8 = sb("top8", [P, NT, 8])
        above = sb("above", [P, NT, NE])
        tied = sb("tied", [P, NT, NE])
        room = sb("room", [P, NT])
        PAD = 8
        scan = sb("scan", [P, 2, NT, PAD + NE])
        wts = sb("wts", [P, NT, NW])
        wT = part_of(area_b, 0, NW, NT, P)
        bias_bank = [bank[n] for n in (7, 4, 5, 6, 7, 4)]
        wra = sb("wra", [P, 2, 2, HID])
        wrb = sb("wrb", [P, 2, 2, HID])
        wdn = sb("wdn", [P, 2, E])
        bcol = sb("bcol", [P, 2, 2])
        sil = part_of(area_b, NT * P, P, 2, CW)
        hidT = sb("hidT", [P, 2, CW])
        with nc.sbuf_tensor("wacc", [P, WR, E], F32) as wacc:
            pass
        xah = sb("xah", [P, PAIRS, CW], F32R)
        xal = sb("xal", [P, PAIRS, CW], F32R)
        xbh = sb("xbh", [P, PAIRS, CW], F32R)
        xbl = sb("xbl", [P, PAIRS, CW], F32R)
        wah = sb("wah", [P, 2, 2, HID], F32R)
        wal = sb("wal", [P, 2, 2, HID], F32R)
        wbs = sb("wbs", [P, 2, 2, HID], F32R)
        wbt = sb("wbt", [P, 2, HID], F32R)

        s_const = sem("s_const")
        s_x = sem("s_x")
        s_tokw = sem("s_tokw")
        s_xpat = sem("s_xpat")
        s_pos = sem("s_pos")
        s_wo = sem("s_wo")
        s_small = sem("s_small")
        s_small2 = sem("s_small2")
        s_text = sem("s_text")
        s_emb = sem("s_emb")
        s_zero = sem("s_zero")
        s_posx = sem("s_posx")
        s_patps = sem("s_patps")
        s_patT = sem("s_patT")
        s_embps = sem("s_embps")
        s_embsb = sem("s_embsb")
        s_wops = sem("s_wops")
        s_woT = sem("s_woT")
        s_wqps = sem("s_wqps")
        s_w2 = sem("s_w2")
        var_ready = sem("var_ready")
        rstd_ready = sem("rstd_ready")
        z_ready = sem("z_ready")
        xn_ready = sem("xn_ready")
        xnT_psum = sem("xnT_psum")
        xnT_ready = sem("xnT_ready")
        qa_ready = sem("qa_ready")
        qb_ready = sem("qb_ready")
        scores_main = sem("scores_main")
        scores_tail = sem("scores_tail")
        max_main = sem("max_main")
        max_tail = sem("max_tail")
        exp_main = sem("exp_main")
        exp_tail = sem("exp_tail")
        prob_main = sem("prob_main")
        prob_tail = sem("prob_tail")
        turned_main = sem("turned_main")
        turned_tail = sem("turned_tail")
        probT_main = sem("probT_main")
        probT_tail = sem("probT_tail")
        pv_done = sem("pv_done")
        ot_act = sem("ot_act")
        ot_dve = sem("ot_dve")
        wo_done = sem("wo_done")
        proj_read = sem("proj_read")
        wte_in = sem("wte_in")
        wte_rest = sem("wte_rest")
        wsum_ready = sem("wsum_ready")
        avg_psum = sem("avg_psum")
        avg_ready = sem("avg_ready")
        c_psum = sem("c_psum")
        xf_ready = sem("xf_ready")
        xfT_psum = sem("xfT_psum")
        xfT_act = sem("xfT_act")
        xfT_dve = sem("xfT_dve")
        x_low = sem("x_low")
        gate_psum = sem("gate_psum")
        gate_ready = sem("gate_ready")
        nmx_ready = sem("nmx_ready")
        gexp = sem("gexp")
        wts_ready = sem("wts_ready")
        wT_psum = sem("wT_psum")
        wT_ready = sem("wT_ready")
        bias_psum = sem("bias_psum")
        bias_added = sem("bias_added")
        w_in = [sem("w_in0"), sem("w_in1")]
        wd_in = [sem("wd_in0"), sem("wd_in1")]
        wh_ready = sem("wh_ready")
        wal_ready = sem("wal_ready")
        wbs_ready = sem("wbs_ready")
        up_ready = sem("up_ready")
        gt_ready = sem("gt_ready")
        silu_ready = sem("silu_ready")
        hid_ready = sem("hid_ready")
        down_done = sem("down_done")
        acc_done = sem("acc_done")
        out_done = sem("out_done")
        dve_own = sem("dve_own")
        pool_own = sem("pool_own")

        WLOADS = 6
        DLOADS = 3
        block = ctx.enter_context(nc.Block())

        @block.sync
        def _(sp):
            for b in range(B // 2):
                sp.dma_start(ximg[b * G:(b + 1) * G, :, :],
                             x[b].rearrange("c (g p) w -> g c (p w)", p=PS)).then_inc(s_x, 16)
            sp.dma_start(wtok[:], tok_W.rearrange("(k p) e -> p k e", p=P)).then_inc(s_tokw, 16)
            sp.dma_start(brow[:], tok_b.rearrange("(a e) -> a e", a=1)).then_inc(s_tokw, 16)
            sp.wait_ge(s_zero, 2)
            TM = P - NIMG
            for b in range(B):
                sp.dma_start(hin[0:1, b, 0, :], tok_cls[0]).then_inc(s_text, 16)
                sp.dma_start(hin[NIMG:P, b, 0, :], txt[b, 0:TM, :]).then_inc(s_text, 16)
                sp.dma_start(hin[0:TAIL, b, 1, :], txt[b, TM:NTXT, :]).then_inc(s_text, 16)
                sp.dma_start(htail[TAIL * (b % 2):TAIL * (b % 2) + TAIL, b // 2, :], txt[b, TM:NTXT, :]).then_inc(s_text, 16)
            sp.wait_ge(s_embsb, G)
            for b in range(B):
                sp.dma_start(hin[1:NIMG, b, 0, :], emb[b * G:(b + 1) * G, :, :]).then_inc(s_emb, 16)

            def load_in(slot, up, gt):
                for c, w in enumerate((up, gt)):
                    sp.dma_start(wra[:, slot, c, :], w[0:P, :]).then_inc(w_in[slot], 16)
                    sp.dma_start(wrb[0:64, slot, c, :], w[P:E, :]).then_inc(w_in[slot], 16)
                    sp.dma_start(wrb[64:P, slot, c, :], w[P:E, :]).then_inc(w_in[slot], 16)

            def load_down(slot, dn, b1, b2):
                sp.dma_start(wdn[:, slot, :], dn).then_inc(wd_in[slot], 16)
                sp.dma_start(bcol[:, slot, 0:1], b1).then_inc(wd_in[slot], 16)
                sp.dma_start(bcol[:, slot, 1:2], b2).then_inc(wd_in[slot], 16)

            def routed_in(slot, e):
                load_in(slot, Wu[bass.ds(e, 1)].rearrange("a k h -> (a k) h"),
                        Wg[bass.ds(e, 1)].rearrange("a k h -> (a k) h"))

            def routed_down(slot, e):
                load_down(slot, Wd[bass.ds(e, 1)].rearrange("a k h -> (a k) h"),
                          bu[bass.ds(e, 1)].rearrange("a h -> h a"), bg[bass.ds(e, 1)].rearrange("a h -> h a"))

            def split_done(k):
                sp.wait_ge(wal_ready, k + 1)
                sp.wait_ge(wbs_ready, k + 1)

            load_in(0, sWu, sWg)
            load_down(0, sWd, sbu.rearrange("(h a) -> h a", a=1), sbg.rearrange("(h a) -> h a", a=1))
            routed_in(1, 0)
            routed_down(1, 0)
            split_done(0)
            routed_in(0, 1)
            with sp.Fori(0, (NE - 2) // 2) as j:
                sp.wait_ge(down_done, 16 * j + 8)
                routed_down(0, 2 * j + 1)
                split_done(2 * j + 1)
                routed_in(1, 2 * j + 2)
                sp.wait_ge(down_done, 16 * j + 16)
                routed_down(1, 2 * j + 2)
                split_done(2 * j + 2)
                routed_in(0, 2 * j + 3)
            sp.wait_ge(down_done, 8 * (NE - 1))
            routed_down(0, NE - 1)
            for i in range(PAIRS):
                sp.wait_ge(acc_done, 2 * (PAIRS * NE + i + 1))
                for k in range(2):
                    sp.dma_start(out[2 * i + k, 0:P, :], R[:, 3 * i + k, :]).then_inc(out_done, 16)
                    sp.dma_start(out[2 * i + k, P:S, :], R[TAIL * k:TAIL * k + TAIL, 3 * i + 2, :]).then_inc(out_done, 16)
            sp.wait_ge(out_done, 16 * 4 * PAIRS)

        @block.gpsimd
        def _(pool):
            own = Tally(pool_own)
            wte_v = wte[0:P * WROWS, :].rearrange("(p c r) e -> c p r e", p=P, r=WR)
            own.mark(pool.memset(ident[:], 0.0))
            own.mark(pool.memset(cmask[:], 0.0))
            own.mark(pool.memset(tmask[:], 0.0))
            own.mark(pool.memset(wrest[:], 0.0))
            own.mark(pool.memset(upper[:], 0.0))
            own.mark(pool.memset(sign[:], 1.0))
            pool.wait_ge(pool_own, own.at)
            own.mark(pool.affine_select(out=ident[:], in_=ident[:], compare_op=ALU.not_equal, fill=1.0,
                                        base=0, pattern=[[-1, P]], channel_multiplier=1))
            own.mark(pool.affine_select(out=cmask[:], in_=cmask[:], compare_op=ALU.is_ge, fill=MASKED,
                                        base=0, pattern=[[-1, P]], channel_multiplier=1))
            own.mark(pool.affine_select(out=tmask[0:64, :], in_=tmask[0:64, :], compare_op=ALU.is_ge, fill=MASKED,
                                        base=0, pattern=[[-1, 64]], channel_multiplier=1))
            pool.wait_ge(pool_own, own.at)
            own.mark(pool.affine_select(out=tmask[64:P, :], in_=tmask[64:P, :], compare_op=ALU.is_ge, fill=MASKED,
                                        base=0, pattern=[[-1, 64]], channel_multiplier=1))
            pool.wait_ge(pool_own, own.at)
            own.mark(pool.affine_select(out=upper[:], in_=upper[:], compare_op=ALU.is_gt, fill=1.0,
                                        base=64, pattern=[[0, 1]], channel_multiplier=-1))
            own.mark(pool.affine_select(out=sign[:], in_=sign[:], compare_op=ALU.is_gt, fill=-1.0,
                                        base=64, pattern=[[0, 1]], channel_multiplier=-1))
            own.mark(pool.memset(ones[:], 1.0))
            own.mark(pool.memset(mhalf[:], -0.5))
            own.mark(pool.memset(vmean[:], 1.0 / V))
            own.mark(pool.iota(nregi[:, 0:1], pattern=[[0, 1]], base=1, channel_multiplier=1))
            own.mark(pool.iota(nregi[:, 1:2], pattern=[[0, 1]], base=P + 1 - TAIL, channel_multiplier=1))
            own.mark(pool.memset(firsthalf[:], 0.0))
            pool.wait_ge(pool_own, own.at)
            own.mark(pool.affine_select(out=firsthalf[:], in_=firsthalf[:], compare_op=ALU.is_ge, fill=float(TAIL),
                                        base=-TAIL, pattern=[[0, 1]], channel_multiplier=1))
            own.mark(pool.tensor_copy(identb[:], ident[:]))
            own.mark(pool.tensor_copy(nregf[:], nregi[:]))
            pool.wait_ge(pool_own, own.at)
            own.mark(pool.tensor_tensor(nregf[:, 1:2], nregf[:, 1:2], firsthalf[:], ALU.add))
            pool.wait_ge(pool_own, own.at)
            for i in range(PAIRS):
                own.mark(pool.memset(R[:, 3 * i + 2, :], 0.0))
            pool.wait_ge(pool_own, own.at)
            pool.memset(wts[:], 1.0).then_inc(s_const, 1)
            pool.wait_ge(s_x, 16 * B)
            pool.dma_start(wacc[:], wte_v[0]).then_inc(wte_in, 16)
            pool.dma_start(wrest[0:WREST, :], wte[P * WROWS:V, :]).then_inc(wte_rest, 16)

            def rstd(n, count):
                pool.wait_ge(var_ready, count)
                pool.tensor_tensor(rs[:, 0:n], ve[:, 0:n], mhalf[:, 0:n], ALU.pow).then_inc(rstd_ready, 1)

            def batch(bt, b):
                pool.wait_ge(xnT_ready, 2 * bt + 2)
                for h in range(NH):
                    last = (pool.tensor_tensor(qb[:, b, 0, :], xb[:, b, :], w2b[:, 0:1].broadcast_to([64, SP]), ALU.mult)
                            if h == 0 else
                            pool.tensor_scalar(qb[:, b, h, :], xb[:, b, :], w2b[:, h:h + 1], None, ALU.mult))
                    if h % GRP == GRP - 1:
                        last.then_inc(qb_ready, 1)

            def add_rows(c):
                pool.wait_ge(wte_in, 16 * c)
                pool.dma_start(wacc[:], wte_v[bass.ds(c, 1)].rearrange("a p r e -> (a p) r e"),
                               accum_op=ALU.add, max_dma_last_dim=4 * WR * E // 6).then_inc(wte_in, 16)

            pool.wait_ge(s_w2, 2)
            rstd(4, 1)
            rstd(4, 2)
            batch(0, 0)
            add_rows(1)
            batch(1, 1)
            with pool.Fori(0, PAIRS - 1) as i:
                add_rows(2 * i + 2)
                rstd(4, 2 * i + 3)
                rstd(4, 2 * i + 4)
                batch(2 * i + 2, 0)
                add_rows(2 * i + 3)
                batch(2 * i + 3, 1)
            pool.wait_ge(wte_in, 16 * B)
            n = WR // 2
            while n >= 3:
                own.mark(pool.tensor_tensor(wacc[:, 0:n, :], wacc[:, 0:n, :], wacc[:, n:2 * n, :], ALU.add))
                pool.wait_ge(pool_own, own.at)
                n //= 2
            pool.wait_ge(wte_rest, 16)
            pool.memset(mhalf[:, 3:4], -0.5).then_inc(wsum_ready, 1)

            def x_lows(i):
                pool.wait_ge(xfT_act, 2 * i + 2)
                pool.tensor_tensor(xal[:, i], fa[:, i], xah[:, i].bitcast(F32), ALU.subtract).then_inc(x_low, 1)
                pool.wait_ge(xfT_dve, 2 * i + 2)
                pool.tensor_tensor(xbl[:, i], fb[:, i], xbh[:, i].bitcast(F32), ALU.subtract).then_inc(x_low, 1)

            for i in range(PAIRS):
                rstd(3, 2 * PAIRS + i + 1)
            for i in range(PAIRS):
                x_lows(i)

            def w_low(slot, k):
                pool.wait_ge(wh_ready, 2 * k + 1)
                pool.tensor_tensor(wal[:, slot], wra[:, slot], wah[:, slot].bitcast(F32),
                                   ALU.subtract).then_inc(wal_ready, 1)

            w_low(0, 0)
            w_low(1, 1)
            with pool.Fori(0, NE // 2 - 1) as j:
                w_low(0, 2 * j + 2)
                w_low(1, 2 * j + 3)
            w_low(0, NE)

        @block.scalar
        def _(act):
            for b in range(B // 2, B):
                act.dma_start(ximg[b * G:(b + 1) * G, :, :],
                              x[b].rearrange("c (g p) w -> g c (p w)", p=PS)).then_inc(s_x, 16)
            act.dma_start(posr[:, 0, :], tok_pos[0, 0:P].rearrange("d h w -> d (h w)")).then_inc(s_pos, 16)
            act.dma_start(posr[0:64, 1, :], tok_pos[0, P:E].rearrange("d h w -> d (h w)")).then_inc(s_pos, 16)
            act.dma_start(wqk[:], W_qk).then_inc(s_small, 16)
            act.dma_start(lnw[:], ln_w.rearrange("(a e) -> a e", a=1).broadcast_to([P, E])).then_inc(s_small, 16)
            for part, rows in ((0, P), (1, 64)):
                src = W_o[P * part:P * part + rows, :].rearrange("o (q j e) -> o q j e", q=NH // 2, j=2)
                dst = wo_raw[0:rows, part].rearrange("o (q c) e -> o q c e", c=3)
                for j in range(2):
                    act.dma_start(dst[:, :, j, :], src[:, :, j, 0:P]).then_inc(s_wo, 16)
                    act.dma_start(dst[:, :, 2, 64 * j:64 * j + 64], src[:, :, j, P:E]).then_inc(s_wo, 16)
            act.dma_start(gwa[:], gate_w[0:P, :]).then_inc(s_small2, 16)
            act.dma_start(gwb[:], gate_w[P:E, :]).then_inc(s_small2, 16)
            act.dma_start(gbb[:], gate_b.rearrange("(a e) -> a e", a=1).broadcast_to([P, NE])).then_inc(s_small2, 16)
            act.dma_start(rbias[:], bias.rearrange("(a e) -> a e", a=1).broadcast_to([P, NE])).then_inc(s_small2, 16)
            act.dma_start(bdx[0:NE, :], bd).then_inc(s_small2, 16)
            act.dma_start(bdx[NE:NW, :], sbd.rearrange("(a e) -> a e", a=1)).then_inc(s_small2, 16)
            act.wait_ge(s_x, 16 * B)
            act.activation(xpat[:, 1].rearrange("t g (r w) -> t g r w", w=PS),
                           ximg[:, 1].rearrange("t (r g w) -> t g r w", g=G, w=PS), ACT.Copy).then_inc(s_xpat, 1)
            act.activation(xpat[:, 2].rearrange("t g (r w) -> t g r w", w=PS)[:, :, PS // 2:PS],
                           ximg[:, 2].rearrange("t (r g w) -> t g r w", g=G, w=PS)[:, :, PS // 2:PS],
                           ACT.Copy).then_inc(s_xpat, 1)
            for g in range(G):
                act.wait_ge(s_patps, g + 1)
                if g >= 2:
                    act.wait_ge(s_embps, g - 1)
                act.activation(patT[:, g % 2], bank[g % 2][:, 0:KC * BG].rearrange("p (k t) -> p k t", k=KC),
                               ACT.Copy).then_inc(s_patT, 1)
            for c in range(NCH):
                act.wait_ge(s_wops, c + 1)
                act.activation(woT[:, c, :], bank[4 + c % 2][:, 0:E],
                               ACT.Copy).then_inc(s_woT if c + 1 < NCH else proj_read, 1)

            def turn_out(b, bt):
                act.wait_ge(xnT_psum, bt + 1)
                act.activation(xa[:, b, :], bank[7][:, 0:SP], ACT.Copy).then_inc(xnT_ready, 1)
                act.activation(xb[:, b, :], bank[7][0:64, SP:2 * SP], ACT.Copy).then_inc(xnT_ready, 1)

            def exps(u, U):
                sl = u % 2
                act.wait_ge(max_main, U + 1)
                for j in range(GRP):
                    last = act.activation(pm[:, sl, j, :], bank[0][:, j * P:(j + 1) * P], ACT.Exp,
                                          bias=nmax[:, sl, j:j + 1], accum_out=psums[:, sl, j:j + 1])
                last.then_inc(exp_main, 1)
                act.wait_ge(max_tail, U + 1)
                for k in range(2):
                    last = act.activation(pt[:, sl, k, :], bank[1][:, k * S:(k + 1) * S], ACT.Exp,
                                          bias=nmax[:, sl, 4 + k:5 + k], accum_out=psums[:, sl, 4 + k:5 + k])
                last.then_inc(exp_tail, 1)

            def prob_out(u, U):
                act.wait_ge(turned_main, U + 1)
                at = 0 if u < UPB else TAIL
                act.activation(pT0[:, :, at:at + P], bank[2][:, :].rearrange("p (j t) -> p j t", j=GRP),
                               ACT.Copy).then_inc(probT_main, 1)

            def mix_out(u, U):
                g, b = u % UPB, u // UPB
                act.wait_ge(pv_done, 3 * U + 1)
                act.activation(oT[:, 6 * g:6 * g + 2, b * S:(b + 1) * S],
                               bank[4][:, 0:2 * S].rearrange("p (j t) -> p j t", j=2), ACT.Copy).then_inc(ot_act, 1)

            turn_out(0, 0)
            exps(0, 0)
            turn_out(1, 1)

            def pair(i, last):
                U = UPP * i
                for u in range(UPP - 1):
                    exps(u + 1, U + u + 1)
                    if u >= 1:
                        mix_out(u - 1, U + u - 1)
                    if u == 3 and not last:
                        turn_out(0, 2 * i + 2)
                    prob_out(u, U + u)
                mix_out(4, U + 4)
                if not last:
                    turn_out(1, 2 * i + 3)
                prob_out(5, U + 5)
                if not last:
                    exps(0, U + 6)
                mix_out(5, U + 5)

            with act.Fori(0, PAIRS - 1) as i:
                pair(i, False)
            pair(PAIRS - 1, True)

            act.wait_ge(avg_psum, 1)
            for i in range(PAIRS):
                act.wait_ge(xfT_psum, i + 1)
                act.activation(fa[:, i, :], bank[i % 2][:, 0:CW], ACT.Copy).then_inc(xfT_act, 1)
                act.activation(xah[:, i, :], bank[i % 2][:, 0:CW], ACT.Copy).then_inc(xfT_act, 1)
            act.wait_ge(w_in[0], 16 * WLOADS)
            act.activation(wah[:, 0], wra[:, 0], ACT.Copy).then_inc(wh_ready, 1)
            act.activation(wbt[:], wrb[:, 0], ACT.Copy, scale=sign[:, 0:1]).then_inc(wh_ready, 1)
            act.wait_ge(nmx_ready, 1)
            act.activation(sc[:], lg[:], ACT.Exp).then_inc(gexp, 1)

            def silu(st_, n):
                sl = n % 2
                act.wait_ge(up_ready, st_ + 1)
                if n >= 2:
                    act.wait_ge(hid_ready, st_ - 1)
                act.activation(sil[:, sl, :], bank[sl][:, 0:CW], ACT.Silu,
                               bias=bcol[:, (n // PAIRS) % 2, 0:1]).then_inc(silu_ready, 1)

            def w_high(slot, loads):
                act.wait_ge(w_in[slot], 16 * WLOADS * loads)
                act.activation(wah[:, slot], wra[:, slot], ACT.Copy).then_inc(wh_ready, 1)
                act.activation(wbt[:], wrb[:, slot], ACT.Copy, scale=sign[:, 0:1]).then_inc(wh_ready, 1)

            act.wait_ge(wd_in[0], 16 * DLOADS)
            for n in range(PAIRS):
                if n == 2:
                    w_high(1, 1)
                silu(n, n)

            def two_silus(j, last):
                for m in range(2 * PAIRS):
                    if m == 2:
                        w_high(0, j + 2)
                    if m == PAIRS + 2 and not last:
                        w_high(1, j + 2)
                    if m == 0:
                        act.wait_ge(wd_in[1], 16 * DLOADS * (j + 1))
                    if m == PAIRS:
                        act.wait_ge(wd_in[0], 16 * DLOADS * (j + 2))
                    silu(2 * PAIRS * j + PAIRS + m, PAIRS + m)

            with act.Fori(0, NE // 2 - 1) as j:
                two_silus(j, False)
            two_silus(NE // 2 - 1, True)

        @block.tensor
        def _(pe):
            pe.wait_ge(s_const, 1)
            pe.wait_ge(s_xpat, 4)

            def patch_turn(g):
                if g >= 2:
                    pe.wait_ge(s_patT, g - 1)
                for k in range(KC):
                    src = xpat[:, k // 2, g, (k % 2) * P:(k % 2) * P + P]
                    last = pe.transpose(bank[g % 2][:, k * BG:(k + 1) * BG], src, ident[0:BG, 0:BG])
                last.then_inc(s_patps, 1)

            def patch_embed(g):
                o = bank[2 + g % 2]
                pe.wait_ge(s_patT, g + 1)
                if g >= 2:
                    pe.wait_ge(s_embsb, g - 1)
                for k in range(KC):
                    pe.matmul(o[0:BG, 0:E], patT[:, g % 2, k, :], wtok[:, k, :], start=(k == 0), stop=False)
                pe.matmul(o[0:BG, 0:E], ones[0:1, 0:BG], brow[:], start=False, stop=True)
                pe.matmul(o[0:BG, 0:P], posx[:, 0, g].rearrange("p b h -> p (b h)"), ident[:], start=False, stop=True,
                          skip_group_check=True)
                pe.matmul(o[0:BG, P:E], posx[0:64, 1, g].rearrange("p b h -> p (b h)"), ident[0:64, 0:64], start=False,
                          stop=True, skip_group_check=True).then_inc(s_embps, 1)

            patch_turn(0)
            pe.wait_ge(s_tokw, 32)
            pe.wait_ge(s_posx, 2)
            for g in range(G):
                if g + 1 < G:
                    patch_turn(g + 1)
                patch_embed(g)
            pe.wait_ge(s_small, 32)
            pe.transpose(bank[6][:, 0:NH], wqk[:, 0:P], ident[0:NH, 0:NH])
            pe.transpose(bank[6][0:64, NH:2 * NH], wqk[:, P:E], ident[0:NH, 0:NH]).then_inc(s_wqps, 1)
            pe.wait_ge(s_wo, 16 * 8)
            for c in range(NCH):
                if c >= 2:
                    pe.wait_ge(s_woT, c - 1)
                for part, rows in ((0, P), (1, 64)):
                    last = pe.transpose(bank[4 + c % 2][:, part * P:part * P + rows], wo_raw[0:rows, part, c, :],
                                        ident[0:rows, 0:rows])
                last.then_inc(s_wops, 1)

            def turn_in(b, bt, i):
                pe.wait_ge(z_ready, i + 1)
                if not isinstance(bt, int) or bt:
                    pe.wait_ge(xnT_ready, 2 * bt)
                pe.transpose(bank[7][:, 0:P], z[:, b, 0, 0:P], ident[:])
                pe.transpose(bank[7][:, P:SP], z[0:64, b, 1, 0:P], ident[0:64, 0:64])
                pe.transpose(bank[7][0:64, SP:SP + P], z[:, b, 0, P:E], ident[:])
                pe.transpose(bank[7][0:64, SP + P:2 * SP], z[0:64, b, 1, P:E], ident[0:64, 0:64]).then_inc(xnT_psum, 1)

            def scores(u, U):
                g, b = u % UPB, u // UPB
                h = GRP * g
                main = bank[0][:, :].rearrange("p (j t) -> p j t", j=GRP)
                if not isinstance(U, int) or U:
                    pe.wait_ge(exp_main, U)
                pe.matmul(main, xa[:, b, 0:P], qa[:, b, h:h + GRP, 0:P], start=True, stop=False)
                pe.matmul(main, xb[:, b, 0:P], qb[:, b, h:h + GRP, 0:P], start=False, stop=False)
                pe.matmul(main, identb[:], cmask[:].rearrange("p (a t) -> p a t", a=1).broadcast_to([P, GRP, P]),
                          start=False, stop=True).then_inc(scores_main, 1)
                if not isinstance(U, int) or U:
                    pe.wait_ge(exp_tail, U)
                for half in range(2):
                    o = bank[1][64 * half:64 * half + 64, 0:2 * S].rearrange("p (j t) -> p j t", j=2)
                    hh = h + 2 * half
                    pe.matmul(o, xa[:, b, P:SP], qa[:, b, hh:hh + 2, 0:S], start=True, stop=False)
                    pe.matmul(o, xb[:, b, P:SP], qb[:, b, hh:hh + 2, 0:S], start=False, stop=True)
                o = bank[1][:, 0:2 * S].rearrange("p (j t) -> p j t", j=2)[:, :, P:S]
                pe.matmul(o, identb[:], tmask[:, 0:TAIL].rearrange("p (a t) -> p a t", a=1).broadcast_to([P, 2, TAIL]),
                          start=False, stop=True, skip_group_check=True).then_inc(scores_tail, 1)

            def queries_in(bt, g):
                pe.wait_ge(qa_ready, UPB * bt + g + 1)
                pe.wait_ge(qb_ready, UPB * bt + g + 1)

            def turn_probs(u, U):
                sl = u % 2
                pe.wait_ge(prob_main, U + 1)
                for j in range(GRP):
                    last = pe.transpose(bank[2][:, j * P:(j + 1) * P], pm[:, sl, j, :], ident[:])
                last.then_inc(turned_main, 1)
                pe.wait_ge(prob_tail, U + 1)
                for k in range(2):
                    pe.transpose(bank[3][:, k * P:(k + 1) * P], pt[:, sl, k, 0:P], ident[:])
                    last = pe.transpose(bank[3][0:TAIL, (2 + k) * P:(3 + k) * P], pt[:, sl, k, P:S], ident[:])
                last.then_inc(turned_tail, 1)

            def mix(u, U, i):
                b = u // UPB
                tl = slice(P, S) if b == 0 else slice(0, TAIL)
                pe.wait_ge(probT_main, U + 1)
                pe.wait_ge(probT_tail, 2 * U + 2)
                if u == 0:
                    pe.wait_ge(proj_read, 3 * i + 1)
                if u % UPB == 0:
                    pe.wait_ge(xn_ready, 2 * i + b + 1)
                for q in range(2):
                    if u >= 1:
                        if q == 0:
                            pe.wait_ge(ot_act, U)
                        else:
                            pe.wait_ge(ot_dve, 2 * U)
                    o = bank[4 + q][:, 0:2 * S].rearrange("p (j t) -> p j t", j=2)
                    pe.matmul(o, xn[:, b, 0, 0:P], pT0[:, 2 * q:2 * q + 2, :], start=True, stop=True)
                    pe.matmul(o[:, :, tl], xn[0:TAIL, b, 1, 0:P], pT1[0:TAIL, 2 * q:2 * q + 2, :], start=False,
                              stop=True, skip_group_check=True).then_inc(pv_done, 1)
                halves = [bank[6][64 * jj:64 * jj + 64, 0:2 * S].rearrange("p (q t) -> p q t", q=2) for jj in range(2)]
                for jj, o in enumerate(halves):
                    pe.matmul(o, xn[:, b, 0, P:E], pT0[:, jj:GRP:2, :], start=True, stop=True)
                for jj, o in enumerate(halves):
                    last = pe.matmul(o[:, :, tl], xn[0:TAIL, b, 1, P:E], pT1[0:TAIL, jj:GRP:2, :], start=False,
                                     stop=True, skip_group_check=True)
                last.then_inc(pv_done, 1)

            def project(U):
                pe.wait_ge(ot_act, U + UPP)
                pe.wait_ge(ot_dve, 2 * (U + UPP))
                for t, (at, n) in enumerate(COLS):
                    o = bank[4][:, t * E:(t + 1) * E] if t < 2 else bank[5][0:TT, 0:E]
                    for c in range(NCH):
                        last = pe.matmul(o, oT[:, c, at:at + n], woT[:, c, :], start=(c == 0), stop=(c == NCH - 1))
                    if t >= 1:
                        last.then_inc(wo_done, 1)

            turn_in(0, 0, 0)
            turn_in(1, 1, 0)
            queries_in(0, 0)
            scores(0, 0)

            def mean():
                pe.wait_ge(wsum_ready, 1)
                pe.wait_ge(xnT_ready, 2 * B)
                parts = [wacc[:, r, :] for r in (0, 1, 2, WR - 1)] + [wrest[:]]
                for o, at, m in ((bank[7][:, 0:1], 0, P), (bank[7][0:64, 1:2], P, 64), (bank[7][64:P, 1:2], P, 64)):
                    for k, part in enumerate(parts):
                        last = pe.matmul(o, part[:, at:at + m], vmean[:], start=(k == 0), stop=(k == len(parts) - 1))
                last.then_inc(avg_psum, 1)

            def mean_projected():
                pe.wait_ge(avg_ready, 1)
                for c in range(NCH):
                    m = 0 if c % 3 < 2 else 1
                    last = pe.matmul(bank[7][:, E:2 * E], avg[:, m:m + 1].broadcast_to([P, P]), woT[:, c, :],
                                     start=(c == 0), stop=(c == NCH - 1))
                last.then_inc(c_psum, 1)

            def pair(i, last):
                U = UPP * i
                for u in range(UPP - 1):
                    queries_in(2 * i + (u + 1) // UPB, (u + 1) % UPB)
                    scores(u + 1, U + u + 1)
                    if u >= 1:
                        mix(u - 1, U + u - 1, i)
                    if u == 3 and not last:
                        turn_in(0, 2 * i + 2, i + 1)
                    if u == 3 and last:
                        mean()
                    if u == 4 and last:
                        mean_projected()
                    turn_probs(u, U + u)
                mix(4, U + 4, i)
                if not last:
                    turn_in(1, 2 * i + 3, i + 1)
                turn_probs(5, U + 5)
                if not last:
                    queries_in(2 * i + 2, 0)
                    scores(0, U + 6)
                mix(5, U + 5, i)
                project(U)

            pe.wait_ge(s_woT, NCH - 1)
            with pe.Fori(0, PAIRS - 1) as i:
                pair(i, False)
            pair(PAIRS - 1, True)

            def turn_ffn(i):
                pe.wait_ge(xf_ready, i + 1)
                if i >= 2:
                    pe.wait_ge(xfT_act, 2 * (i - 1))
                    pe.wait_ge(xfT_dve, 2 * (i - 1))
                for t, (at, n) in enumerate(COLS):
                    pe.transpose(bank[i % 2][:, at:at + n], xf[0:n, i, t, 0:P], ident[0:n, 0:n])
                    last = pe.transpose(bank[2 + i % 2][:, at:at + n], xf[0:n, i, t, P:2 * P], ident[0:n, 0:n])
                last.then_inc(xfT_psum, 1)

            def gate(i):
                pe.wait_ge(xfT_act, 2 * i + 1)
                pe.wait_ge(xfT_dve, 2 * i + 1)
                if i >= 1:
                    pe.wait_ge(gate_ready, i)
                for t, (at, n) in enumerate(COLS):
                    o = bank[6][0:n, t * NE:(t + 1) * NE]
                    pe.matmul(o, fa[:, i, at:at + n], gwa[:], start=True, stop=False)
                    last = pe.matmul(o, fb[0:64, i, at:at + n], gwb[:], start=False, stop=True)
                last.then_inc(gate_psum, 1)

            pe.wait_ge(s_small2, 96)
            turn_ffn(0)
            for i in range(PAIRS):
                if i + 1 < PAIRS:
                    turn_ffn(i + 1)
                gate(i)

            def products(dst, c, i, k):
                o = dst[:, 0:CW]
                pe.matmul(o, wah[:, k, c], xah[:, i], start=True, stop=False)
                pe.matmul(o, wah[:, k, c], xal[:, i], start=False, stop=False)
                pe.matmul(o, wal[:, k, c], xah[:, i], start=False, stop=False)
                pe.matmul(o, wbs[:, k, c], xbh[:, i], start=False, stop=False)
                return pe.matmul(o, wbs[:, k, c], xbl[:, i], start=False, stop=True)

            def expert_in(k, loads, slot):
                pe.wait_ge(w_in[slot], 16 * WLOADS * loads)
                pe.wait_ge(wd_in[slot], 16 * DLOADS * loads)
                pe.wait_ge(wh_ready, 2 * k + 2)
                pe.wait_ge(wal_ready, k + 1)
                pe.wait_ge(wbs_ready, k + 1)

            def up_gate(n, st_, k):
                sl = n % 2
                if n >= 2:
                    pe.wait_ge(silu_ready, st_ - 1)
                products(bank[sl], 0, n % PAIRS, k).then_inc(up_ready, 1)
                if n >= 2:
                    pe.wait_ge(hid_ready, st_ - 1)
                products(bank[2 + sl], 1, n % PAIRS, k).then_inc(gt_ready, 1)

            def down(n, st_, k):
                sl = n % 2
                pe.wait_ge(hid_ready, st_ + 1)
                for t, (at, rows) in enumerate(COLS):
                    if n >= 2 and t != 1:
                        pe.wait_ge(acc_done, 2 * (st_ - 1) - (1 if t == 0 else 0))
                    o = bank[4 + sl][:, t * E:(t + 1) * E] if t < 2 else bank[6 + sl][0:TT, 0:E]
                    last = pe.matmul(o, hidT[:, sl, at:at + rows], wdn[:, k, :], start=True, stop=True)
                    if t >= 1:
                        last.then_inc(down_done, 1)

            def expert_steps(n0, st0, j, first, last):
                count = PAIRS if first else 2 * PAIRS
                for m in range(count):
                    n, s_ = n0 + m, st0 + m
                    if not (last and m == count - 1):
                        if (n + 1) % PAIRS == 0:
                            k = ((n + 1) // PAIRS) % 2
                            if first:
                                expert_in(1, 1, 1)
                            elif k == 0:
                                expert_in(2 * j + 2, j + 2, 0)
                            else:
                                expert_in(2 * j + 3, j + 2, 1)
                        up_gate(n + 1, s_ + 1, ((n + 1) // PAIRS) % 2)
                    down(n, s_, (n // PAIRS) % 2)

            pe.wait_ge(gate_ready, PAIRS)
            pe.wait_ge(x_low, 2 * PAIRS)
            expert_in(0, 1, 0)
            up_gate(0, 0, 0)
            expert_steps(0, 0, None, True, False)
            pe.wait_ge(wts_ready, 1)
            pe.wait_ge(acc_done, 2 * PAIRS)
            for t in range(NT):
                last = pe.transpose(bank[4 + t // 4][0:NW, (t % 4) * P:(t % 4 + 1) * P], wts[:, t, :], ident[:])
                if t % 4 == 3:
                    last.then_inc(wT_psum, 1)
            for r in range(NT // 2):
                if r >= 4:
                    pe.wait_ge(bias_added, r - 3)
                else:
                    pe.wait_ge(wT_ready, max(r, 1))
                for t in (2 * r, 2 * r + 1):
                    if t % 4 == 0 and t // 4 + 1 > r:
                        pe.wait_ge(wT_ready, t // 4 + 1)
                    last = pe.matmul(bias_bank[r][:, (t % 2) * E:(t % 2 + 1) * E], wT[:, t, :], bdx[:], start=True,
                                     stop=True)
                last.then_inc(bias_psum, 1)
            pe.wait_ge(bias_added, NT // 2)
            with pe.Fori(0, NE // 2 - 1) as j:
                expert_steps(PAIRS, 2 * PAIRS * j + PAIRS, j, False, False)
            expert_steps(PAIRS, 2 * PAIRS * (NE // 2 - 1) + PAIRS, NE // 2 - 1, False, True)

        @block.vector
        def _(dve):
            own = Tally(dve_own)

            def link(ins):
                own.mark(ins)
                dve.wait_ge(dve_own, own.at)

            dve.memset(hin[:], 0.0).then_inc(s_zero, 1)
            dve.memset(htail[:], 0.0).then_inc(s_zero, 1)
            own.mark(dve.memset(lg[:], 0.0))
            own.mark(dve.memset(scan[:], 0.0))
            own.mark(dve.memset(mv[:], 1.0))
            dve.wait_ge(s_x, 16 * B)
            dve.tensor_copy(xpat[:, 0].rearrange("t g (r w) -> t g r w", w=PS),
                            ximg[:, 0].rearrange("t (r g w) -> t g r w", g=G, w=PS)).then_inc(s_xpat, 1)
            dve.tensor_copy(xpat[:, 2].rearrange("t g (r w) -> t g r w", w=PS)[:, :, 0:PS // 2],
                            ximg[:, 2].rearrange("t (r g w) -> t g r w", g=G, w=PS)[:, :, 0:PS // 2]).then_inc(s_xpat, 1)
            dve.wait_ge(s_pos, 32)
            for part, rows in ((0, P), (1, 64)):
                grid = posr[0:rows, part, :].rearrange("p (h a w c) -> p h a w c", h=G, a=2, c=2)
                for g in range(G):
                    src = grid[:, :, 0, g, 0].rearrange("p (a h) -> p a h", a=1).broadcast_to([rows, B, G])
                    last = dve.tensor_copy(posx[0:rows, part, g], src)
                last.then_inc(s_posx, 1)
            dve.wait_ge(s_const, 1)
            own.mark(dve.reciprocal(nreg[:], nregf[:]))
            dve.wait_ge(dve_own, own.at)
            own.mark(dve.tensor_scalar(nnreg[:], nreg[:], -1.0, None, ALU.mult))
            for g in range(G):
                dve.wait_ge(s_embps, g + 1)
                dve.tensor_copy(emb[:, g, :], bank[2 + g % 2][0:BG, 0:E]).then_inc(s_embsb, 1)
            dve.wait_ge(s_wqps, 1)
            link(dve.tensor_copy(w2a[:], bank[6][:, 0:NH]))
            link(dve.tensor_copy(w2b[:], bank[6][0:64, NH:2 * NH]))
            dve.scalar_tensor_tensor(out=w2a[:], in0=w2a[:], scalar=SCALE, in1=w2a[:], op0=ALU.mult,
                                     op1=ALU.mult).then_inc(s_w2, 1)
            dve.scalar_tensor_tensor(out=w2b[:], in0=w2b[:], scalar=SCALE, in1=w2b[:], op0=ALU.mult,
                                     op1=ALU.mult).then_inc(s_w2, 1)
            dve.wait_ge(s_w2, 2)
            dve.wait_ge(s_text, 16 * 4 * B)
            dve.wait_ge(s_emb, 16 * B)
            dve.wait_ge(s_small, 32)

            def stats_begin(tiles):
                n = len(tiles)
                for t, src in enumerate(tiles):
                    own.mark(dve.bn_stats(st[0:src.shape[0], t, :], src))
                dve.wait_ge(dve_own, own.at)
                dve.memset(pause[:], 0.0)
                for t, src in enumerate(tiles):
                    own.mark(dve.bn_aggr(mv[0:src.shape[0], t, :], st[0:src.shape[0], t, :]))
                dve.wait_ge(dve_own, own.at)
                dve.tensor_scalar(ve[:, 0:n], mv[:, 0:n, 1], EPS, None, ALU.add).then_inc(var_ready, 1)

            def stats(tiles, count):
                stats_begin(tiles)
                dve.wait_ge(rstd_ready, count)

            def norm_begin(i, h):
                stats_begin([h[:, 0, 0, :], h[:, 0, 1, :], h[:, 1, 0, :], h[:, 1, 1, :]])

            def norm_middle(i, h):
                dve.wait_ge(rstd_ready, 2 * i + 1)
                for t in range(4):
                    own.mark(dve.tensor_scalar(z[:, t // 2, t % 2, :], h[:, t // 2, t % 2, :], mv[:, t, 0:1], rs[:, t:t + 1],
                                               ALU.subtract, ALU.mult))
                dve.wait_ge(dve_own, own.at)
                stats_begin([z[:, t // 2, t % 2, :] for t in range(4)])

            def norm_end(i):
                dve.wait_ge(rstd_ready, 2 * i + 2)
                for t in range(4):
                    own.mark(dve.tensor_scalar(z[:, t // 2, t % 2, :], z[:, t // 2, t % 2, :], mv[:, t, 0:1], rs[:, t:t + 1],
                                               ALU.subtract, ALU.mult))
                dve.wait_ge(dve_own, own.at)
                dve.tensor_tensor(z[:], z[:], lnw[:].rearrange("p (a c e) -> p a c e", a=1, c=1)
                                  .broadcast_to([P, 2, 2, E]), ALU.mult).then_inc(z_ready, 1)

            def keep(b, i):
                dve.wait_ge(z_ready, i + 1)
                dve.tensor_copy(xn[:, b], z[:, b]).then_inc(xn_ready, 1)

            def queries(b, bt):
                dve.wait_ge(xnT_ready, 2 * bt + 2)
                for h in range(NH):
                    last = dve.tensor_scalar(qa[:, b, h, :], xa[:, b, :], w2a[:, h:h + 1], None, ALU.mult)
                    if h % GRP == GRP - 1:
                        last.then_inc(qa_ready, 1)

            def maxima(u, U):
                sl = u % 2
                dve.wait_ge(scores_main, U + 1)
                dve.tensor_reduce(nmax[:, sl, 0:GRP], bank[0][:, :].rearrange("p (j t) -> p j t", j=GRP), AX.X,
                                  ALU.max, negate=True).then_inc(max_main, 1)
                dve.wait_ge(scores_tail, U + 1)
                dve.tensor_reduce(nmax[:, sl, GRP:GRP + 2], bank[1][:, 0:2 * S].rearrange("p (j t) -> p j t", j=2),
                                  AX.X, ALU.max, negate=True).then_inc(max_tail, 1)

            def divide(u, U):
                sl = u % 2
                dve.wait_ge(exp_main, U + 1)
                dve.wait_ge(exp_tail, U + 1)
                link(dve.reciprocal(rsum[:], psums[:, sl, :]))
                dve.tensor_tensor(pm[:, sl], pm[:, sl],
                                  rsum[:, 0:GRP].rearrange("p (j a) -> p j a", a=1).broadcast_to([P, GRP, P]),
                                  ALU.mult).then_inc(prob_main, 1)
                dve.tensor_tensor(pt[:, sl], pt[:, sl],
                                  rsum[:, GRP:GRP + 2].rearrange("p (j a) -> p j a", a=1).broadcast_to([P, 2, S]),
                                  ALU.mult).then_inc(prob_tail, 1)

            def tails_out(u, U):
                at = P if u < UPB else 0
                dve.wait_ge(turned_tail, U + 1)
                for half in range(2):
                    src = bank[3][:, 0:2 * P].rearrange("p (k a t) -> p k a t", k=2, a=2)[:, :, half, 0:TAIL]
                    last = dve.tensor_copy(pT0[:, 2 * half:2 * half + 2, at:at + TAIL], src)
                last.then_inc(probT_tail, 1)
                for half in range(2):
                    src = bank[3][0:TAIL, 2 * P:4 * P].rearrange("p (k a t) -> p k a t", k=2, a=2)[:, :, half, 0:TAIL]
                    last = dve.tensor_copy(pT1[0:TAIL, 2 * half:2 * half + 2, :], src)
                last.then_inc(probT_tail, 1)

            def mix_out(u, U):
                g, b = u % UPB, u // UPB
                dve.wait_ge(pv_done, 3 * U + 2)
                dve.tensor_copy(oT[:, 6 * g + 3:6 * g + 5, b * S:(b + 1) * S],
                                bank[5][:, 0:2 * S].rearrange("p (j t) -> p j t", j=2)).then_inc(ot_dve, 1)
                dve.wait_ge(pv_done, 3 * U + 3)
                dve.tensor_copy(oT[:, 6 * g + 2:6 * g + 6:3, b * S:(b + 1) * S],
                                bank[6][:, 0:2 * S].rearrange("p (q t) -> p q t", q=2)).then_inc(ot_dve, 1)

            def residual(i):
                for t in range(3):
                    dve.wait_ge(wo_done, 2 * i + (1 if t < 2 else 2))
                    n, m = COLS[t][1], t // 2
                    src = bank[4][:, t * E:(t + 1) * E] if t < 2 else bank[5][0:n, 0:E]
                    old = hin[:, 2 * i + t, 0, :] if t < 2 else htail[0:n, i, :]
                    dve.scalar_tensor_tensor(out=R[0:n, 3 * i + t, :], in0=src, scalar=nreg[0:n, m:m + 1], in1=old,
                                             op0=ALU.mult, op1=ALU.add).then_inc(proj_read, 1)

            def logits(i):
                dve.wait_ge(gate_psum, i + 1)
                dve.tensor_tensor(lg[:, 3 * i:3 * i + 2, :], bank[6][:, 0:2 * NE].rearrange("p (t e) -> p t e", t=2),
                                  gbb[:].rearrange("p (a e) -> p a e", a=1).broadcast_to([P, 2, NE]), ALU.add)
                dve.tensor_tensor(lg[0:TT, 3 * i + 2, :], bank[6][0:TT, 2 * NE:3 * NE], gbb[0:TT, :],
                                  ALU.add).then_inc(gate_ready, 1)

            def tiles_of(i):
                return [R[0:COLS[t][1], 3 * i + t, :] for t in range(3)]

            def correct(i):
                dve.wait_ge(proj_read, 3 * (PAIRS if i == PAIRS - 1 else PAIRS - 1) + 1)
                tiles = tiles_of(i)
                for t in range(3):
                    n, m = COLS[t][1], t // 2
                    own.mark(dve.scalar_tensor_tensor(out=tiles[t], in0=cbc[0:n, :], scalar=nnreg[0:n, m:m + 1],
                                                      in1=tiles[t], op0=ALU.mult, op1=ALU.add))
                dve.wait_ge(dve_own, own.at)
                stats_begin(tiles)

            def experts_in(i):
                dve.wait_ge(rstd_ready, 2 * PAIRS + i + 1)
                tiles = tiles_of(i)
                for t in range(3):
                    n = COLS[t][1]
                    dve.tensor_scalar(xf[0:n, i, t, 0:E], tiles[t], mv[0:n, t, 0:1], rs[0:n, t:t + 1],
                                      ALU.subtract, ALU.mult)
                    last = dve.tensor_scalar(xf[0:n, i, t, E:2 * P], tiles[t][:, P:E], mv[0:n, t, 0:1],
                                             rs[0:n, t:t + 1], ALU.subtract, ALU.mult)
                last.then_inc(xf_ready, 1)

            def features_out(i):
                dve.wait_ge(xfT_psum, i + 1)
                dve.tensor_copy(fb[:, i, :], bank[2 + i % 2][:, 0:CW]).then_inc(xfT_dve, 1)
                dve.tensor_copy(xbh[:, i, :], bank[2 + i % 2][:, 0:CW]).then_inc(xfT_dve, 1)

            norm_begin(0, hin[:, 0:2])
            norm_middle(0, hin[:, 0:2])
            norm_end(0)
            keep(0, 0)
            keep(1, 0)
            queries(0, 0)
            maxima(0, 0)
            queries(1, 1)

            def pair(i, last):
                U = UPP * i
                h = hin[:, 2 * (i + 1):2 * (i + 1) + 2] if isinstance(i, int) and not last else (
                    None if last else hin[:, bass.ds(2 * i + 2, 2)])
                for u in range(UPP - 1):
                    divide(u, U + u)
                    maxima(u + 1, U + u + 1)
                    if u >= 1:
                        mix_out(u - 1, U + u - 1)
                    tails_out(u, U + u)
                    if last:
                        if u == 3:
                            dve.wait_ge(avg_psum, 1)
                            dve.tensor_copy(avg[:], bank[7][:, 0:2]).then_inc(avg_ready, 1)
                        if u == 4:
                            dve.wait_ge(c_psum, 1)
                            link(dve.tensor_copy(cbc[:], bank[7][:, E:2 * E]))
                            correct(0)
                    if not last:
                        if u == 0:
                            norm_begin(i + 1, h)
                        if u == 1:
                            norm_middle(i + 1, h)
                        if u == 2:
                            norm_end(i + 1)
                        if u == 3:
                            keep(0, i + 1)
                            queries(0, 2 * i + 2)
                divide(5, U + 5)
                mix_out(4, U + 4)
                tails_out(5, U + 5)
                if not last:
                    maxima(0, U + 6)
                mix_out(5, U + 5)
                if not last:
                    keep(1, i + 1)
                else:
                    for k in range(1, PAIRS - 1):
                        experts_in(k - 1)
                        correct(k)
                    experts_in(PAIRS - 2)
                residual(i)
                if not last:
                    queries(1, 2 * i + 3)

            start = own.at
            per = UPP + 2 * (4 + 4 + 4)
            with dve.Fori(0, PAIRS - 1) as i:
                own.restart(per * i + start)
                pair(i, False)
                assert own.n == per
            own.restart(start + per * (PAIRS - 1))
            pair(PAIRS - 1, True)

            correct(PAIRS - 1)
            features_out(0)
            experts_in(PAIRS - 1)
            for i in range(1, PAIRS):
                features_out(i)
                logits(i - 1)
            logits(PAIRS - 1)

            def rows(v, n):
                return v.rearrange("p (t a) -> p t a", a=1).broadcast_to([P, NT, n])

            def w_stack(slot, k):
                dve.wait_ge(wh_ready, 2 * k + 2)
                dve.scalar_tensor_tensor(out=wbs[:, slot], in0=wrb[:, slot], scalar=upper[:, 0:1],
                                         in1=wbt[:].bitcast(F32), op0=ALU.mult, op1=ALU.add).then_inc(wbs_ready, 1)

            def softmax_start():
                dve.wait_ge(gate_ready, PAIRS)
                link(dve.tensor_reduce(mx[:], lg[:], AX.X, ALU.max))
                dve.tensor_tensor(lg[:], lg[:], rows(mx[:], NE), ALU.subtract).then_inc(nmx_ready, 1)

            def softmax_end():
                dve.wait_ge(gexp, 1)
                link(dve.tensor_reduce(mx[:], sc[:], AX.X, ALU.add))
                link(dve.reciprocal(mx[:], mx[:]))
                link(dve.tensor_tensor(sc[:], sc[:], rows(mx[:], NE), ALU.mult))
                link(dve.tensor_tensor(sel[:], sc[:],
                                       rbias[:].rearrange("p (a e) -> p a e", a=1).broadcast_to([P, NT, NE]), ALU.add))
                link(dve.tensor_reduce(gs[:], sel[:].rearrange("p t (g a) -> p t g a", a=2), AX.X, ALU.add))

            def first_four(v, n):
                a, c = above[:, :, 0:n], tied[:, :, 0:n]
                for t in range(NT):
                    own.mark(dve.max(out=top8[:, t, :], in_=v[:, t, 0:n]))
                dve.wait_ge(dve_own, own.at)
                fourth = top8[:, :, TOPK - 1:TOPK].broadcast_to([P, NT, n])
                own.mark(dve.tensor_tensor(scan[:, 0, :, PAD:PAD + n], v[:, :, 0:n], fourth, ALU.is_equal))
                own.mark(dve.tensor_tensor(c, v[:, :, 0:n], fourth, ALU.is_equal))
                link(dve.tensor_tensor(a, v[:, :, 0:n], fourth, ALU.is_gt))
                own.mark(dve.tensor_reduce(room[:], a, AX.X, ALU.add))
                side, step = 0, 1
                while step < n:
                    link(dve.tensor_tensor(scan[:, 1 - side, :, PAD:PAD + n], scan[:, side, :, PAD:PAD + n],
                                           scan[:, side, :, PAD - step:PAD - step + n], ALU.add))
                    side, step = 1 - side, 2 * step
                own.mark(dve.tensor_tensor(scan[:, side, :, PAD:PAD + n], scan[:, side, :, PAD:PAD + n], rows(room[:], n),
                                           ALU.add))
                dve.wait_ge(dve_own, own.at)
                link(dve.scalar_tensor_tensor(out=c, in0=scan[:, side, :, PAD:PAD + n], scalar=float(TOPK), in1=c,
                                              op0=ALU.is_le, op1=ALU.mult))
                link(dve.tensor_tensor(a, a, c, ALU.add))

            def choose_groups():
                first_four(gs, TG)
                pairs = above[:, :, 0:TG].rearrange("p t (g a) -> p t g a", a=1).broadcast_to([P, NT, TG, 2])
                link(dve.tensor_tensor(sel[:].rearrange("p t (g a) -> p t g a", a=2),
                                       sel[:].rearrange("p t (g a) -> p t g a", a=2), pairs, ALU.mult))
                link(dve.tensor_scalar(gs[:], above[:, :, 0:TG], -1.0, -NEVER, ALU.add, ALU.mult))
                pairs = gs[:].rearrange("p t (g a) -> p t g a", a=1).broadcast_to([P, NT, TG, 2])
                link(dve.tensor_tensor(sel[:].rearrange("p t (g a) -> p t g a", a=2),
                                       sel[:].rearrange("p t (g a) -> p t g a", a=2), pairs, ALU.add))

            def choose_experts():
                first_four(sel, NE)
                dve.scalar_tensor_tensor(out=wts[:, :, 0:NE], in0=above[:], scalar=ROUTE, in1=sc[:], op0=ALU.mult,
                                         op1=ALU.mult).then_inc(wts_ready, 1)

            def fuse(n, st_):
                sl = n % 2
                dve.wait_ge(gt_ready, st_ + 1)
                dve.wait_ge(silu_ready, st_ + 1)
                if n >= 2:
                    dve.wait_ge(down_done, 2 * (st_ - 1))
                dve.scalar_tensor_tensor(out=hidT[:, sl, 0:CW], in0=bank[2 + sl][:, 0:CW],
                                         scalar=bcol[:, (n // PAIRS) % 2, 1:2], in1=sil[:, sl, :], op0=ALU.add,
                                         op1=ALU.mult).then_inc(hid_ready, 1)

            def gather(n, st_, e):
                sl, i = n % 2, n % PAIRS
                for t in range(3):
                    rows_ = COLS[t][1]
                    if t != 1:
                        dve.wait_ge(down_done, 2 * st_ + (1 if t < 2 else 2))
                    src = bank[4 + sl][:, t * E:(t + 1) * E] if t < 2 else bank[6 + sl][0:TT, 0:E]
                    if t == 0:
                        dve.wait_ge(acc_done, 2 * (st_ - PAIRS + 1)) if n >= PAIRS else None
                    old = R[0:rows_, 3 * i + t, :]
                    last = dve.scalar_tensor_tensor(out=old, in0=src,
                                                    scalar=wts[0:rows_, 3 * i + t, bass.ds(e, 1)], in1=old,
                                                    op0=ALU.mult, op1=ALU.add)
                    if t >= 1:
                        last.then_inc(acc_done, 1)

            softmax_start()
            w_stack(0, 0)
            softmax_end()
            dve.wait_ge(wd_in[0], 16 * DLOADS)
            fuse(0, 0)
            choose_groups()
            for n in range(PAIRS):
                if n == 1:
                    w_stack(1, 1)
                if n == 2:
                    choose_experts()
                if n == PAIRS - 1:
                    dve.wait_ge(wd_in[1], 16 * DLOADS)
                fuse(n + 1, n + 1)
                gather(n, n, NE)
            dve.wait_ge(wts_ready, 1)
            for q in range(NT // 4):
                dve.wait_ge(wT_psum, q + 1)
                dve.tensor_copy(wT[:, 4 * q:4 * q + 4, :],
                                bank[4 + q][0:NW, :].rearrange("p (t r) -> p t r", t=4)).then_inc(wT_ready, 1)
            dve.wait_ge(acc_done, 2 * PAIRS)
            for r in range(NT // 2):
                dve.wait_ge(bias_psum, r + 1)
                dve.tensor_tensor(R[:, 2 * r:2 * r + 2, :], bias_bank[r][:, 0:2 * E].rearrange("p (t e) -> p t e", t=2),
                                  R[:, 2 * r:2 * r + 2, :], ALU.add).then_inc(bias_added, 1)
            dve.wait_ge(bias_added, NT // 2)

            def two_experts(j, last):
                for m in range(2 * PAIRS):
                    n, s_ = PAIRS + m, 2 * PAIRS * j + PAIRS + m
                    if m == 1:
                        w_stack(0, 2 * j + 2)
                    if m == PAIRS + 1 and not last:
                        w_stack(1, 2 * j + 3)
                    if m == PAIRS - 1:
                        dve.wait_ge(wd_in[0], 16 * DLOADS * j + 32 * DLOADS)
                    if m == 2 * PAIRS - 1 and not last:
                        dve.wait_ge(wd_in[1], 16 * DLOADS * j + 32 * DLOADS)
                    if not (last and m == 2 * PAIRS - 1):
                        fuse(n + 1, s_ + 1)
                    gather(n, s_, 2 * j + m // PAIRS)

            with dve.Fori(0, NE // 2 - 1) as j:
                two_experts(j, False)
            two_experts(NE // 2 - 1, True)


_INS = ['x', 'txt', 'L0_tok_W', 'L0_tok_b', 'L0_tok_positions', 'L0_tok_cls_embedding', 'L0_attn_ln_w', 'L0_attn_W_qk',
        'L0_attn_W_o', 'L0_attn_wte', 'L0_ffn_gate_w', 'L0_ffn_gate_b', 'L0_ffn_bias', 'L0_ffn_Wu', 'L0_ffn_bu',
        'L0_ffn_Wg', 'L0_ffn_bg', 'L0_ffn_Wd', 'L0_ffn_bd', 'L0_ffn_sWu', 'L0_ffn_sbu', 'L0_ffn_sWg', 'L0_ffn_sbg',
        'L0_ffn_sWd', 'L0_ffn_sbd']
_OUTS = [((8, 178, 192), 'float32')]


def kernel(**inputs):
    import numpy as _np
    import concourse.bacc as _bacc
    from concourse import mybir as _mybir
    from concourse.bass_utils import run_bass_kernel_spmd as _run

    nc = _bacc.Bacc("TRN2", target_bir_lowering=False, num_devices=1)
    arrays, args = {}, []
    for name in _INS:
        a = _np.ascontiguousarray(inputs[name])
        arrays[f"in_{name}_dram"] = a
        args.append(nc.dram_tensor(f"in_{name}_dram", a.shape, _mybir.dt.from_np(a.dtype), kind="ExternalInput").ap())
    for i, (shape, dtype) in enumerate(_OUTS):
        dt = _mybir.dt.from_np(_np.dtype(dtype))
        args.append(nc.dram_tensor(f"out_{i}_dram", shape, dt, kind="ExternalOutput").ap())
    early_fusion_kernel(nc, *args)
    r = _run(nc, [arrays], core_ids=[0])
    return r.results[0]["out_0_dram"]
```

```python
from contextlib import ExitStack

import concourse.bass as bass
from concourse import mybir

F32 = mybir.dt.float32
F32R = mybir.dt.float32r
BF16 = mybir.dt.bfloat16
ALU = mybir.AluOpType
ACT = mybir.ActivationFunctionType
AX = mybir.AxisListType

P = 128
EPS = 1e-5
MASKED = -1e30
NEVER = -3e38


class Tally:

    def __init__(self, sem):
        self.sem, self.base, self.n = sem, 0, 0

    @property
    def at(self):
        return self.base + self.n

    def mark(self, ins):
        ins.then_inc(self.sem, 1)
        self.n += 1

    def restart(self, base):
        self.base, self.n = base, 0


def early_fusion_kernel(nc, x, txt, tok_W, tok_b, tok_pos, tok_cls, ln_w, W_qk, W_o, wte,
                        gate_w, gate_b, bias, Wu, bu, Wg, bg, Wd, bd, sWu, sbu, sWg, sbg, sWd, sbd, out):
    B, C, HI, WI = x.shape
    NTXT, E = txt.shape[1:]
    PS = 16
    G = HI // PS
    NIMG = 1 + G * G
    S = NIMG + NTXT
    TAIL = S - P
    NH = W_qk.shape[0]
    EB = E - P
    V = wte.shape[0]
    NE = Wu.shape[0]
    HID = Wu.shape[2]
    PAIRS = B // 2
    GRP = 4
    UPB = NH // GRP
    UPP = 2 * UPB
    SP = P + 64
    CW = 2 * S
    TT = 2 * TAIL
    COLS = [(0, P), (CW - P, P), (P, TT)]
    NCH = NH * E // P
    SCALE = float(E) ** -0.5
    KC = C * PS * PS // P
    BG = B * G
    WROWS = V // P
    WR = 49
    WREST = V - P * WROWS
    assert TAIL <= 64 and EB == 64 and HID == P and WROWS == WR * B and NH == GRP * UPB
    assert PAIRS == 4
    NT = 3 * PAIRS
    TG = NE // 2
    TOPK = 4
    ROUTE = 2.5
    NW = NE + 1

    with ExitStack() as ctx:
        def sb(name, shape, dt=F32):
            return ctx.enter_context(nc.sbuf_tensor(name, shape, dt))

        def sem(name):
            return ctx.enter_context(nc.semaphore(name))

        bank = [ctx.enter_context(nc.psum_tensor(f"bank{n}", [P, 512], F32)) for n in range(8)]

        ident = sb("ident", [P, P])
        identb = sb("identb", [P, P], BF16)
        cmask = sb("cmask", [P, P], BF16)
        tmask = sb("tmask", [P, 64], BF16)
        mhalf = sb("mhalf", [P, 4])
        vmean = sb("vmean", [P, 1])
        nregi = sb("nregi", [P, 2], mybir.dt.int32)
        nregf = sb("nregf", [P, 2])
        firsthalf = sb("firsthalf", [P, 1])
        nreg = sb("nreg", [P, 2])
        nnreg = sb("nnreg", [P, 2])
        upper = sb("upper", [P, 1])
        sign = sb("sign", [P, 1])
        wtok = sb("wtok", [P, KC, E])
        tokb = sb("tokb", [P, 2])
        posr = sb("posr", [P, 2, 4 * G * G])
        posx = sb("posx", [P, 2, G, B, G])
        area_a = sb("area_a", [P, 2 * NH * SP])
        area_b = sb("area_b", [P, C * PS * WI])

        def part_of(area, at, *shape):
            n = 1
            for d in shape[1:]:
                n *= d
            names = "abcd"[:len(shape) - 1]
            dims = {c: d for c, d in zip(names, shape[1:])}
            return area[0:shape[0], at:at + n].rearrange(f"p ({' '.join(names)}) -> p {' '.join(names)}", **dims)

        wo_raw = part_of(area_a, 0, P, 2, NCH, P)
        xpat = part_of(area_b, 0, BG, C, G, PS * PS)
        woT = sb("woT", [P, NCH, E])
        wqk = sb("wqk", [NH, E])
        w2a = sb("w2a", [P, NH])
        w2b = sb("w2b", [64, NH])
        lnw = sb("lnw", [P, E])
        gwa = sb("gwa", [P, NE])
        gwb = sb("gwb", [64, NE])
        gbb = sb("gbb", [P, NE])
        rbias = sb("rbias", [P, NE])
        bdx = sb("bdx", [NW, E])
        patT = sb("patT", [P, 2, KC, BG])
        emb = sb("emb", [BG, G, E])
        hin = sb("hin", [P, B, 2, E])
        htail = sb("htail", [P, PAIRS, E])
        R = sb("R", [P, NT, E])
        z = sb("z", [P, 2, 2, E])
        st = sb("st", [P, 4, 6])
        mv = sb("mv", [P, 4, 2])
        pause = sb("pause", [P, 1])
        ve = sb("ve", [P, 4])
        rs = sb("rs", [P, 4])
        xn = sb("xn", [P, 2, 2, E])
        xa = sb("xa", [P, 2, SP])
        xb = sb("xb", [64, 2, SP])
        qa = part_of(area_a, 0, P, 2, NH, SP)
        qb = part_of(area_b, 0, 64, 2, NH, SP)
        nmax = sb("nmax", [P, 2, 6])
        psums = sb("psums", [P, 2, 6])
        rsum = sb("rsum", [P, 6])
        pm = sb("pm", [P, 2, GRP, P])
        pt = sb("pt", [P, 2, 2, S])
        pT0 = sb("pT0", [P, GRP, S])
        pT1 = sb("pT1", [64, GRP, TAIL])
        oT = sb("oT", [P, NCH, CW])
        ximg = oT[0:BG].rearrange("p c t -> p (c t)")[:, 0:C * PS * WI].rearrange("p (c w) -> p c w", c=C)
        wrest = sb("wrest", [P, E])
        avg = sb("avg", [P, 2])
        cbc = sb("cbc", [P, E])
        fa = part_of(area_a, 0, P, PAIRS, CW)
        fb = part_of(area_a, PAIRS * CW, P, PAIRS, CW)
        xf = hin[:].rearrange("p b c e -> p (b c e)").rearrange("p (i t e) -> p i t e", i=PAIRS, t=3)
        lg = sb("lg", [P, NT, NE])
        mx = sb("mx", [P, NT])
        sc = sb("sc", [P, NT, NE])
        sel = sb("sel", [P, NT, NE])
        gs = sb("gs", [P, NT, TG])
        top8 = sb("top8", [P, NT, 8])
        above = sb("above", [P, NT, NE])
        tied = sb("tied", [P, NT, NE])
        room = sb("room", [P, NT])
        PAD = 8
        scan = sb("scan", [P, 2, NT, PAD + NE])
        wts = sb("wts", [P, NT, NW])
        wT = part_of(area_b, 0, NW, NT, P)
        wT_bank = [bank[n] for n in (0, 2, 1)]
        bias_bank = [bank[n] for n in (3, 0, 2, 1, 4, 6)]
        wra = sb("wra", [P, 2, 2, HID])
        wrb = sb("wrb", [P, 2, 2, HID])
        wdn = sb("wdn", [P, 2, E])
        bcol = sb("bcol", [P, 2, 2])
        sil = part_of(area_b, NT * P, P, 2, CW)
        hidT = sb("hidT", [P, 2, CW])
        with nc.sbuf_tensor("wacc", [P, WR, E], F32) as wacc:
            pass
        xah = sb("xah", [P, PAIRS, CW], F32R)
        xal = sb("xal", [P, PAIRS, CW], F32R)
        xbh = sb("xbh", [P, PAIRS, CW], F32R)
        xbl = sb("xbl", [P, PAIRS, CW], F32R)
        wah = sb("wah", [P, 2, 2, HID], F32R)
        wal = sb("wal", [P, 2, 2, HID], F32R)
        wbs = sb("wbs", [P, 2, 2, HID], F32R)
        wbt = sb("wbt", [P, 2, HID], F32R)

        s_const = sem("s_const")
        s_x = sem("s_x")
        s_tokw = sem("s_tokw")
        s_xpat = sem("s_xpat")
        s_pos = sem("s_pos")
        s_wo = sem("s_wo")
        s_small = sem("s_small")
        s_small2 = sem("s_small2")
        s_text = sem("s_text")
        s_emb = [sem("s_emb_first"), sem("s_emb_rest")]
        s_zero = sem("s_zero")
        s_posx = sem("s_posx")
        s_posps = sem("s_posps")
        s_patps = sem("s_patps")
        s_patT = sem("s_patT")
        s_embps = sem("s_embps")
        s_embsb = sem("s_embsb")
        s_wops = sem("s_wops")
        s_woT = sem("s_woT")
        s_wqps = sem("s_wqps")
        s_w2 = sem("s_w2")
        var_ready = sem("var_ready")
        rstd_ready = sem("rstd_ready")
        z_ready = sem("z_ready")
        xn_ready = sem("xn_ready")
        xnT_psum = sem("xnT_psum")
        xnT_ready = sem("xnT_ready")
        qa_ready = sem("qa_ready")
        qb_ready = sem("qb_ready")
        scores_main = sem("scores_main")
        scores_tail = sem("scores_tail")
        max_main = sem("max_main")
        max_tail = sem("max_tail")
        exp_main = sem("exp_main")
        exp_tail = sem("exp_tail")
        prob_main = sem("prob_main")
        prob_tail = sem("prob_tail")
        turned_main = sem("turned_main")
        turned_tail = sem("turned_tail")
        probT_main = sem("probT_main")
        probT_tail = sem("probT_tail")
        pv_done = sem("pv_done")
        ot_act = sem("ot_act")
        ot_dve = sem("ot_dve")
        wo_done = sem("wo_done")
        proj_read = sem("proj_read")
        wte_in = sem("wte_in")
        wte_rest = sem("wte_rest")
        wsum_ready = sem("wsum_ready")
        avg_psum = sem("avg_psum")
        avg_ready = sem("avg_ready")
        c_psum = sem("c_psum")
        xf_ready = sem("xf_ready")
        xfT_psum = sem("xfT_psum")
        xfT_act = sem("xfT_act")
        xfT_dve = sem("xfT_dve")
        x_low = sem("x_low")
        gate_psum = sem("gate_psum")
        gate_ready = sem("gate_ready")
        nmx_ready = sem("nmx_ready")
        gexp = sem("gexp")
        wts_ready = sem("wts_ready")
        wT_psum = sem("wT_psum")
        wT_ready = sem("wT_ready")
        bias_psum = sem("bias_psum")
        bias_added = sem("bias_added")
        w_in = [sem("w_in0"), sem("w_in1")]
        wd_in = [sem("wd_in0"), sem("wd_in1")]
        wh_ready = sem("wh_ready")
        wal_ready = sem("wal_ready")
        wbs_ready = sem("wbs_ready")
        up_ready = sem("up_ready")
        gt_ready = sem("gt_ready")
        silu_ready = sem("silu_ready")
        hid_ready = sem("hid_ready")
        down_done = sem("down_done")
        acc_done = sem("acc_done")
        out_done = sem("out_done")
        dve_own = sem("dve_own")
        pool_own = sem("pool_own")

        WLOADS = 6
        DLOADS = 3
        block = ctx.enter_context(nc.Block())

        @block.sync
        def _(sp):
            sp.dma_start(tokb[:, 0:1], tok_b[0:P].rearrange("(e a) -> e a", a=1)).then_inc(s_pos, 16)
            sp.dma_start(tokb[0:64, 1:2], tok_b[P:E].rearrange("(e a) -> e a", a=1)).then_inc(s_pos, 16)
            for b in range(B // 2):
                sp.dma_start(ximg[b * G:(b + 1) * G, :, :],
                             x[b].rearrange("c (g p) w -> g c (p w)", p=PS)).then_inc(s_x, 16)
            sp.dma_start(wtok[:], tok_W.rearrange("(k p) e -> p k e", p=P)).then_inc(s_tokw, 16)
            sp.wait_ge(s_zero, 2)
            TM = P - NIMG
            for b in range(B):
                sp.dma_start(hin[0:1, b, 0, :], tok_cls[0]).then_inc(s_text, 16)
                sp.dma_start(hin[NIMG:P, b, 0, :], txt[b, 0:TM, :]).then_inc(s_text, 16)
                sp.dma_start(hin[0:TAIL, b, 1, :], txt[b, TM:NTXT, :]).then_inc(s_text, 16)
                sp.dma_start(htail[TAIL * (b % 2):TAIL * (b % 2) + TAIL, b // 2, :], txt[b, TM:NTXT, :]).then_inc(s_text, 16)
            sp.wait_ge(s_x, 16 * B)
            for part, rows in ((0, P), (1, 64)):
                src = W_o[P * part:P * part + rows, :].rearrange("o (q j e) -> o q j e", q=NH // 2, j=2)
                dst = wo_raw[0:rows, part].rearrange("o (q c) e -> o q c e", c=3)
                for j in range(2):
                    sp.dma_start(dst[:, :, j, :], src[:, :, j, 0:P]).then_inc(s_wo, 16)
                    sp.dma_start(dst[:, :, 2, 64 * j:64 * j + 64], src[:, :, j, P:E]).then_inc(s_wo, 16)
            sp.dma_start(gwa[:], gate_w[0:P, :]).then_inc(s_small2, 16)
            sp.dma_start(gwb[:], gate_w[P:E, :]).then_inc(s_small2, 16)
            sp.dma_start(gbb[:], gate_b.rearrange("(a e) -> a e", a=1).broadcast_to([P, NE])).then_inc(s_small2, 16)
            sp.dma_start(rbias[:], bias.rearrange("(a e) -> a e", a=1).broadcast_to([P, NE])).then_inc(s_small2, 16)
            sp.dma_start(bdx[0:NE, :], bd).then_inc(s_small2, 16)
            sp.dma_start(bdx[NE:NW, :], sbd.rearrange("(a e) -> a e", a=1)).then_inc(s_small2, 16)
            sp.wait_ge(s_embsb, G)
            for b in range(B):
                sp.dma_start(hin[1:NIMG, b, 0, :], emb[b * G:(b + 1) * G, :, :]).then_inc(s_emb[min(b // 2, 1)], 16)

            def load_in(slot, up, gt):
                for c, w in enumerate((up, gt)):
                    sp.dma_start(wra[:, slot, c, :], w[0:P, :]).then_inc(w_in[slot], 16)
                    sp.dma_start(wrb[0:64, slot, c, :], w[P:E, :]).then_inc(w_in[slot], 16)
                    sp.dma_start(wrb[64:P, slot, c, :], w[P:E, :]).then_inc(w_in[slot], 16)

            def load_down(slot, dn, b1, b2):
                sp.dma_start(wdn[:, slot, :], dn).then_inc(wd_in[slot], 16)
                sp.dma_start(bcol[:, slot, 0:1], b1).then_inc(wd_in[slot], 16)
                sp.dma_start(bcol[:, slot, 1:2], b2).then_inc(wd_in[slot], 16)

            def routed_in(slot, e):
                load_in(slot, Wu[bass.ds(e, 1)].rearrange("a k h -> (a k) h"),
                        Wg[bass.ds(e, 1)].rearrange("a k h -> (a k) h"))

            def routed_down(slot, e):
                load_down(slot, Wd[bass.ds(e, 1)].rearrange("a k h -> (a k) h"),
                          bu[bass.ds(e, 1)].rearrange("a h -> h a"), bg[bass.ds(e, 1)].rearrange("a h -> h a"))

            def split_done(k):
                sp.wait_ge(wal_ready, k + 1)
                sp.wait_ge(wbs_ready, k + 1)

            load_in(0, sWu, sWg)
            load_down(0, sWd, sbu.rearrange("(h a) -> h a", a=1), sbg.rearrange("(h a) -> h a", a=1))
            routed_in(1, 0)
            routed_down(1, 0)
            split_done(0)
            routed_in(0, 1)
            with sp.Fori(0, (NE - 2) // 2) as j:
                sp.wait_ge(down_done, 16 * j + 8)
                routed_down(0, 2 * j + 1)
                split_done(2 * j + 1)
                routed_in(1, 2 * j + 2)
                sp.wait_ge(down_done, 16 * j + 16)
                routed_down(1, 2 * j + 2)
                split_done(2 * j + 2)
                routed_in(0, 2 * j + 3)
            sp.wait_ge(down_done, 8 * (NE - 1))
            routed_down(0, NE - 1)
            for i in range(PAIRS):
                sp.wait_ge(bias_added, (3 * i + 2) // 2 + 1)
                for k in range(2):
                    sp.dma_start(out[2 * i + k, 0:P, :], R[:, 3 * i + k, :]).then_inc(out_done, 16)
                    sp.dma_start(out[2 * i + k, P:S, :], R[TAIL * k:TAIL * k + TAIL, 3 * i + 2, :]).then_inc(out_done, 16)
            sp.wait_ge(out_done, 16 * 4 * PAIRS)

        @block.gpsimd
        def _(pool):
            own = Tally(pool_own)
            wte_v = wte[0:P * WROWS, :].rearrange("(p c r) e -> c p r e", p=P, r=WR)
            own.mark(pool.memset(ident[:], 0.0))
            own.mark(pool.memset(cmask[:], 0.0))
            own.mark(pool.memset(tmask[:], 0.0))
            own.mark(pool.memset(wrest[:], 0.0))
            own.mark(pool.memset(upper[:], 0.0))
            own.mark(pool.memset(sign[:], 1.0))
            pool.wait_ge(pool_own, own.at)
            own.mark(pool.affine_select(out=ident[:], in_=ident[:], compare_op=ALU.not_equal, fill=1.0,
                                        base=0, pattern=[[-1, P]], channel_multiplier=1))
            own.mark(pool.affine_select(out=cmask[:], in_=cmask[:], compare_op=ALU.is_ge, fill=MASKED,
                                        base=0, pattern=[[-1, P]], channel_multiplier=1))
            own.mark(pool.affine_select(out=tmask[0:64, :], in_=tmask[0:64, :], compare_op=ALU.is_ge, fill=MASKED,
                                        base=0, pattern=[[-1, 64]], channel_multiplier=1))
            pool.wait_ge(pool_own, own.at)
            own.mark(pool.affine_select(out=tmask[64:P, :], in_=tmask[64:P, :], compare_op=ALU.is_ge, fill=MASKED,
                                        base=0, pattern=[[-1, 64]], channel_multiplier=1))
            pool.wait_ge(pool_own, own.at)
            own.mark(pool.affine_select(out=upper[:], in_=upper[:], compare_op=ALU.is_gt, fill=1.0,
                                        base=64, pattern=[[0, 1]], channel_multiplier=-1))
            own.mark(pool.affine_select(out=sign[:], in_=sign[:], compare_op=ALU.is_gt, fill=-1.0,
                                        base=64, pattern=[[0, 1]], channel_multiplier=-1))
            own.mark(pool.memset(mhalf[:], -0.5))
            own.mark(pool.memset(vmean[:], 1.0 / V))
            own.mark(pool.iota(nregi[:, 0:1], pattern=[[0, 1]], base=1, channel_multiplier=1))
            own.mark(pool.iota(nregi[:, 1:2], pattern=[[0, 1]], base=P + 1 - TAIL, channel_multiplier=1))
            own.mark(pool.memset(firsthalf[:], 0.0))
            pool.wait_ge(pool_own, own.at)
            own.mark(pool.affine_select(out=firsthalf[:], in_=firsthalf[:], compare_op=ALU.is_ge, fill=float(TAIL),
                                        base=-TAIL, pattern=[[0, 1]], channel_multiplier=1))
            own.mark(pool.tensor_copy(identb[:], ident[:]))
            own.mark(pool.tensor_copy(nregf[:], nregi[:]))
            pool.wait_ge(pool_own, own.at)
            own.mark(pool.tensor_tensor(nregf[:, 1:2], nregf[:, 1:2], firsthalf[:], ALU.add))
            pool.wait_ge(pool_own, own.at)
            for i in range(PAIRS):
                own.mark(pool.memset(R[:, 3 * i + 2, :], 0.0))
            pool.wait_ge(pool_own, own.at)
            pool.memset(wts[:], 1.0).then_inc(s_const, 1)
            pool.wait_ge(s_wo, 16 * 8)
            pool.dma_start(wacc[:], wte_v[0]).then_inc(wte_in, 16)
            pool.dma_start(wrest[0:WREST, :], wte[P * WROWS:V, :]).then_inc(wte_rest, 16)

            def rstd(n, count):
                pool.wait_ge(var_ready, count)
                pool.tensor_tensor(rs[:, 0:n], ve[:, 0:n], mhalf[:, 0:n], ALU.pow).then_inc(rstd_ready, 1)

            def batch(bt, b):
                pool.wait_ge(xnT_ready, 2 * bt + 2)
                for h in range(NH):
                    last = (pool.tensor_tensor(qb[:, b, 0, :], xb[:, b, :], w2b[:, 0:1].broadcast_to([64, SP]), ALU.mult)
                            if h == 0 else
                            pool.tensor_scalar(qb[:, b, h, :], xb[:, b, :], w2b[:, h:h + 1], None, ALU.mult))
                    if h % GRP == GRP - 1:
                        last.then_inc(qb_ready, 1)

            def add_rows(c):
                pool.wait_ge(wte_in, 16 * c)
                pool.dma_start(wacc[:], wte_v[bass.ds(c, 1)].rearrange("a p r e -> (a p) r e"),
                               accum_op=ALU.add, max_dma_last_dim=4 * WR * E // 6).then_inc(wte_in, 16)

            pool.wait_ge(s_w2, 2)
            rstd(4, 1)
            rstd(4, 2)
            rstd(4, 3)
            rstd(4, 4)
            batch(1, 1)
            add_rows(1)
            with pool.Fori(0, PAIRS - 2) as i:
                add_rows(2 * i + 2)
                batch(2 * i + 2, 0)
                add_rows(2 * i + 3)
                batch(2 * i + 3, 1)
                rstd(4, 2 * i + 5)
                rstd(4, 2 * i + 6)
            add_rows(B - 2)
            batch(B - 2, 0)
            add_rows(B - 1)
            batch(B - 1, 1)
            pool.wait_ge(wte_in, 16 * B)
            n = WR // 2
            while n > 3:
                own.mark(pool.tensor_tensor(wacc[:, 0:n, :], wacc[:, 0:n, :], wacc[:, n:2 * n, :], ALU.add))
                pool.wait_ge(pool_own, own.at)
                n //= 2
            pool.tensor_tensor(wacc[:, 0:n, :], wacc[:, 0:n, :], wacc[:, n:2 * n, :], ALU.add).then_inc(wsum_ready, 1)

            def x_lows(i):
                pool.wait_ge(xfT_act, 2 * i + 2)
                pool.tensor_tensor(xal[:, i], fa[:, i], xah[:, i].bitcast(F32), ALU.subtract).then_inc(x_low, 1)
                pool.wait_ge(xfT_dve, 2 * i + 2)
                pool.tensor_tensor(xbl[:, i], fb[:, i], xbh[:, i].bitcast(F32), ALU.subtract).then_inc(x_low, 1)

            for i in range(PAIRS - 1):
                rstd(3, 2 * PAIRS + i + 1)
            x_lows(0)
            x_lows(1)

            def w_low(slot, k):
                pool.wait_ge(wh_ready, 2 * k + 1)
                pool.tensor_tensor(wal[:, slot], wra[:, slot], wah[:, slot].bitcast(F32),
                                   ALU.subtract).then_inc(wal_ready, 1)

            w_low(0, 0)
            rstd(3, 3 * PAIRS)
            x_lows(2)
            x_lows(3)
            w_low(1, 1)
            with pool.Fori(0, NE // 2 - 1) as j:
                w_low(0, 2 * j + 2)
                w_low(1, 2 * j + 3)
            w_low(0, NE)

        @block.scalar
        def _(act):
            act.dma_start(posr[:, 0, :], tok_pos[0, 0:P].rearrange("d h w -> d (h w)")).then_inc(s_pos, 16)
            act.dma_start(posr[0:64, 1, :], tok_pos[0, P:E].rearrange("d h w -> d (h w)")).then_inc(s_pos, 16)
            for b in range(B // 2, B):
                act.dma_start(ximg[b * G:(b + 1) * G, :, :],
                              x[b].rearrange("c (g p) w -> g c (p w)", p=PS)).then_inc(s_x, 16)
            act.dma_start(wqk[:], W_qk).then_inc(s_small, 16)
            act.dma_start(lnw[:], ln_w.rearrange("(a e) -> a e", a=1).broadcast_to([P, E])).then_inc(s_small, 16)
            act.wait_ge(s_x, 16 * B)
            act.activation(xpat[:, 1].rearrange("t g (r w) -> t g r w", w=PS),
                           ximg[:, 1].rearrange("t (r g w) -> t g r w", g=G, w=PS), ACT.Copy).then_inc(s_xpat, 1)
            act.activation(xpat[:, 2].rearrange("t g (r w) -> t g r w", w=PS)[:, :, PS // 2:PS],
                           ximg[:, 2].rearrange("t (r g w) -> t g r w", g=G, w=PS)[:, :, PS // 2:PS],
                           ACT.Copy).then_inc(s_xpat, 1)
            for g in range(G):
                act.wait_ge(s_patps, g + 1)
                if g >= 2:
                    act.wait_ge(s_embps, g - 1)
                act.activation(patT[:, g % 2], bank[g % 2][:, 0:KC * BG].rearrange("p (k t) -> p k t", k=KC),
                               ACT.Copy).then_inc(s_patT, 1)
            for c in range(NCH):
                act.wait_ge(s_wops, c + 1)
                act.activation(woT[:, c, :], bank[4 + c % 2][:, 0:E],
                               ACT.Copy).then_inc(s_woT if c + 1 < NCH else proj_read, 1)

            def turn_out(b, bt):
                act.wait_ge(xnT_psum, bt + 1)
                act.activation(xa[:, b, :], bank[7][:, 0:SP], ACT.Copy).then_inc(xnT_ready, 1)
                act.activation(xb[:, b, :], bank[7][0:64, SP:2 * SP], ACT.Copy).then_inc(xnT_ready, 1)

            def exps(u, U):
                sl = u % 2
                act.wait_ge(max_main, U + 1)
                for j in range(GRP):
                    last = act.activation(pm[:, sl, j, :], bank[0][:, j * P:(j + 1) * P], ACT.Exp,
                                          bias=nmax[:, sl, j:j + 1], accum_out=psums[:, sl, j:j + 1])
                last.then_inc(exp_main, 1)
                act.wait_ge(max_tail, U + 1)
                for k in range(2):
                    last = act.activation(pt[:, sl, k, :], bank[1][:, k * S:(k + 1) * S], ACT.Exp,
                                          bias=nmax[:, sl, 4 + k:5 + k], accum_out=psums[:, sl, 4 + k:5 + k])
                last.then_inc(exp_tail, 1)

            def prob_out(u, U):
                act.wait_ge(turned_main, U + 1)
                at = 0 if u < UPB else TAIL
                act.activation(pT0[:, :, at:at + P], bank[2][:, :].rearrange("p (j t) -> p j t", j=GRP),
                               ACT.Copy).then_inc(probT_main, 1)

            def mix_out(u, U):
                g, b = u % UPB, u // UPB
                act.wait_ge(pv_done, 3 * U + 1)
                act.activation(oT[:, 6 * g:6 * g + 2, b * S:(b + 1) * S],
                               bank[4][:, 0:2 * S].rearrange("p (j t) -> p j t", j=2), ACT.Copy).then_inc(ot_act, 1)

            turn_out(0, 0)
            act.wait_ge(xnT_ready, 2)
            act.wait_ge(s_w2, 2)
            for h in range(NH):
                last = act.activation(qb[:, 0, h, :], xb[:, 0, :], ACT.Copy, scale=w2b[:, h:h + 1])
                if h % GRP == GRP - 1:
                    last.then_inc(qb_ready, 1)
            turn_out(1, 1)
            exps(0, 0)
            act.wait_ge(xnT_ready, 4)
            for h in range(NH):
                last = act.activation(qa[:, 1, h, :], xa[:, 1, :], ACT.Copy, scale=w2a[:, h:h + 1])
                if h % GRP == GRP - 1:
                    last.then_inc(qa_ready, 1)

            def pair(i, last):
                U = UPP * i
                for u in range(UPP - 1):
                    exps(u + 1, U + u + 1)
                    if u >= 1:
                        mix_out(u - 1, U + u - 1)
                    if u == 3 and not last:
                        turn_out(0, 2 * i + 2)
                    prob_out(u, U + u)
                mix_out(4, U + 4)
                if not last:
                    turn_out(1, 2 * i + 3)
                prob_out(5, U + 5)
                if not last:
                    exps(0, U + 6)
                mix_out(5, U + 5)

            with act.Fori(0, PAIRS - 1) as i:
                pair(i, False)
            pair(PAIRS - 1, True)

            act.wait_ge(avg_psum, 1)
            def features_act(i):
                act.wait_ge(xfT_psum, i + 1)
                act.activation(fa[:, i, :], bank[i % 2][:, 0:CW], ACT.Copy).then_inc(xfT_act, 1)
                act.activation(xah[:, i, :], bank[i % 2][:, 0:CW], ACT.Copy).then_inc(xfT_act, 1)
            def silu(st_, n):
                sl = n % 2
                act.wait_ge(up_ready, st_ + 1)
                if n >= 2:
                    act.wait_ge(hid_ready, st_ - 1)
                act.activation(sil[:, sl, :], bank[sl][:, 0:CW], ACT.Silu,
                               bias=bcol[:, (n // PAIRS) % 2, 0:1]).then_inc(silu_ready, 1)

            features_act(0)
            features_act(1)
            act.wait_ge(w_in[0], 16 * WLOADS)
            act.activation(wah[:, 0], wra[:, 0], ACT.Copy).then_inc(wh_ready, 1)
            act.activation(wbt[:], wrb[:, 0], ACT.Copy, scale=sign[:, 0:1]).then_inc(wh_ready, 1)
            features_act(2)
            act.wait_ge(wd_in[0], 16 * DLOADS)
            silu(0, 0)
            features_act(3)
            act.wait_ge(nmx_ready, 1)
            act.activation(sc[:], lg[:], ACT.Exp).then_inc(gexp, 1)

            def w_high(slot, loads):
                act.wait_ge(w_in[slot], 16 * WLOADS * loads)
                act.activation(wah[:, slot], wra[:, slot], ACT.Copy).then_inc(wh_ready, 1)
                act.activation(wbt[:], wrb[:, slot], ACT.Copy, scale=sign[:, 0:1]).then_inc(wh_ready, 1)

            for n in range(1, PAIRS):
                if n == 2:
                    w_high(1, 1)
                silu(n, n)

            def two_silus(j, last):
                for m in range(2 * PAIRS):
                    if m == 2:
                        w_high(0, j + 2)
                    if m == PAIRS + 2 and not last:
                        w_high(1, j + 2)
                    if m == 0:
                        act.wait_ge(wd_in[1], 16 * DLOADS * (j + 1))
                    if m == PAIRS:
                        act.wait_ge(wd_in[0], 16 * DLOADS * (j + 2))
                    silu(2 * PAIRS * j + PAIRS + m, PAIRS + m)

            with act.Fori(0, NE // 2 - 1) as j:
                two_silus(j, False)
            two_silus(NE // 2 - 1, True)
            for q in range(NT // 4):
                act.wait_ge(wT_psum, q + 1)
                act.activation(wT[:, 4 * q:4 * q + 4, :], wT_bank[q][0:NW, :].rearrange("p (t r) -> p t r", t=4),
                               ACT.Copy).then_inc(wT_ready, 1)

        @block.tensor
        def _(pe):
            pe.wait_ge(s_const, 1)
            pe.wait_ge(s_pos, 64)
            pe.wait_ge(s_posx, 2)
            for g in range(G):
                o = bank[4 + g // 2][0:BG, (g % 2) * E:(g % 2 + 1) * E]
                pe.matmul(o[:, 0:P], posx[:, 0, g].rearrange("p b h -> p (b h)"), ident[:], start=True, stop=True)
                last = pe.matmul(o[:, P:E], posx[0:64, 1, g].rearrange("p b h -> p (b h)"), ident[0:64, 0:64],
                                 start=True, stop=True)
            last.then_inc(s_posps, 1)
            pe.wait_ge(s_xpat, 4)

            def patch_turn(g):
                if g >= 2:
                    pe.wait_ge(s_patT, g - 1)
                for k in range(KC):
                    src = xpat[:, k // 2, g, (k % 2) * P:(k % 2) * P + P]
                    last = pe.transpose(bank[g % 2][:, k * BG:(k + 1) * BG], src, ident[0:BG, 0:BG])
                last.then_inc(s_patps, 1)

            def patch_embed(g):
                o = bank[2 + g % 2]
                pe.wait_ge(s_patT, g + 1)
                if g >= 2:
                    pe.wait_ge(s_embsb, g - 1)
                for k in range(KC):
                    last = pe.matmul(o[0:BG, 0:E], patT[:, g % 2, k, :], wtok[:, k, :], start=(k == 0), stop=(k == KC - 1))
                last.then_inc(s_embps, 1)

            patch_turn(0)
            pe.wait_ge(s_tokw, 16)
            for g in range(G):
                if g + 1 < G:
                    patch_turn(g + 1)
                patch_embed(g)
            pe.wait_ge(s_small, 32)
            pe.transpose(bank[6][:, 0:NH], wqk[:, 0:P], ident[0:NH, 0:NH])
            pe.transpose(bank[6][0:64, NH:2 * NH], wqk[:, P:E], ident[0:NH, 0:NH]).then_inc(s_wqps, 1)
            pe.wait_ge(s_wo, 16 * 8)
            for c in range(NCH):
                if c >= 2:
                    pe.wait_ge(s_woT, c - 1)
                for part, rows in ((0, P), (1, 64)):
                    last = pe.transpose(bank[4 + c % 2][:, part * P:part * P + rows], wo_raw[0:rows, part, c, :],
                                        ident[0:rows, 0:rows])
                last.then_inc(s_wops, 1)

            def turn_in(b, bt, i):
                pe.wait_ge(z_ready, 2 * i + b + 1)
                if not isinstance(bt, int) or bt:
                    pe.wait_ge(xnT_ready, 2 * bt)
                pe.transpose(bank[7][:, 0:P], z[:, b, 0, 0:P], ident[:])
                pe.transpose(bank[7][:, P:SP], z[0:64, b, 1, 0:P], ident[0:64, 0:64])
                pe.transpose(bank[7][0:64, SP:SP + P], z[:, b, 0, P:E], ident[:])
                pe.transpose(bank[7][0:64, SP + P:2 * SP], z[0:64, b, 1, P:E], ident[0:64, 0:64]).then_inc(xnT_psum, 1)

            def scores(u, U):
                g, b = u % UPB, u // UPB
                h = GRP * g
                main = bank[0][:, :].rearrange("p (j t) -> p j t", j=GRP)
                if not isinstance(U, int) or U:
                    pe.wait_ge(exp_main, U)
                pe.matmul(main, xa[:, b, 0:P], qa[:, b, h:h + GRP, 0:P], start=True, stop=False)
                pe.matmul(main, xb[:, b, 0:P], qb[:, b, h:h + GRP, 0:P], start=False, stop=False)
                pe.matmul(main, identb[:], cmask[:].rearrange("p (a t) -> p a t", a=1).broadcast_to([P, GRP, P]),
                          start=False, stop=True).then_inc(scores_main, 1)
                if not isinstance(U, int) or U:
                    pe.wait_ge(exp_tail, U)
                for half in range(2):
                    o = bank[1][64 * half:64 * half + 64, 0:2 * S].rearrange("p (j t) -> p j t", j=2)
                    hh = h + 2 * half
                    pe.matmul(o, xa[:, b, P:SP], qa[:, b, hh:hh + 2, 0:S], start=True, stop=False)
                    pe.matmul(o, xb[:, b, P:SP], qb[:, b, hh:hh + 2, 0:S], start=False, stop=True)
                o = bank[1][:, 0:2 * S].rearrange("p (j t) -> p j t", j=2)[:, :, P:S]
                pe.matmul(o, identb[:], tmask[:, 0:TAIL].rearrange("p (a t) -> p a t", a=1).broadcast_to([P, 2, TAIL]),
                          start=False, stop=True, skip_group_check=True).then_inc(scores_tail, 1)

            def queries_in(bt, g):
                pe.wait_ge(qa_ready, UPB * bt + g + 1)
                pe.wait_ge(qb_ready, UPB * bt + g + 1)

            def turn_probs(u, U):
                sl = u % 2
                pe.wait_ge(prob_main, U + 1)
                for j in range(GRP):
                    last = pe.transpose(bank[2][:, j * P:(j + 1) * P], pm[:, sl, j, :], ident[:])
                last.then_inc(turned_main, 1)
                pe.wait_ge(prob_tail, U + 1)
                for k in range(2):
                    pe.transpose(bank[3][:, k * P:(k + 1) * P], pt[:, sl, k, 0:P], ident[:])
                    last = pe.transpose(bank[3][0:TAIL, (2 + k) * P:(3 + k) * P], pt[:, sl, k, P:S], ident[:])
                last.then_inc(turned_tail, 1)

            def mix(u, U, i):
                b = u // UPB
                tl = slice(P, S) if b == 0 else slice(0, TAIL)
                pe.wait_ge(probT_main, U + 1)
                pe.wait_ge(probT_tail, 2 * U + 2)
                if u == 0:
                    pe.wait_ge(proj_read, 3 * i + 1)
                if u % UPB == 0:
                    pe.wait_ge(xn_ready, 2 * i + b + 1)
                for q in range(2):
                    if u >= 1:
                        if q == 0:
                            pe.wait_ge(ot_act, U)
                        else:
                            pe.wait_ge(ot_dve, 2 * U)
                    o = bank[4 + q][:, 0:2 * S].rearrange("p (j t) -> p j t", j=2)
                    pe.matmul(o, xn[:, b, 0, 0:P], pT0[:, 2 * q:2 * q + 2, :], start=True, stop=True)
                    pe.matmul(o[:, :, tl], xn[0:TAIL, b, 1, 0:P], pT1[0:TAIL, 2 * q:2 * q + 2, :], start=False,
                              stop=True, skip_group_check=True).then_inc(pv_done, 1)
                halves = [bank[6][64 * jj:64 * jj + 64, 0:2 * S].rearrange("p (q t) -> p q t", q=2) for jj in range(2)]
                for jj, o in enumerate(halves):
                    pe.matmul(o, xn[:, b, 0, P:E], pT0[:, jj:GRP:2, :], start=True, stop=True)
                for jj, o in enumerate(halves):
                    last = pe.matmul(o[:, :, tl], xn[0:TAIL, b, 1, P:E], pT1[0:TAIL, jj:GRP:2, :], start=False,
                                     stop=True, skip_group_check=True)
                last.then_inc(pv_done, 1)

            def turn_ffn(i):
                pe.wait_ge(xf_ready, i + 1)
                if i >= 2:
                    pe.wait_ge(xfT_act, 2 * (i - 1))
                    pe.wait_ge(xfT_dve, 2 * (i - 1))
                for t, (at, n) in enumerate(COLS):
                    pe.transpose(bank[i % 2][:, at:at + n], xf[0:n, i, t, 0:P], ident[0:n, 0:n])
                    last = pe.transpose(bank[2 + i % 2][:, at:at + n], xf[0:n, i, t, P:2 * P], ident[0:n, 0:n])
                last.then_inc(xfT_psum, 1)

            def gate(i):
                pe.wait_ge(xfT_act, 2 * i + 1)
                pe.wait_ge(xfT_dve, 2 * i + 1)
                if i >= 1:
                    pe.wait_ge(gate_ready, i)
                for t, (at, n) in enumerate(COLS):
                    o = bank[6][0:n, t * NE:(t + 1) * NE]
                    pe.matmul(o, fa[:, i, at:at + n], gwa[:], start=True, stop=False)
                    last = pe.matmul(o, fb[0:64, i, at:at + n], gwb[:], start=False, stop=True)
                last.then_inc(gate_psum, 1)

            def project(U, between=()):
                pe.wait_ge(ot_act, U + UPP)
                pe.wait_ge(ot_dve, 2 * (U + UPB))
                for t, (at, n) in enumerate(COLS):
                    if t == 1:
                        pe.wait_ge(ot_dve, 2 * (U + UPP))
                    o = bank[4][:, t * E:(t + 1) * E] if t < 2 else bank[5][0:TT, 0:E]
                    for c in range(NCH):
                        last = pe.matmul(o, oT[:, c, at:at + n], woT[:, c, :], start=(c == 0), stop=(c == NCH - 1))
                    if t >= 1:
                        last.then_inc(wo_done, 1)
                    for step, k in between[t] if between else ():
                        step(k)

            turn_in(0, 0, 0)
            turn_in(1, 1, 0)
            queries_in(0, 0)
            scores(0, 0)

            def mean():
                pe.wait_ge(wsum_ready, 1)
                pe.wait_ge(wte_rest, 16)
                pe.wait_ge(xnT_ready, 2 * B)
                parts = [wacc[:, r, :] for r in (0, 1, 2, WR - 1)] + [wrest[:]]
                for o, at, m in ((bank[7][:, 0:1], 0, P), (bank[7][0:64, 1:2], P, 64), (bank[7][64:P, 1:2], P, 64)):
                    for k, part in enumerate(parts):
                        last = pe.matmul(o, part[:, at:at + m], vmean[:], start=(k == 0), stop=(k == len(parts) - 1))
                last.then_inc(avg_psum, 1)

            def mean_projected():
                pe.wait_ge(avg_ready, 1)
                for c in range(NCH):
                    m = 0 if c % 3 < 2 else 1
                    last = pe.matmul(bank[7][:, E:2 * E], avg[:, m:m + 1].broadcast_to([P, P]), woT[:, c, :],
                                     start=(c == 0), stop=(c == NCH - 1))
                last.then_inc(c_psum, 1)

            def pair(i, last):
                U = UPP * i
                for u in range(UPP - 1):
                    queries_in(2 * i + (u + 1) // UPB, (u + 1) % UPB)
                    scores(u + 1, U + u + 1)
                    if u >= 1:
                        mix(u - 1, U + u - 1, i)
                    if u == 3 and not last:
                        turn_in(0, 2 * i + 2, i + 1)
                    if u == 3 and last:
                        mean()
                    if u == 4 and last:
                        mean_projected()
                    turn_probs(u, U + u)
                mix(4, U + 4, i)
                if not last:
                    turn_in(1, 2 * i + 3, i + 1)
                turn_probs(5, U + 5)
                if not last:
                    queries_in(2 * i + 2, 0)
                    scores(0, U + 6)
                mix(5, U + 5, i)
                if last:
                    pe.wait_ge(s_small2, 96)
                    project(U, (((turn_ffn, 0),), ((turn_ffn, 1), (gate, 0), (turn_ffn, 2)), ((gate, 1),)))
                else:
                    project(U)

            pe.wait_ge(s_woT, NCH - 1)
            with pe.Fori(0, PAIRS - 1) as i:
                pair(i, False)
            pair(PAIRS - 1, True)

            def products(dst, c, i, k):
                o = dst[:, 0:CW]
                pe.matmul(o, wah[:, k, c], xah[:, i], start=True, stop=False)
                pe.matmul(o, wah[:, k, c], xal[:, i], start=False, stop=False)
                pe.matmul(o, wal[:, k, c], xah[:, i], start=False, stop=False)
                pe.matmul(o, wbs[:, k, c], xbh[:, i], start=False, stop=False)
                return pe.matmul(o, wbs[:, k, c], xbl[:, i], start=False, stop=True)

            def expert_in(k, loads, slot):
                pe.wait_ge(w_in[slot], 16 * WLOADS * loads)
                pe.wait_ge(wd_in[slot], 16 * DLOADS * loads)
                pe.wait_ge(wh_ready, 2 * k + 2)
                pe.wait_ge(wal_ready, k + 1)
                pe.wait_ge(wbs_ready, k + 1)

            def up_gate(n, st_, k):
                sl = n % 2
                if n >= 2:
                    pe.wait_ge(silu_ready, st_ - 1)
                products(bank[sl], 0, n % PAIRS, k).then_inc(up_ready, 1)
                if n >= 2:
                    pe.wait_ge(hid_ready, st_ - 1)
                products(bank[2 + sl], 1, n % PAIRS, k).then_inc(gt_ready, 1)

            def down(n, st_, k):
                sl = n % 2
                pe.wait_ge(hid_ready, st_ + 1)
                for t, (at, rows) in enumerate(COLS):
                    if n >= 2 and t != 1:
                        pe.wait_ge(acc_done, 2 * (st_ - 1) - (1 if t == 0 else 0))
                    o = bank[4 + sl][:, t * E:(t + 1) * E] if t < 2 else bank[6 + sl][0:TT, 0:E]
                    last = pe.matmul(o, hidT[:, sl, at:at + rows], wdn[:, k, :], start=True, stop=True)
                    if t >= 1:
                        last.then_inc(down_done, 1)

            def expert_steps(n0, st0, j, first, last):
                count = PAIRS if first else 2 * PAIRS
                for m in range(count):
                    n, s_ = n0 + m, st0 + m
                    if not (last and m == count - 1):
                        if (n + 1) % PAIRS == 0:
                            k = ((n + 1) // PAIRS) % 2
                            if first:
                                expert_in(1, 1, 1)
                            elif k == 0:
                                expert_in(2 * j + 2, j + 2, 0)
                            else:
                                expert_in(2 * j + 3, j + 2, 1)
                        up_gate(n + 1, s_ + 1, ((n + 1) // PAIRS) % 2)
                    if last and m == count - 1:
                        pe.wait_ge(wts_ready, 1)
                        pe.wait_ge(hid_ready, s_ + 1)
                        for t in range(NT):
                            turned = pe.transpose(wT_bank[t // 4][0:NW, (t % 4) * P:(t % 4 + 1) * P], wts[:, t, :], ident[:])
                            if t % 4 == 3:
                                turned.then_inc(wT_psum, 1)
                    down(n, s_, (n // PAIRS) % 2)

            gate(2)
            expert_in(0, 1, 0)
            pe.wait_ge(x_low, 2)
            pe.wait_ge(xfT_act, 6)
            pe.wait_ge(xfT_dve, 6)
            up_gate(0, 0, 0)
            turn_ffn(3)
            gate(3)
            pe.wait_ge(gate_ready, PAIRS)
            pe.wait_ge(x_low, 2 * PAIRS)
            pe.wait_ge(xfT_act, 8)
            pe.wait_ge(xfT_dve, 8)
            expert_steps(0, 0, None, True, False)
            with pe.Fori(0, NE // 2 - 1) as j:
                expert_steps(PAIRS, 2 * PAIRS * j + PAIRS, j, False, False)
            expert_steps(PAIRS, 2 * PAIRS * (NE // 2 - 1) + PAIRS, NE // 2 - 1, False, True)
            pe.wait_ge(acc_done, 2 * (PAIRS * (NE + 1) - 1))
            for r in range(NT // 2):
                pe.wait_ge(wT_ready, min(NT // 4, max(r, 1)))
                for t in (2 * r, 2 * r + 1):
                    last = pe.matmul(bias_bank[r][:, (t % 2) * E:(t % 2 + 1) * E], wT[:, t, :], bdx[:], start=True,
                                     stop=True)
                last.then_inc(bias_psum, 1)

        @block.vector
        def _(dve):
            own = Tally(dve_own)

            def link(ins):
                own.mark(ins)
                dve.wait_ge(dve_own, own.at)

            dve.memset(hin[:], 0.0).then_inc(s_zero, 1)
            dve.memset(htail[:], 0.0).then_inc(s_zero, 1)
            own.mark(dve.memset(lg[:], 0.0))
            own.mark(dve.memset(scan[:], 0.0))
            own.mark(dve.memset(mv[:], 1.0))
            dve.wait_ge(s_pos, 64)
            for part, rows in ((0, P), (1, 64)):
                grid = posr[0:rows, part, :].rearrange("p (h a w c) -> p h a w c", h=G, a=2, c=2)
                for g in range(G):
                    src = grid[:, :, 0, g, 0].rearrange("p (a h) -> p a h", a=1).broadcast_to([rows, B, G])
                    last = dve.tensor_scalar(posx[0:rows, part, g], src, tokb[0:rows, part:part + 1], None, ALU.add)
                last.then_inc(s_posx, 1)
            dve.wait_ge(s_const, 1)
            own.mark(dve.reciprocal(nreg[:], nregf[:]))
            dve.wait_ge(dve_own, own.at)
            own.mark(dve.tensor_scalar(nnreg[:], nreg[:], -1.0, None, ALU.mult))
            dve.wait_ge(s_x, 16 * B)
            dve.tensor_copy(xpat[:, 0].rearrange("t g (r w) -> t g r w", w=PS),
                            ximg[:, 0].rearrange("t (r g w) -> t g r w", g=G, w=PS)).then_inc(s_xpat, 1)
            dve.tensor_copy(xpat[:, 2].rearrange("t g (r w) -> t g r w", w=PS)[:, :, 0:PS // 2],
                            ximg[:, 2].rearrange("t (r g w) -> t g r w", g=G, w=PS)[:, :, 0:PS // 2]).then_inc(s_xpat, 1)
            dve.wait_ge(s_posps, 1)
            for g in range(0, G, 2):
                n = min(2, G - g)
                own.mark(dve.tensor_copy(emb[:, g:g + n, :],
                                         bank[4 + g // 2][0:BG, 0:n * E].rearrange("p (g e) -> p g e", g=n)))
            dve.wait_ge(dve_own, own.at)
            for g in range(G):
                dve.wait_ge(s_embps, g + 1)
                dve.tensor_tensor(emb[:, g, :], bank[2 + g % 2][0:BG, 0:E], emb[:, g, :], ALU.add).then_inc(s_embsb, 1)
            dve.wait_ge(s_wqps, 1)
            link(dve.tensor_copy(w2a[:], bank[6][:, 0:NH]))
            link(dve.tensor_copy(w2b[:], bank[6][0:64, NH:2 * NH]))
            dve.scalar_tensor_tensor(out=w2a[:], in0=w2a[:], scalar=SCALE, in1=w2a[:], op0=ALU.mult,
                                     op1=ALU.mult).then_inc(s_w2, 1)
            dve.scalar_tensor_tensor(out=w2b[:], in0=w2b[:], scalar=SCALE, in1=w2b[:], op0=ALU.mult,
                                     op1=ALU.mult).then_inc(s_w2, 1)
            dve.wait_ge(s_w2, 2)
            dve.wait_ge(s_text, 16 * 4 * B)
            dve.wait_ge(s_emb[0], 32)
            dve.wait_ge(s_small, 32)

            def stats_begin(tiles):
                n = len(tiles)
                for t, src in enumerate(tiles):
                    own.mark(dve.bn_stats(st[0:src.shape[0], t, :], src))
                dve.wait_ge(dve_own, own.at)
                dve.memset(pause[:], 0.0)
                for t, src in enumerate(tiles):
                    own.mark(dve.bn_aggr(mv[0:src.shape[0], t, :], st[0:src.shape[0], t, :]))
                dve.wait_ge(dve_own, own.at)
                dve.tensor_scalar(ve[:, 0:n], mv[:, 0:n, 1], EPS, None, ALU.add).then_inc(var_ready, 1)

            def stats(tiles, count):
                stats_begin(tiles)
                dve.wait_ge(rstd_ready, count)

            def norm_begin(i, h):
                stats_begin([h[:, 0, 0, :], h[:, 0, 1, :], h[:, 1, 0, :], h[:, 1, 1, :]])

            def norm_middle(i, h):
                dve.wait_ge(rstd_ready, 2 * i + 1)
                for t in range(4):
                    own.mark(dve.tensor_scalar(z[:, t // 2, t % 2, :], h[:, t // 2, t % 2, :], mv[:, t, 0:1], rs[:, t:t + 1],
                                               ALU.subtract, ALU.mult))
                dve.wait_ge(dve_own, own.at)
                stats_begin([z[:, t // 2, t % 2, :] for t in range(4)])

            def norm_end(i):
                dve.wait_ge(rstd_ready, 2 * i + 2)
                for b in range(2):
                    for t in range(2):
                        own.mark(dve.tensor_scalar(z[:, b, t, :], z[:, b, t, :], mv[:, 2 * b + t, 0:1],
                                                   rs[:, 2 * b + t:2 * b + t + 1], ALU.subtract, ALU.mult))
                    dve.wait_ge(dve_own, own.at)
                    dve.tensor_tensor(z[:, b], z[:, b], lnw[:].rearrange("p (a e) -> p a e", a=1)
                                      .broadcast_to([P, 2, E]), ALU.mult).then_inc(z_ready, 1)

            def keep(b, i):
                dve.wait_ge(z_ready, 2 * i + b + 1)
                dve.tensor_copy(xn[:, b], z[:, b]).then_inc(xn_ready, 1)

            def queries(b, bt, groups=range(UPB)):
                dve.wait_ge(xnT_ready, 2 * bt + 2)
                for h in range(GRP * groups[0], GRP * (groups[-1] + 1)):
                    last = dve.tensor_scalar(qa[:, b, h, :], xa[:, b, :], w2a[:, h:h + 1], None, ALU.mult)
                    if h % GRP == GRP - 1:
                        last.then_inc(qa_ready, 1)

            def maxima(u, U):
                sl = u % 2
                dve.wait_ge(scores_main, U + 1)
                dve.tensor_reduce(nmax[:, sl, 0:GRP], bank[0][:, :].rearrange("p (j t) -> p j t", j=GRP), AX.X,
                                  ALU.max, negate=True).then_inc(max_main, 1)
                dve.wait_ge(scores_tail, U + 1)
                dve.tensor_reduce(nmax[:, sl, GRP:GRP + 2], bank[1][:, 0:2 * S].rearrange("p (j t) -> p j t", j=2),
                                  AX.X, ALU.max, negate=True).then_inc(max_tail, 1)

            def divide(u, U):
                sl = u % 2
                dve.wait_ge(exp_main, U + 1)
                dve.wait_ge(exp_tail, U + 1)
                link(dve.reciprocal(rsum[:], psums[:, sl, :]))
                dve.tensor_tensor(pm[:, sl], pm[:, sl],
                                  rsum[:, 0:GRP].rearrange("p (j a) -> p j a", a=1).broadcast_to([P, GRP, P]),
                                  ALU.mult).then_inc(prob_main, 1)
                dve.tensor_tensor(pt[:, sl], pt[:, sl],
                                  rsum[:, GRP:GRP + 2].rearrange("p (j a) -> p j a", a=1).broadcast_to([P, 2, S]),
                                  ALU.mult).then_inc(prob_tail, 1)

            def tails_out(u, U):
                at = P if u < UPB else 0
                dve.wait_ge(turned_tail, U + 1)
                for half in range(2):
                    src = bank[3][:, 0:2 * P].rearrange("p (k a t) -> p k a t", k=2, a=2)[:, :, half, 0:TAIL]
                    last = dve.tensor_copy(pT0[:, 2 * half:2 * half + 2, at:at + TAIL], src)
                last.then_inc(probT_tail, 1)
                for half in range(2):
                    src = bank[3][0:TAIL, 2 * P:4 * P].rearrange("p (k a t) -> p k a t", k=2, a=2)[:, :, half, 0:TAIL]
                    last = dve.tensor_copy(pT1[0:TAIL, 2 * half:2 * half + 2, :], src)
                last.then_inc(probT_tail, 1)

            def mix_out(u, U):
                g, b = u % UPB, u // UPB
                dve.wait_ge(pv_done, 3 * U + 2)
                dve.tensor_copy(oT[:, 6 * g + 3:6 * g + 5, b * S:(b + 1) * S],
                                bank[5][:, 0:2 * S].rearrange("p (j t) -> p j t", j=2)).then_inc(ot_dve, 1)
                dve.wait_ge(pv_done, 3 * U + 3)
                dve.tensor_copy(oT[:, 6 * g + 2:6 * g + 6:3, b * S:(b + 1) * S],
                                bank[6][:, 0:2 * S].rearrange("p (q t) -> p q t", q=2)).then_inc(ot_dve, 1)

            def residual(i):
                for t in range(3):
                    dve.wait_ge(wo_done, 2 * i + (1 if t < 2 else 2))
                    n, m = COLS[t][1], t // 2
                    src = bank[4][:, t * E:(t + 1) * E] if t < 2 else bank[5][0:n, 0:E]
                    old = hin[:, 2 * i + t, 0, :] if t < 2 else htail[0:n, i, :]
                    dve.scalar_tensor_tensor(out=R[0:n, 3 * i + t, :], in0=src, scalar=nreg[0:n, m:m + 1], in1=old,
                                             op0=ALU.mult, op1=ALU.add).then_inc(proj_read, 1)

            def logits(i):
                dve.wait_ge(gate_psum, i + 1)
                dve.tensor_tensor(lg[:, 3 * i:3 * i + 2, :], bank[6][:, 0:2 * NE].rearrange("p (t e) -> p t e", t=2),
                                  gbb[:].rearrange("p (a e) -> p a e", a=1).broadcast_to([P, 2, NE]), ALU.add)
                dve.tensor_tensor(lg[0:TT, 3 * i + 2, :], bank[6][0:TT, 2 * NE:3 * NE], gbb[0:TT, :],
                                  ALU.add).then_inc(gate_ready, 1)

            def tiles_of(i):
                return [R[0:COLS[t][1], 3 * i + t, :] for t in range(3)]

            def correct(i):
                dve.wait_ge(proj_read, 3 * (PAIRS if i == PAIRS - 1 else PAIRS - 1) + 1)
                tiles = tiles_of(i)
                for t in range(3):
                    n, m = COLS[t][1], t // 2
                    own.mark(dve.scalar_tensor_tensor(out=tiles[t], in0=cbc[0:n, :], scalar=nnreg[0:n, m:m + 1],
                                                      in1=tiles[t], op0=ALU.mult, op1=ALU.add))
                dve.wait_ge(dve_own, own.at)
                stats_begin(tiles)

            def experts_in(i):
                dve.wait_ge(rstd_ready, 2 * PAIRS + i + 1)
                tiles = tiles_of(i)
                for t in range(3):
                    n = COLS[t][1]
                    dve.tensor_scalar(xf[0:n, i, t, 0:E], tiles[t], mv[0:n, t, 0:1], rs[0:n, t:t + 1],
                                      ALU.subtract, ALU.mult)
                    last = dve.tensor_scalar(xf[0:n, i, t, E:2 * P], tiles[t][:, P:E], mv[0:n, t, 0:1],
                                             rs[0:n, t:t + 1], ALU.subtract, ALU.mult)
                last.then_inc(xf_ready, 1)

            def w_stack(slot, k):
                dve.wait_ge(wh_ready, 2 * k + 2)
                dve.scalar_tensor_tensor(out=wbs[:, slot], in0=wrb[:, slot], scalar=upper[:, 0:1],
                                         in1=wbt[:].bitcast(F32), op0=ALU.mult, op1=ALU.add).then_inc(wbs_ready, 1)

            def fuse(n, st_):
                sl = n % 2
                dve.wait_ge(gt_ready, st_ + 1)
                dve.wait_ge(silu_ready, st_ + 1)
                if n >= 2:
                    dve.wait_ge(down_done, 2 * (st_ - 1))
                dve.scalar_tensor_tensor(out=hidT[:, sl, 0:CW], in0=bank[2 + sl][:, 0:CW],
                                         scalar=bcol[:, (n // PAIRS) % 2, 1:2], in1=sil[:, sl, :], op0=ALU.add,
                                         op1=ALU.mult).then_inc(hid_ready, 1)

            def features_out(i):
                dve.wait_ge(xfT_psum, i + 1)
                dve.tensor_copy(fb[:, i, :], bank[2 + i % 2][:, 0:CW]).then_inc(xfT_dve, 1)
                dve.tensor_copy(xbh[:, i, :], bank[2 + i % 2][:, 0:CW]).then_inc(xfT_dve, 1)

            norm_begin(0, hin[:, 0:2])
            norm_middle(0, hin[:, 0:2])
            norm_end(0)
            queries(0, 0)
            keep(0, 0)
            keep(1, 0)
            dve.wait_ge(s_emb[1], 16 * (B - 2))
            norm_begin(1, hin[:, 2:4])
            maxima(0, 0)
            dve.wait_ge(xnT_ready, 4)
            norm_middle(1, hin[:, 2:4])

            def pair(i, last, norms):
                U = UPP * i
                for u in range(UPP - 1):
                    divide(u, U + u)
                    maxima(u + 1, U + u + 1)
                    if u >= 1:
                        mix_out(u - 1, U + u - 1)
                    tails_out(u, U + u)
                    if last:
                        if u == 3:
                            dve.wait_ge(avg_psum, 1)
                            dve.tensor_copy(avg[:], bank[7][:, 0:2]).then_inc(avg_ready, 1)
                        if u == 4:
                            dve.wait_ge(c_psum, 1)
                            link(dve.tensor_copy(cbc[:], bank[7][:, E:2 * E]))
                    if not last:
                        if u == 1:
                            norm_end(i + 1)
                        if u == 3:
                            keep(0, i + 1)
                            queries(0, 2 * i + 2, [0])
                        if u == 4:
                            queries(0, 2 * i + 2, [1, 2])
                divide(5, U + 5)
                mix_out(4, U + 4)
                tails_out(5, U + 5)
                if last:
                    correct(0)
                if not last:
                    maxima(0, U + 6)
                mix_out(5, U + 5)
                if not last:
                    keep(1, i + 1)
                    queries(1, 2 * i + 3)
                    if norms:
                        h = hin[:, bass.ds(2 * i + 4, 2)]
                        norm_begin(i + 2, h)
                        norm_middle(i + 2, h)
                else:
                    experts_in(0)
                    correct(1)
                    experts_in(1)
                    features_out(0)
                    correct(2)
                    experts_in(2)
                    features_out(1)
                    logits(0)
                    w_stack(0, 0)
                    features_out(2)
                residual(i)

            start = own.at
            per = UPP + 2 * (4 + 4 + 4)
            with dve.Fori(0, PAIRS - 2) as i:
                own.restart(per * i + start)
                pair(i, False, True)
                assert own.n == per
            own.restart(start + per * (PAIRS - 2))
            pair(PAIRS - 2, False, False)
            pair(PAIRS - 1, True, False)

            logits(1)
            correct(3)
            experts_in(3)
            logits(2)
            features_out(3)
            dve.wait_ge(wd_in[0], 16 * DLOADS)
            fuse(0, 0)
            logits(3)

            def rows(v, n):
                return v.rearrange("p (t a) -> p t a", a=1).broadcast_to([P, NT, n])

            def softmax_start():
                dve.wait_ge(gate_ready, PAIRS)
                link(dve.tensor_reduce(mx[:], lg[:], AX.X, ALU.max))
                dve.tensor_tensor(lg[:], lg[:], rows(mx[:], NE), ALU.subtract).then_inc(nmx_ready, 1)

            def softmax_end():
                dve.wait_ge(gexp, 1)
                link(dve.tensor_reduce(mx[:], sc[:], AX.X, ALU.add))
                link(dve.reciprocal(mx[:], mx[:]))
                link(dve.tensor_tensor(sc[:], sc[:], rows(mx[:], NE), ALU.mult))
                link(dve.tensor_tensor(sel[:], sc[:],
                                       rbias[:].rearrange("p (a e) -> p a e", a=1).broadcast_to([P, NT, NE]), ALU.add))
                link(dve.tensor_reduce(gs[:], sel[:].rearrange("p t (g a) -> p t g a", a=2), AX.X, ALU.add))

            def first_four(v, n):
                a, c = above[:, :, 0:n], tied[:, :, 0:n]
                for t in range(NT):
                    own.mark(dve.max(out=top8[:, t, :], in_=v[:, t, 0:n]))
                dve.wait_ge(dve_own, own.at)
                fourth = top8[:, :, TOPK - 1:TOPK].broadcast_to([P, NT, n])
                own.mark(dve.tensor_tensor(scan[:, 0, :, PAD:PAD + n], v[:, :, 0:n], fourth, ALU.is_equal))
                own.mark(dve.tensor_tensor(c, v[:, :, 0:n], fourth, ALU.is_equal))
                link(dve.tensor_tensor(a, v[:, :, 0:n], fourth, ALU.is_gt))
                own.mark(dve.tensor_reduce(room[:], a, AX.X, ALU.add))
                side, step = 0, 1
                while step < n:
                    link(dve.tensor_tensor(scan[:, 1 - side, :, PAD:PAD + n], scan[:, side, :, PAD:PAD + n],
                                           scan[:, side, :, PAD - step:PAD - step + n], ALU.add))
                    side, step = 1 - side, 2 * step
                own.mark(dve.tensor_tensor(scan[:, side, :, PAD:PAD + n], scan[:, side, :, PAD:PAD + n], rows(room[:], n),
                                           ALU.add))
                dve.wait_ge(dve_own, own.at)
                link(dve.scalar_tensor_tensor(out=c, in0=scan[:, side, :, PAD:PAD + n], scalar=float(TOPK), in1=c,
                                              op0=ALU.is_le, op1=ALU.mult))
                link(dve.tensor_tensor(a, a, c, ALU.add))

            def choose_groups():
                first_four(gs, TG)
                pairs = above[:, :, 0:TG].rearrange("p t (g a) -> p t g a", a=1).broadcast_to([P, NT, TG, 2])
                link(dve.tensor_tensor(sel[:].rearrange("p t (g a) -> p t g a", a=2),
                                       sel[:].rearrange("p t (g a) -> p t g a", a=2), pairs, ALU.mult))
                link(dve.tensor_scalar(gs[:], above[:, :, 0:TG], -1.0, -NEVER, ALU.add, ALU.mult))
                pairs = gs[:].rearrange("p t (g a) -> p t g a", a=1).broadcast_to([P, NT, TG, 2])
                link(dve.tensor_tensor(sel[:].rearrange("p t (g a) -> p t g a", a=2),
                                       sel[:].rearrange("p t (g a) -> p t g a", a=2), pairs, ALU.add))

            def choose_experts():
                first_four(sel, NE)
                dve.scalar_tensor_tensor(out=wts[:, :, 0:NE], in0=above[:], scalar=ROUTE, in1=sc[:], op0=ALU.mult,
                                         op1=ALU.mult).then_inc(wts_ready, 1)

            def gather(n, st_, e):
                sl, i = n % 2, n % PAIRS
                for t in range(3):
                    rows_ = COLS[t][1]
                    if t != 1:
                        dve.wait_ge(down_done, 2 * st_ + (1 if t < 2 else 2))
                    src = bank[4 + sl][:, t * E:(t + 1) * E] if t < 2 else bank[6 + sl][0:TT, 0:E]
                    if t == 0:
                        dve.wait_ge(acc_done, 2 * (st_ - PAIRS + 1)) if n >= PAIRS else None
                    old = R[0:rows_, 3 * i + t, :]
                    last = dve.scalar_tensor_tensor(out=old, in0=src,
                                                    scalar=wts[0:rows_, 3 * i + t, bass.ds(e, 1)], in1=old,
                                                    op0=ALU.mult, op1=ALU.add)
                    if t >= 1:
                        last.then_inc(acc_done, 1)

            softmax_start()
            softmax_end()
            fuse(1, 1)
            gather(0, 0, NE)
            choose_groups()
            for n in range(1, PAIRS):
                if n == 1:
                    w_stack(1, 1)
                if n == 2:
                    choose_experts()
                if n == PAIRS - 1:
                    dve.wait_ge(wd_in[1], 16 * DLOADS)
                fuse(n + 1, n + 1)
                gather(n, n, NE)
            dve.wait_ge(wts_ready, 1)

            def two_experts(j, last):
                for m in range(2 * PAIRS):
                    n, s_ = PAIRS + m, 2 * PAIRS * j + PAIRS + m
                    if m == 1:
                        w_stack(0, 2 * j + 2)
                    if m == PAIRS + 1 and not last:
                        w_stack(1, 2 * j + 3)
                    if m == PAIRS - 1:
                        dve.wait_ge(wd_in[0], 16 * DLOADS * j + 32 * DLOADS)
                    if m == 2 * PAIRS - 1 and not last:
                        dve.wait_ge(wd_in[1], 16 * DLOADS * j + 32 * DLOADS)
                    if not (last and m == 2 * PAIRS - 1):
                        fuse(n + 1, s_ + 1)
                    gather(n, s_, 2 * j + m // PAIRS)

            with dve.Fori(0, NE // 2 - 1) as j:
                two_experts(j, False)
            two_experts(NE // 2 - 1, True)
            dve.wait_ge(acc_done, 2 * PAIRS * (NE + 1))
            for r in range(NT // 2):
                dve.wait_ge(bias_psum, r + 1)
                dve.tensor_tensor(R[:, 2 * r:2 * r + 2, :], bias_bank[r][:, 0:2 * E].rearrange("p (t e) -> p t e", t=2),
                                  R[:, 2 * r:2 * r + 2, :], ALU.add).then_inc(bias_added, 1)


_INS = ['x', 'txt', 'L0_tok_W', 'L0_tok_b', 'L0_tok_positions', 'L0_tok_cls_embedding', 'L0_attn_ln_w', 'L0_attn_W_qk',
        'L0_attn_W_o', 'L0_attn_wte', 'L0_ffn_gate_w', 'L0_ffn_gate_b', 'L0_ffn_bias', 'L0_ffn_Wu', 'L0_ffn_bu',
        'L0_ffn_Wg', 'L0_ffn_bg', 'L0_ffn_Wd', 'L0_ffn_bd', 'L0_ffn_sWu', 'L0_ffn_sbu', 'L0_ffn_sWg', 'L0_ffn_sbg',
        'L0_ffn_sWd', 'L0_ffn_sbd']
_OUTS = [((8, 178, 192), 'float32')]


def kernel(**inputs):
    import numpy as _np
    import concourse.bacc as _bacc
    from concourse import mybir as _mybir
    from concourse.bass_utils import run_bass_kernel_spmd as _run

    nc = _bacc.Bacc("TRN2", target_bir_lowering=False, num_devices=1)
    arrays, args = {}, []
    for name in _INS:
        a = _np.ascontiguousarray(inputs[name])
        arrays[f"in_{name}_dram"] = a
        args.append(nc.dram_tensor(f"in_{name}_dram", a.shape, _mybir.dt.from_np(a.dtype), kind="ExternalInput").ap())
    for i, (shape, dtype) in enumerate(_OUTS):
        dt = _mybir.dt.from_np(_np.dtype(dtype))
        args.append(nc.dram_tensor(f"out_{i}_dram", shape, dt, kind="ExternalOutput").ap())
    early_fusion_kernel(nc, *args)
    r = _run(nc, [arrays], core_ids=[0])
    return r.results[0]["out_0_dram"]
```
